# Optimizing a Trainium2 kernel written in Bass

```python
import numpy as np
import jax
import jax.numpy as jnp

def _softmax(x, axis=-1):
    return jax.nn.softmax(x, axis=axis)

def _gelu(x):
    return jax.nn.gelu(x, approximate=True)

def _silu(x):
    return jax.nn.silu(x)

def _sigmoid(x):
    return jax.nn.sigmoid(x)

def _layernorm(x, axis=-1, eps=1e-05):
    m = jnp.mean(x, axis=axis, keepdims=True)
    v = jnp.var(x, axis=axis, keepdims=True)
    return (x - m) / jnp.sqrt(v + eps)

def _scatter_add(tgt, idx, src, axis=0):
    return tgt.at[idx].add(src)

def _segment_sum(src, seg, n):
    return jax.ops.segment_sum(src, seg, n)
kernel_name = 'mk_gnn_resnorm_d4_gnn_r8_c5ec19'

def setup_inputs(seed: int=0):
    np.random.seed(seed)
    _w = jnp.asarray

    def _rec_inputs():
        import jax
        import jax.numpy as jnp
        _gk = jax.random.key(seed)
        x = -0.0003713 + 1 * jax.random.normal(jax.random.fold_in(_gk, 1), (12500, 128), jnp.float32)
        _s = jax.random.randint(jax.random.fold_in(_gk, 2), (100000,), 0, 12500, jnp.int32)
        _d = jax.random.randint(jax.random.fold_in(_gk, 3), (100000,), 0, 12500, jnp.int32)
        _loop = jnp.arange(12500, dtype=jnp.int32)
        src = jnp.concatenate([_s, _d, _loop])
        dst = jnp.concatenate([_d, _s, _loop])
        _o = jnp.argsort(dst, stable=True)
        src = src[_o]
        dst = dst[_o]
        edge_attr_64 = 0.000167468 + 1.0002 * jax.random.normal(jax.random.fold_in(_gk, 12), (212500, 64), jnp.float32)
        edge_attr_8 = -0.000191324 + 0.999809 * jax.random.normal(jax.random.fold_in(_gk, 13), (212500, 8), jnp.float32)
        return (x, src, dst, edge_attr_64, edge_attr_8)
    x, src, dst, edge_attr_64, edge_attr_8 = _rec_inputs()

    def _L0_gnn_setup():
        import jax, jax.numpy as jnp
        import numpy as np
        N = 12500
        E = 200000
        IN = 128
        H = 128
        NH = 8
        DH = H // NH

        def _linear_init(key, fan_in, fan_out):
            kw, kb = jax.random.split(key)
            s = 1.0 / np.sqrt(fan_in)
            W = jax.random.uniform(kw, (fan_in, fan_out), jnp.float32, -s, s)
            b = jax.random.uniform(kb, (fan_out,), jnp.float32, -s, s)
            return (W, b)
        key = jax.random.key(seed)
        kx, kr, kc, k0, k1, k2, k3 = jax.random.split(key, 7)
        W_in, b_in = _linear_init(k0, IN, H)
        Wq, bq = _linear_init(k1, H, H)
        Wk, bk = _linear_init(k2, H, H)
        Wv, bv = _linear_init(k3, H, H)
        return {'X': jax.random.normal(kx, (N, IN), jnp.float32), 'rows': jax.random.randint(kr, (E,), 0, N, jnp.int32), 'cols': jax.random.randint(kc, (E,), 0, N, jnp.int32), 'W_in': W_in, 'b_in': b_in, 'Wq': Wq, 'bq': bq, 'Wk': Wk, 'bk': bk, 'Wv': Wv, 'bv': bv}
    _L0_gnn_all = _L0_gnn_setup()
    _L0_gnn_in = {k: v for k, v in _L0_gnn_all.items() if k in ('W_in', 'b_in', 'Wq', 'bq', 'Wk', 'bk', 'Wv', 'bv')}
    del _L0_gnn_all

    def _L1_gnn_setup():
        import jax, jax.numpy as jnp
        import numpy as np
        N_NODES = 1250
        N_EDGES = 80000
        D_FEAT = 128
        F_FILTER = 8
        F_WEIGHT = 64
        key = jax.random.key(seed)
        k1, k2, k3, k4, k5 = jax.random.split(key, 5)
        x = jax.random.normal(k1, (N_NODES, D_FEAT), dtype=jnp.float32)
        edge_filter = jax.random.normal(k2, (N_EDGES, F_FILTER), dtype=jnp.float32)
        weight = jax.random.normal(k3, (N_EDGES, F_WEIGHT), dtype=jnp.float32)
        edge_src = jax.random.randint(k4, (N_EDGES,), 0, N_NODES, dtype=jnp.int64)
        edge_dst = jax.random.randint(k5, (N_EDGES,), 0, N_NODES, dtype=jnp.int64)
        return {'x': x, 'edge_filter': edge_filter, 'weight': weight, 'edge_src': edge_src, 'edge_dst': edge_dst}
    _L1_gnn_all = _L1_gnn_setup()
    _L1_gnn_in = {k: v for k, v in _L1_gnn_all.items() if k in ()}
    del _L1_gnn_all

    def _L2_gnn_setup():
        import jax, jax.numpy as jnp
        import numpy as np
        N_NODES = 12500
        N_EDGES = 200000
        C_IN = 128
        C_OUT = 128
        key = jax.random.key(seed)
        k1, k2, k3, k4, k5 = jax.random.split(key, 5)
        x = jax.random.normal(k1, (N_NODES, C_IN), dtype=jnp.float32)
        W = jax.random.normal(k2, (2 * C_IN, C_OUT), dtype=jnp.float32) * (1.0 / np.sqrt(2 * C_IN))
        b = jax.random.normal(k3, (C_OUT,), dtype=jnp.float32) * 0.01
        src = jax.random.randint(k4, (N_EDGES,), 0, N_NODES, dtype=jnp.int64 if jax.config.jax_enable_x64 else jnp.int32)
        dst = jax.random.randint(k5, (N_EDGES,), 0, N_NODES, dtype=jnp.int64 if jax.config.jax_enable_x64 else jnp.int32)
        return {'x': x, 'W': W, 'b': b, 'src': src, 'dst': dst}
    _L2_gnn_all = _L2_gnn_setup()
    _L2_gnn_in = {k: v for k, v in _L2_gnn_all.items() if k in ('W', 'b')}
    del _L2_gnn_all

    def _L3_gnn_setup():
        import jax, jax.numpy as jnp
        import numpy as np
        N = 12500
        D = 128
        E = 78125

        def _gcn_conv(x, row, col, norm, W, b):
            h = x @ W
            msg = h[row] * norm[:, None]
            out = jax.ops.segment_sum(msg, col, num_segments=N)
            return out + b
        key = jax.random.key(seed)
        k1, k2, k3, k4, k5, k6 = jax.random.split(key, 6)
        x = jax.random.normal(k1, (N, D), dtype=jnp.float32)
        edge_index = jax.random.randint(k2, (2, E), 0, N, dtype=jnp.int64)
        s = 1.0 / np.sqrt(D)
        W1 = jax.random.uniform(k3, (D, D), dtype=jnp.float32, minval=-s, maxval=s)
        b1 = jnp.zeros((D,), dtype=jnp.float32)
        W2 = jax.random.uniform(k4, (D, D), dtype=jnp.float32, minval=-s, maxval=s)
        b2 = jnp.zeros((D,), dtype=jnp.float32)
        return {'x': x, 'edge_index': edge_index, 'W1': W1, 'b1': b1, 'W2': W2, 'b2': b2}
    _L3_gnn_all = _L3_gnn_setup()
    _L3_gnn_in = {k: v for k, v in _L3_gnn_all.items() if k in ('W1', 'b1', 'W2', 'b2')}
    del _L3_gnn_all
    return {'x': x, 'src': src, 'dst': dst, 'edge_attr_64': edge_attr_64, 'edge_attr_8': edge_attr_8, 'L0_gnn_W_in': _L0_gnn_in['W_in'], 'L0_gnn_b_in': _L0_gnn_in['b_in'], 'L0_gnn_Wq': _L0_gnn_in['Wq'], 'L0_gnn_bq': _L0_gnn_in['bq'], 'L0_gnn_Wk': _L0_gnn_in['Wk'], 'L0_gnn_bk': _L0_gnn_in['bk'], 'L0_gnn_Wv': _L0_gnn_in['Wv'], 'L0_gnn_bv': _L0_gnn_in['bv'], 'L2_gnn_W': _L2_gnn_in['W'], 'L2_gnn_b': _L2_gnn_in['b'], 'L3_gnn_W1': _L3_gnn_in['W1'], 'L3_gnn_b1': _L3_gnn_in['b1'], 'L3_gnn_W2': _L3_gnn_in['W2'], 'L3_gnn_b2': _L3_gnn_in['b2']}

def reference(x, src, dst, edge_attr_64, edge_attr_8, L0_gnn_W_in, L0_gnn_b_in, L0_gnn_Wq, L0_gnn_bq, L0_gnn_Wk, L0_gnn_bk, L0_gnn_Wv, L0_gnn_bv, L2_gnn_W, L2_gnn_b, L3_gnn_W1, L3_gnn_b1, L3_gnn_W2, L3_gnn_b2):
    import jax
    import jax.numpy as jnp

    def _L0_gnn_ref(X, rows, cols, W_in, b_in, Wq, bq, Wk, bk, Wv, bv):
        import jax, jax.numpy as jnp
        import numpy as np
        N = 12500
        E = 200000
        IN = 128
        H = 128
        NH = 8
        DH = H // NH

        def _linear_init(key, fan_in, fan_out):
            kw, kb = jax.random.split(key)
            s = 1.0 / np.sqrt(fan_in)
            W = jax.random.uniform(kw, (fan_in, fan_out), jnp.float32, -s, s)
            b = jax.random.uniform(kb, (fan_out,), jnp.float32, -s, s)
            return (W, b)
        h = X @ W_in + b_in
        q = (h @ Wq + bq).reshape(N, DH, NH) * DH ** (-0.5)
        k = (h @ Wk + bk).reshape(N, DH, NH)
        v = (h @ Wv + bv).reshape(N, DH, NH)
        score = jnp.einsum('edh,edh->eh', q[rows], k[cols])
        m = jax.ops.segment_max(score, rows, num_segments=N)
        p = jnp.exp(score - m[rows])
        denom = jax.ops.segment_sum(p, rows, num_segments=N)
        attn = p / denom[rows]
        out = jax.ops.segment_sum(attn[:, None, :] * v[cols], rows, num_segments=N)
        return out.reshape(N, H)

    def _L1_gnn_ref(x, edge_filter, weight, edge_src, edge_dst):
        import jax, jax.numpy as jnp
        import numpy as np
        N_NODES = 1250
        N_EDGES = 80000
        D_FEAT = 128
        F_FILTER = 8
        F_WEIGHT = 64
        scale = edge_filter.sum(axis=1, keepdims=True) * weight.sum(axis=1, keepdims=True)
        msg = x[edge_src] * scale
        out = jax.ops.segment_sum(msg, edge_dst, num_segments=x.shape[0])
        return out

    def _L2_gnn_ref(x, W, b, src, dst):
        import jax, jax.numpy as jnp
        import numpy as np
        N_NODES = 12500
        N_EDGES = 200000
        C_IN = 128
        C_OUT = 128
        diff = x[dst] - x[src]
        max_diff = jax.ops.segment_max(diff, dst, num_segments=x.shape[0])
        max_diff = jnp.where(jnp.isneginf(max_diff), jnp.zeros_like(max_diff), max_diff)
        h = jnp.concatenate([x, max_diff], axis=1)
        return jax.nn.relu(h @ W + b)

    def _L3_gnn_ref(x, edge_index, W1, b1, W2, b2):
        import jax, jax.numpy as jnp
        import numpy as np
        N = 12500
        D = 128
        E = 78125

        def _gcn_conv(x, row, col, norm, W, b):
            h = x @ W
            msg = h[row] * norm[:, None]
            out = jax.ops.segment_sum(msg, col, num_segments=N)
            return out + b
        loop = jnp.arange(N, dtype=edge_index.dtype)
        row = jnp.concatenate([edge_index[0], loop])
        col = jnp.concatenate([edge_index[1], loop])
        deg = jax.ops.segment_sum(jnp.ones_like(col, dtype=x.dtype), col, num_segments=N)
        dinv = jnp.where(deg > 0, jax.lax.rsqrt(deg), 0.0)
        norm = dinv[row] * dinv[col]
        h = jax.nn.relu(_gcn_conv(x, row, col, norm, W1, b1))
        return _gcn_conv(h, row, col, norm, W2, b2)
    edge_index = jnp.stack([src, dst])
    x = _layernorm(x + _L0_gnn_ref(x, src, dst, L0_gnn_W_in, L0_gnn_b_in, L0_gnn_Wq, L0_gnn_bq, L0_gnn_Wk, L0_gnn_bk, L0_gnn_Wv, L0_gnn_bv), axis=-1)
    x = _layernorm(x + _L1_gnn_ref(x, edge_attr_8, edge_attr_64, src, dst), axis=-1)
    x = _layernorm(x + _L2_gnn_ref(x, L2_gnn_W, L2_gnn_b, src, dst), axis=-1)
    x = _layernorm(x + _L3_gnn_ref(x, edge_index, L3_gnn_W1, L3_gnn_b1, L3_gnn_W2, L3_gnn_b2), axis=-1)
    return x

_drawn_inputs = setup_inputs


def setup_inputs(seed=0):
    import zlib

    import numpy as np

    out = dict(_drawn_inputs(seed))
    spreads = {'L3_gnn_b1': (0.0, 0.1), 'L3_gnn_b2': (0.0, 0.1)}
    factors = {'L0_gnn_Wq': 6.152,
     'L0_gnn_bq': 8.0,
     'L0_gnn_Wk': 6.056,
     'L0_gnn_bk': 8.0,
     'L2_gnn_b': 8.0}
    for name, (base, spread) in spreads.items():
        noise = np.random.default_rng([zlib.crc32(name.encode()), seed]).standard_normal(out[name].shape)
        drawn = base * np.exp(spread * noise) if base else spread * noise
        out[name] = jnp.asarray(drawn.astype(out[name].dtype))
    for name, factor in factors.items():
        out[name] = (out[name] * factor).astype(out[name].dtype)
    return out
```

```python
import concourse.bass as bass
from concourse import mybir
from contextlib import ExitStack


FP = mybir.dt.float32
BF = mybir.dt.bfloat16
I32 = mybir.dt.int32
ALU = mybir.AluOpType
ACT = mybir.ActivationFunctionType
AX = mybir.AxisListType

N = 12500
E = 212500
D = 128
HEADS = 8
DH = D // HEADS
P = 128
RING = 32
TILES = -(-E // (P * RING)) * RING
CHUNK = 3 * P
CHUNKS = -(-(N + P) // CHUNK)
NP = CHUNKS * CHUNK
BIG = 3.0e38
TINY = 1e-30
EPS = 1e-5


def wait(engine, sem, value):
    if not isinstance(value, int) or value > 0:
        engine.wait_ge(sem, value)


def pipeline(engine, count, lag, unroll, emit, peel=0):
    head = -(-max(lag, unroll, peel) // unroll)
    full = count // unroll

    def peeled(first, last):
        for s in range(first, last):
            emit(s, s // unroll, s % unroll, lambda l, s=s: 0 <= s - l < count)

    peeled(0, head * unroll)
    with engine.Fori(head, full) as i:
        for m in range(unroll):
            emit(i * unroll + m, i, m, lambda l: True)
    peeled(full * unroll, count + lag)


class Memory:

    def __init__(self, nc, ctx):
        self.nc, self.ctx = nc, ctx
        self.acc = self.sb("acc", [P, 2, NP])
        self.rel = self.sb("rel", [P, TILES], BF)
        self.rel_end = self.sb("rel_end", [P, TILES], BF)
        self.first_dst = self.sb("first_dst", [1, TILES], I32)
        self.iota = self.sb("iota", [P, P])
        self.ident = self.sb("ident", [P, P])
        self.mean_w = self.sb("mean_w", [P, P])
        self.ones = self.sb("ones", [P, P])
        self.expand = self.sb("expand", [HEADS, P])
        self.idx = self.sb("idx", [P, RING], I32)
        self.bank = [ctx.enter_context(nc.psum_tensor(f"bank{i}", [P, 512], FP)) for i in range(8)]
        self.gathered = [self.sem(f"gathered{i}") for i in range(RING)]
        self.idx_loaded = [self.sem(f"idx_loaded{i}") for i in range(4)]
        self.q_dram = nc.dram_tensor("q_rows", [NP, D], FP, kind="Internal").ap()
        self.kv_dram = nc.dram_tensor("kv_rows", [NP, 2 * D], FP, kind="Internal").ap()
        self.rows_dram = [nc.dram_tensor(f"rows{i}", [NP, D], FP, kind="Internal").ap() for i in range(4)]
        self.xT_dram = [nc.dram_tensor(f"xT{i}", [P, NP], FP, kind="Internal").ap() for i in range(3)]
        self.start_neg = nc.dram_tensor("start_neg", [1, TILES * P], BF, kind="Internal").ap()
        self.end_neg = nc.dram_tensor("end_neg", [1, TILES * P], BF, kind="Internal").ap()
        self.start_pos = nc.dram_tensor("start_pos", [1, TILES * P], BF, kind="Internal").ap()
        self.gather_steps = self.sem("gather_steps")
        self.gather_rounds = 0

    def sb(self, name, shape, dt=FP):
        return self.ctx.enter_context(self.nc.sbuf_tensor(name, shape, dt))

    def sem(self, name):
        return self.ctx.enter_context(self.nc.semaphore(name))


def semaphores(nc, ctx, prefix):
    made = []

    def release():
        nc.clear_and_free_semaphores(made)
        nc.all_engine_barrier(sem_only=True)

    def sem(name):
        made.append(nc.alloc_semaphore(prefix + name))
        return made[-1]

    ctx.callback(release)
    return sem


def sb_in(nc, ctx, name, shape, dt=FP):
    return ctx.enter_context(nc.sbuf_tensor(name, shape, dt))


def load_firsts(nc, mem, engine_type, first, count):
    _, values = nc.values_load_multi_w_load_instructions(
        mem.first_dst[0:1, bass.ds(first, count)], engines=[engine_type], min_val=0, max_val=N,
        skip_runtime_bounds_check_because="dst lies in 0..N-1 and the padding edges have N")
    return values


def prepare(nc, mem, dst_tiles, next_tiles, dst_flat, prev_flat, next_flat, first_dst):
    with ExitStack() as ctx:
        sem = semaphores(nc, ctx, "p_")
        tmp = sb_in(nc, ctx, "prep_i", [P, 5, TILES], I32)
        f = sb_in(nc, ctx, "prep_f", [P, 4, TILES])
        pen = sb_in(nc, ctx, "prep_pen", [P, 3, TILES], BF)
        pick = sb_in(nc, ctx, "prep_pick", [P, P])
        loaded, firsts_loaded, stored = sem("loaded"), sem("firsts_loaded"), sem("stored")
        filled, iota_ready, ident_ready = sem("filled"), sem("iota_ready"), sem("ident_ready")
        dst_ready, bc_ready, step, pens_ready = sem("dst_ready"), sem("bc_ready"), sem("step"), sem("pens_ready")
        block = ctx.enter_context(nc.Block())
        quarter = TILES // 4

        @block.sync
        def _(sp):
            for i, src in enumerate((dst_tiles, next_tiles, dst_flat, prev_flat, next_flat)):
                sp.dma_start(tmp[:, i, :], src).then_inc(loaded, 16)
            sp.dma_start(mem.first_dst[:, :], first_dst).then_inc(firsts_loaded, 16)
            sp.wait_ge(pens_ready, 3)
            for i, dst in enumerate((mem.start_neg, mem.end_neg, mem.start_pos)):
                sp.dma_start(dst.rearrange("o (p c) -> (o p) c", p=P), pen[:, i, :]).then_inc(stored, 16)
            sp.wait_ge(stored, 48)
            sp.wait_ge(firsts_loaded, 16)

        @block.gpsimd
        def _(pool):
            nc.gpsimd.iota(mem.iota[:, :], [[1, P]], base=0, channel_multiplier=0,
                           allow_small_or_imprecise_dtypes=True).then_inc(iota_ready, 1)
            nc.gpsimd.memset(mem.ones[:, :], 1.0).then_inc(filled, 1)
            pool.wait_ge(filled, 1)
            nc.gpsimd.affine_select(mem.ident[:, :], mem.ones[:, :], [[-1, P]], ALU.is_equal, 0.0,
                                    base=0, channel_multiplier=1).then_inc(ident_ready, 1)
            nc.gpsimd.affine_select(mem.expand[:, :].rearrange("h (d g) -> h d g", g=HEADS),
                                    mem.ones[0:HEADS, :].rearrange("h (d g) -> h d g", g=HEADS),
                                    [[0, DH], [-1, HEADS]], ALU.is_equal, 0.0,
                                    base=0, channel_multiplier=1).then_inc(ident_ready, 1)
            nc.gpsimd.affine_select(pick[:, :], mem.ones[:, :], [[0, P]], ALU.is_equal, 0.0,
                                    base=0, channel_multiplier=1).then_inc(ident_ready, 1)

        @block.tensor
        def _(pe):
            pe.wait_ge(ident_ready, 3)
            pe.wait_ge(dst_ready, 1)
            for c in range(4):
                nc.tensor.matmul(mem.bank[c][:, 0:quarter], pick[:, :], f[:, 0, c * quarter:(c + 1) * quarter],
                                 start=True, stop=True).then_inc(bc_ready, 1)

        @block.vector
        def _(dve):
            nc.vector.memset(mem.mean_w[:, :], 1.0 / D)
            dve.wait_ge(loaded, 80)
            nc.vector.tensor_copy(f[:, 0, :], tmp[:, 0, :]).then_inc(dst_ready, 1)
            nc.vector.tensor_tensor(f[:, 1, :], tmp[:, 0, :], tmp[:, 1, :], ALU.not_equal).then_inc(step, 1)
            nc.vector.tensor_tensor(f[:, 2, :], tmp[:, 2, :], tmp[:, 3, :], ALU.not_equal).then_inc(step, 1)
            nc.vector.tensor_tensor(f[:, 3, :], tmp[:, 2, :], tmp[:, 4, :], ALU.not_equal).then_inc(step, 1)
            dve.wait_ge(step, 3)
            nc.vector.tensor_scalar(pen[:, 0, :], f[:, 2, :], -BIG, None, ALU.mult).then_inc(pens_ready, 1)
            nc.vector.tensor_scalar(pen[:, 1, :], f[:, 3, :], -BIG, None, ALU.mult).then_inc(pens_ready, 1)
            nc.vector.tensor_scalar(pen[:, 2, :], f[:, 2, :], BIG, None, ALU.mult).then_inc(pens_ready, 1)
            dve.wait_ge(bc_ready, 4)
            dve.wait_ge(dst_ready, 1)
            for c in range(4):
                cols = slice(c * quarter, (c + 1) * quarter)
                nc.vector.tensor_tensor(mem.rel[:, cols], f[:, 0, cols], mem.bank[c][:, 0:quarter],
                                        ALU.subtract).then_inc(step, 1)
            dve.wait_ge(step, 7)
            nc.vector.scalar_tensor_tensor(f[:, 2, :], mem.rel[:, :], 1.0, f[:, 1, :], ALU.add, ALU.mult).then_inc(step, 1)
            dve.wait_ge(step, 8)
            dve.wait_ge(pens_ready, 3)
            nc.vector.tensor_scalar(mem.rel_end[:, :], f[:, 2, :], -1.0, None, ALU.add)
            nc.vector.memset(mem.acc[:, :, :], 0.0)


def project_inputs(nc, mem, xT, W_in, b_in, Wq, bq, Wk, bk, Wv, bv):
    with ExitStack() as ctx:
        sem = semaphores(nc, ctx, "d_")
        w_in = sb_in(nc, ctx, "w_in", [P, D])
        w_qkv = sb_in(nc, ctx, "w_qkv", [P, 3 * D])
        bias_in = sb_in(nc, ctx, "bias_in", [P, 1])
        bias_qkv = sb_in(nc, ctx, "bias_qkv", [P, 3 * D])
        x_in = sb_in(nc, ctx, "x_in", [P, 3, CHUNK])
        hT = sb_in(nc, ctx, "hT", [P, 3, CHUNK])
        qkv = sb_in(nc, ctx, "qkv", [P, 3, 3, 3 * D])
        w_loaded, scaled = sem("w_loaded"), sem("scaled")
        x_loaded = [sem(f"x_loaded{i}") for i in range(3)]
        stored = [sem(f"stored{i}") for i in range(3)]
        h_ready, hT_ready, qkv_ps_ready, qkv_ready = sem("h_ready"), sem("hT_ready"), sem("qkv_ps_ready"), sem("qkv_ready")
        block = ctx.enter_context(nc.Block())
        q_view = mem.q_dram.rearrange("(c k p) f -> c p k f", k=3, p=P)
        kv_view = mem.kv_dram.rearrange("(c k p) f -> c p k f", k=3, p=P)

        @block.sync
        def _(sp):
            sp.dma_start(w_in[:, :], W_in).then_inc(w_loaded, 16)
            for i, (w, b) in enumerate(((Wq, bq), (Wk, bk), (Wv, bv))):
                sp.dma_start(w_qkv[:, i * D:(i + 1) * D], w).then_inc(w_loaded, 16)
                sp.dma_start(bias_qkv[:, i * D:(i + 1) * D], b.to_broadcast([P, D])).then_inc(w_loaded, 16)
            sp.dma_start(bias_in[:, :], b_in.rearrange("o f -> f o")).then_inc(w_loaded, 16)

            def load_and_store(s, i, m, on):
                if on(0):
                    wait(sp, h_ready, s - 2)
                    sp.dma_start(x_in[:, m, :], xT[:, bass.ds(s * CHUNK, CHUNK)]).then_inc(x_loaded[m], 16)
                if on(2):
                    c, slot = s - 2, (m - 2) % 3
                    sp.wait_ge(qkv_ready, (c + 1) * 3)
                    sp.dma_start(q_view[bass.ds(c, 1), :, :, :].rearrange("o p k f -> (o p) k f"),
                                 qkv[:, slot, :, 0:D]).then_inc(stored[slot], 16)
                    sp.dma_start(kv_view[bass.ds(c, 1), :, :, :].rearrange("o p k f -> (o p) k f"),
                                 qkv[:, slot, :, D:3 * D]).then_inc(stored[slot], 16)

            pipeline(sp, CHUNKS, 2, 3, load_and_store)
            for i in range(3):
                sp.wait_ge(stored[i], 32 * (CHUNKS // 3))

        @block.tensor
        def _(pe):
            pe.wait_ge(w_loaded, 128)
            pe.wait_ge(scaled, 2)

            def products(s, i, m, on):
                if on(0):
                    pe.wait_ge(x_loaded[m], 16 * (i + 1))
                    wait(pe, hT_ready, s)
                    nc.tensor.matmul(mem.bank[0][:, 0:CHUNK], w_in[:, :], x_in[:, m, :], start=True, stop=True).then_inc(h_ready, 1)
                if on(1):
                    c, slot = s - 1, (m - 1) % 3
                    pe.wait_ge(hT_ready, c + 1)
                    for k in range(3):
                        wait(pe, qkv_ready, c * 3 + k - 2)
                        nc.tensor.matmul(mem.bank[1 + k][:, 0:3 * D], hT[:, slot, k * P:(k + 1) * P], w_qkv[:, :],
                                         start=True, stop=True).then_inc(qkv_ps_ready, 1)

            pipeline(pe, CHUNKS, 1, 3, products)

        @block.scalar
        def _(act):
            act.wait_ge(w_loaded, 128)

            def add_bias(s, i, m, on):
                act.wait_ge(h_ready, s + 1)
                wait(act, qkv_ps_ready, (s - 2) * 3)
                nc.scalar.activation(hT[:, m, :], mem.bank[0][:, 0:CHUNK], ACT.Identity, bias=bias_in[:, 0:1]).then_inc(hT_ready, 1)

            pipeline(act, CHUNKS, 0, 3, add_bias)

        @block.vector
        def _(dve):
            dve.wait_ge(w_loaded, 128)
            nc.vector.tensor_scalar(w_qkv[:, 0:D], w_qkv[:, 0:D], DH ** -0.5, None, ALU.mult).then_inc(scaled, 1)
            nc.vector.tensor_scalar(bias_qkv[:, 0:D], bias_qkv[:, 0:D], DH ** -0.5, None, ALU.mult).then_inc(scaled, 1)
            dve.wait_ge(scaled, 2)

            def add_bias(s, i, m, on):
                wait(dve, stored[m], 32 * i)
                for k in range(3):
                    dve.wait_ge(qkv_ps_ready, s * 3 + k + 1)
                    nc.vector.tensor_tensor(qkv[:, m, k, :], mem.bank[1 + k][:, 0:3 * D], bias_qkv[:, :],
                                            ALU.add).then_inc(qkv_ready, 1)

            pipeline(dve, CHUNKS, 0, 3, add_bias)


def gather_rows(nc, mem, pool, table, ring, steps, released, released_per_step, rounds):

    def gather(s, i, m, on):
        pool.wait_ge(mem.idx_loaded[m], 16 * (rounds + i + 1))
        wait(pool, released, released_per_step * (s - 3))
        pool.sem_inc(mem.gather_steps, 1)
        for k in range(8):
            slot = 8 * m + k
            pool.indirect_dma_start(ring[:, slot, :], None, table,
                                    bass.IndirectOffsetOnAxis(ap=mem.idx[:, slot:slot + 1], axis=0)
                                    ).then_inc(mem.gathered[slot], 16)

    pipeline(pool, steps, 0, 4, gather)


def load_idx(mem, sp, src_tiles, s, m, used, used_per_step):
    wait(sp, used, used_per_step * (s - 3))
    sp.dma_start(mem.idx[:, 8 * m:8 * m + 8], src_tiles[:, bass.ds(8 * s, 8)]).then_inc(mem.idx_loaded[m], 16)


def attention(nc, mem, src_tiles):
    rounds = mem.gather_rounds
    mem.gather_rounds += TILES // RING
    steps = TILES // 8
    with ExitStack() as ctx:
        sem = semaphores(nc, ctx, "a_")
        kv = sb_in(nc, ctx, "kv", [P, RING, 2 * D])
        onehot = sb_in(nc, ctx, "onehot", [P, RING, P])
        onehotT = sb_in(nc, ctx, "onehotT", [P, 2, 4 * P])
        q_win = sb_in(nc, ctx, "q_win", [P, 8, D])
        prod = sb_in(nc, ctx, "prod", [P, 2, 4 * D])
        pv = sb_in(nc, ctx, "pv", [P, 2, 4 * D])
        score = sb_in(nc, ctx, "score", [P, 2, 8 * HEADS])
        below = sb_in(nc, ctx, "below", [P, 8 * HEADS])
        prob = sb_in(nc, ctx, "prob", [P, 2, 8, D])
        scan = sb_in(nc, ctx, "scan", [HEADS, 8 * P])
        resets = sb_in(nc, ctx, "resets", [HEADS, 2, 2, 8 * P], BF)
        carry = sb_in(nc, ctx, "carry", [HEADS, 2])
        gap = sb_in(nc, ctx, "gap", [HEADS, 1])
        alpha = sb_in(nc, ctx, "alpha", [HEADS, 1])
        ps_onehotT, ps_q, ps_sum, ps_score, ps_ref = mem.bank[0:2], mem.bank[2:4], mem.bank[4:6], mem.bank[6], mem.bank[7]
        q_loaded = [sem(f"q_loaded{i}") for i in range(8)]
        resets_loaded = [sem(f"resets_loaded{i}") for i in range(2)]
        onehot_ready, sums_ready, added = sem("onehot_ready"), sem("sums_ready"), sem("added")
        onehotT_ps, onehotT_ready, qe_ready = sem("onehotT_ps"), sem("onehotT_ready"), sem("qe_ready")
        prod_ready, score_ready, pv_ready = sem("prod_ready"), sem("score_ready"), sem("pv_ready")
        score_ps, scan_loaded = sem("score_ps"), sem("scan_loaded")
        forward_done, carry_ready, backward_done, gap_ready = sem("forward_done"), sem("carry_ready"), sem("backward_done"), sem("gap_ready")
        ref_steps, ref_ps, below_ready, prob_ready = sem("ref_steps"), sem("ref_ps"), sem("below_ready"), sem("prob_ready")
        alpha_ready, alpha_ps, rescaled = sem("alpha_ready"), sem("alpha_ps"), sem("rescaled")
        block = ctx.enter_context(nc.Block())

        @block.sync
        def _(sp):
            def loads(s, i, m, on):
                if on(2):
                    b = s - 2
                    firsts = load_firsts(nc, mem, mybir.EngineType.SP, 8 * b, 8)
                    for k in range(8):
                        if k % 4 == 0:
                            wait(sp, qe_ready, 2 * b + k // 4 - 1)
                        sp.dma_start(q_win[:, k, :], mem.q_dram[bass.ds(firsts[k], P), :]).then_inc(q_loaded[k], 16)
                if on(0):
                    load_idx(mem, sp, src_tiles, s, m, score_ready, 2)
                if on(2):
                    wait(sp, backward_done, b - 1)
                    edges = bass.ds(8 * P * b, 8 * P)
                    sp.dma_start(resets[:, m % 2, 0, :], mem.start_neg[:, edges].to_broadcast([HEADS, 8 * P])).then_inc(resets_loaded[m % 2], 16)
                    sp.dma_start(resets[:, m % 2, 1, :], mem.end_neg[:, edges].to_broadcast([HEADS, 8 * P])).then_inc(resets_loaded[m % 2], 16)

            pipeline(sp, steps, 2, 4, loads)

        @block.gpsimd
        def _(pool):
            gather_rows(nc, mem, pool, mem.kv_dram, kv, steps, pv_ready, 2, rounds)

        @block.vector
        def _(dve):
            nc.vector.memset(carry[:, :], 0.0).then_inc(carry_ready, 1)

            def batch(s, i, m, on):
                m1, m2, m3 = (m - 1) % 4, (m - 2) % 4, (m - 3) % 4
                c, par = s - 2, m2 % 2
                if on(3):
                    b = s - 3
                    firsts = load_firsts(nc, mem, mybir.EngineType.DVE, 8 * b, 8)
                    dve.wait_ge(alpha_ps, b + 1)
                    wait(dve, added, 8 * b)
                    column = mem.acc[:, :, bass.ds(firsts[0], 1)]
                    nc.vector.tensor_scalar(column, column, ps_score[:, 0:1], None, ALU.mult).then_inc(rescaled, 1)
                for g in range(2):
                    if on(0):
                        for k in range(4 * g, 4 * g + 4):
                            t = 8 * s + k
                            wait(dve, sums_ready, t - RING + 1)
                            nc.vector.tensor_scalar(onehot[:, 8 * m + k, :], mem.iota[:, :], mem.rel[:, bass.ds(t, 1)], None,
                                                    ALU.is_equal).then_inc(onehot_ready, 1)
                    if on(3):
                        q, slot = 2 * b + g, 8 * m3 + 4 * g
                        dve.wait_ge(prob_ready, b + 1)
                        wait(dve, sums_ready, 4 * (q - 1))
                        nc.vector.tensor_tensor(pv[:, g, :].rearrange("e (k f) -> e k f", k=4), kv[:, slot:slot + 4, D:2 * D],
                                                prob[:, m3 % 2, 4 * g:4 * g + 4, :], ALU.mult).then_inc(pv_ready, 1)
                    if on(1):
                        q, slot = 2 * (s - 1) + g, 8 * m1 + 4 * g
                        dve.wait_ge(qe_ready, q + 1)
                        for k in range(4):
                            dve.wait_ge(mem.gathered[slot + k], 16 * (rounds + i + 1 - int(m < 1)))
                        wait(dve, score_ready, q - 1)
                        nc.vector.tensor_tensor(prod[:, g, :].rearrange("e (k f) -> e k f", k=4), kv[:, slot:slot + 4, 0:D],
                                                ps_q[g][:, :].rearrange("e (k f) -> e k f", k=4), ALU.mult).then_inc(prod_ready, 1)
                        dve.wait_ge(prod_ready, q + 1)
                        if g == 0:
                            wait(dve, below_ready, s - 2)
                        nc.vector.tensor_reduce(score[:, m1 % 2, g * 32:g * 32 + 32],
                                                prod[:, g, :].rearrange("e (k d h) -> e k h d", k=4, h=HEADS),
                                                AX.X, ALU.add).then_inc(score_ready, 1)
                    if on(2) and g == 1:
                        dve.wait_ge(carry_ready, c + 2)
                        nc.vector.tensor_tensor_scan(scan[:, ::-1], resets[:, par, 1, ::-1], scan[:, ::-1], -BIG,
                                                     ALU.add, ALU.max).then_inc(backward_done, 1)
                    if on(3):
                        for k in range(4 * g, 4 * g + 4):
                            t = 8 * b + k
                            dve.wait_ge(sums_ready, t + 2 - k % 2)
                            if k == 0:
                                dve.wait_ge(rescaled, b + 1)
                            wait(dve, added, t)
                            window = mem.acc[:, :, bass.ds(firsts[k], P)]
                            ps = ps_sum[k // 2 % 2][:, k % 2 * 256:k % 2 * 256 + 256].rearrange("f (a j) -> f a j", a=2)
                            nc.vector.tensor_tensor(window, window, ps, ALU.add).then_inc(added, 1)
                    if on(2) and g == 0:
                        dve.wait_ge(scan_loaded, 2 * (c + 1))
                        dve.wait_ge(resets_loaded[par], 32 * (2 * (i - int(m < 2)) + m2 // 2 + 1))
                        dve.wait_ge(carry_ready, c + 1)
                        nc.vector.tensor_tensor_scan(scan[:, :], resets[:, par, 0, :], scan[:, :], carry[:, 1 - par:2 - par],
                                                     ALU.add, ALU.max).then_inc(forward_done, 1)
                        dve.wait_ge(forward_done, c + 1)
                        wait(dve, gap_ready, c)
                        nc.vector.tensor_copy(carry[:, par:par + 1], scan[:, 8 * P - 1:8 * P]).then_inc(carry_ready, 1)
                    if on(2) and g == 1:
                        dve.wait_ge(backward_done, c + 1)
                        wait(dve, alpha_ready, c)
                        nc.vector.tensor_scalar(gap[:, :], carry[:, 1 - par:2 - par], scan[:, 0:1], 0.0,
                                                ALU.subtract, ALU.min).then_inc(gap_ready, 1)
                        dve.wait_ge(ref_ps, c + 1)
                        wait(dve, prob_ready, c)
                        nc.vector.tensor_tensor(below[:, :], score[:, par, :], ps_ref[:, 0:64],
                                                ALU.subtract).then_inc(below_ready, 1)

            pipeline(dve, steps, 3, 4, batch)

        @block.tensor
        def _(pe):
            def batch(s, i, m, on):
                m2, m3 = (m - 2) % 4, (m - 3) % 4
                c, par = s - 2, m2 % 2
                for g in range(2):
                    if on(2):
                        q = 2 * c + g
                        pe.wait_ge(score_ready, q + 1)
                        wait(pe, scan_loaded, q)
                        if g == 0:
                            wait(pe, rescaled, c)
                        for k in range(4):
                            last = nc.tensor.transpose(ps_score[0:HEADS, k * P:(k + 1) * P],
                                                       score[:, par, (4 * g + k) * HEADS:(4 * g + k + 1) * HEADS], mem.ident[:, :])
                        last.then_inc(score_ps, 1)
                    if on(0):
                        q = 2 * s + g
                        wait(pe, onehotT_ready, q - 1)
                        for k in range(4):
                            pe.wait_ge(onehot_ready, 4 * q + k + 1)
                            last = nc.tensor.transpose(ps_onehotT[g][:, k * P:(k + 1) * P], onehot[:, 8 * m + 4 * g + k, :],
                                                       mem.ident[:, :])
                        last.then_inc(onehotT_ps, 1)
                    if on(3):
                        for k in range(4):
                            t, slot = 8 * (s - 3) + 4 * g + k, 8 * m3 + 4 * g + k
                            if k == 0:
                                pe.wait_ge(pv_ready, 2 * (s - 3) + g + 1)
                            if k % 2 == 0:
                                wait(pe, added, t - 2)
                            ps = ps_sum[k // 2][:, k % 2 * 256:k % 2 * 256 + 256]
                            nc.tensor.matmul(ps[:, 0:P], pv[:, g, k * D:(k + 1) * D], onehot[:, slot, :], start=True, stop=True)
                            nc.tensor.matmul(ps[:, P:2 * P], prob[:, m3 % 2, 4 * g + k, :], onehot[:, slot, :],
                                             start=True, stop=True).then_inc(sums_ready, 1)
                    if on(0):
                        q = 2 * s + g
                        pe.wait_ge(onehotT_ready, q + 1)
                        wait(pe, prod_ready, q - 1)
                        for k in range(4):
                            pe.wait_ge(q_loaded[4 * g + k], 16 * (s + 1))
                            last = nc.tensor.matmul(ps_q[g][:, k * D:(k + 1) * D], onehotT[:, g, k * P:(k + 1) * P],
                                                    q_win[:, 4 * g + k, :], start=True, stop=True)
                        last.then_inc(qe_ready, 1)
                if on(2):
                    pe.wait_ge(backward_done, c + 1)
                    wait(pe, below_ready, c)
                    pe.sem_inc(ref_steps, 1)
                    for k in range(8):
                        last = nc.tensor.transpose(ps_ref[:, k * HEADS:(k + 1) * HEADS], scan[:, k * P:(k + 1) * P],
                                                   mem.ident[0:HEADS, 0:HEADS])
                    last.then_inc(ref_ps, 1)
                    pe.wait_ge(alpha_ready, c + 1)
                    pe.wait_ge(scan_loaded, 2 * (c + 1))
                    nc.tensor.matmul(ps_score[:, 0:1], mem.expand[:, :], alpha[:, :], start=True, stop=True).then_inc(alpha_ps, 1)

            pipeline(pe, steps, 3, 4, batch)

        @block.scalar
        def _(act):
            def batch(s, i, m, on):
                c, par = s - 2, (m - 2) % 4 % 2
                for g in range(2):
                    if on(2):
                        act.wait_ge(score_ps, 2 * c + g + 1)
                        if g == 0:
                            wait(act, ref_ps, c)
                            wait(act, gap_ready, c)
                        nc.scalar.copy(scan[:, g * 512:g * 512 + 512], ps_score[0:HEADS, :]).then_inc(scan_loaded, 1)
                    if on(0):
                        q = 2 * s + g
                        act.wait_ge(onehotT_ps, q + 1)
                        wait(act, qe_ready, q - 1)
                        nc.scalar.copy(onehotT[:, g, :], ps_onehotT[g][:, :]).then_inc(onehotT_ready, 1)
                if on(2):
                    act.wait_ge(gap_ready, c + 1)
                    wait(act, alpha_ps, c)
                    nc.scalar.activation(alpha[:, :], gap[:, :], ACT.Exp).then_inc(alpha_ready, 1)
                    act.wait_ge(below_ready, c + 1)
                    wait(act, sums_ready, 8 * (c - 1))
                    nc.scalar.activation(prob[:, par, :, :].rearrange("e k (d h) -> e k d h", h=HEADS),
                                         below[:, :].rearrange("e (k h) -> e k h", h=HEADS).unsqueeze(2).to_broadcast([P, 8, DH, HEADS]),
                                         ACT.Exp).then_inc(prob_ready, 1)

            pipeline(act, steps, 3, 4, batch)


def sum_layer(nc, mem, name, table, src_tiles, attr64=None, attr8=None):
    rounds = mem.gather_rounds
    mem.gather_rounds += TILES // RING
    steps = TILES // 8
    weighted = attr64 is not None
    per_bank = 2 if weighted else 4
    width = 512 // per_bank
    with ExitStack() as ctx:
        sem = semaphores(nc, ctx, name)
        rows = sb_in(nc, ctx, name + "rows", [P, RING, D])
        onehot = sb_in(nc, ctx, name + "onehot", [P, 16, P])
        if weighted:
            scaled = sb_in(nc, ctx, name + "scaled", [P, 16, D])
            a64 = sb_in(nc, ctx, name + "a64", [P, 2, 8, 64])
            a8 = sb_in(nc, ctx, name + "a8", [P, 2, 8, 8])
            sum64 = sb_in(nc, ctx, name + "sum64", [P, 8])
            sum8 = sb_in(nc, ctx, name + "sum8", [P, 8])
            weight = sb_in(nc, ctx, name + "weight", [P, 2, 8])
            attrs_loaded = [sem(f"attrs_loaded{i}") for i in range(2)]
            attrs_summed, weight_ready, scaled_ready = sem("attrs_summed"), sem("weight_ready"), sem("scaled_ready")
        zeroed, onehot_ready, sums_ready, added = sem("zeroed"), sem("onehot_ready"), sem("sums_ready"), sem("added")
        block = ctx.enter_context(nc.Block())

        @block.sync
        def _(sp):
            def loads(s, i, m, on):
                load_idx(mem, sp, src_tiles, s, m, sums_ready, 8)
                if weighted:
                    wait(sp, attrs_summed, 2 * (s - 1))
                    sp.dma_start(a64[:, m % 2, :, :], attr64[:, bass.ds(8 * s, 8), :]).then_inc(attrs_loaded[m % 2], 16)
                    sp.dma_start(a8[:, m % 2, :, :], attr8[:, bass.ds(8 * s, 8), :]).then_inc(attrs_loaded[m % 2], 16)

            pipeline(sp, steps, 0, 4, loads)

        @block.gpsimd
        def _(pool):
            if weighted:
                gather_rows(nc, mem, pool, table, rows, steps, scaled_ready, 8, rounds)
            else:
                gather_rows(nc, mem, pool, table, rows, steps, sums_ready, 8, rounds)

        @block.vector
        def _(dve):
            if weighted:
                nc.vector.memset(mem.acc[:, :, :], 0.0).then_inc(zeroed, 1)

            def step(s, i, m, on):
                if on(0) and weighted:
                    dve.wait_ge(attrs_loaded[m % 2], 32 * (2 * i + m // 2 + 1))
                    wait(dve, weight_ready, s)
                    nc.vector.tensor_reduce(sum64[:, :], a64[:, m % 2, :, :], AX.X, ALU.add).then_inc(attrs_summed, 1)
                    nc.vector.tensor_reduce(sum8[:, :], a8[:, m % 2, :, :], AX.X, ALU.add).then_inc(attrs_summed, 1)
                    dve.wait_ge(attrs_summed, 2 * (s + 1))
                    wait(dve, scaled_ready, 8 * (s - 1))
                    nc.vector.tensor_tensor(weight[:, m % 2, :], sum64[:, :], sum8[:, :], ALU.mult).then_inc(weight_ready, 1)
                if on(1):
                    firsts = load_firsts(nc, mem, mybir.EngineType.DVE, 8 * (s - 1), 8)
                for k in range(8):
                    if on(0):
                        t = 8 * s + k
                        wait(dve, sums_ready, t - 15)
                        nc.vector.tensor_scalar(onehot[:, m % 2 * 8 + k, :], mem.iota[:, :], mem.rel[:, bass.ds(t, 1)], None,
                                                ALU.is_equal).then_inc(onehot_ready, 1)
                    if on(1):
                        t, bank = 8 * (s - 1) + k, ((m - 1) % 4 * 8 + k) // per_bank % 4
                        dve.wait_ge(sums_ready, t + per_bank - k % per_bank)
                        if weighted:
                            dve.wait_ge(zeroed, 1)
                        wait(dve, added, t)
                        ps = mem.bank[bank][:, k % per_bank * width:(k % per_bank + 1) * width]
                        if weighted:
                            window = mem.acc[:, :, bass.ds(firsts[k], P)]
                            ps = ps.rearrange("f (a j) -> f a j", a=2)
                        else:
                            window = mem.acc[:, 0, bass.ds(firsts[k], P)]
                        nc.vector.tensor_tensor(window, window, ps, ALU.add).then_inc(added, 1)

            pipeline(dve, steps, 1, 4, step)

        if weighted:
            @block.scalar
            def _(act):
                def scale(s, i, m, on):
                    act.wait_ge(weight_ready, s + 1)
                    for k in range(8):
                        t, slot = 8 * s + k, 8 * m + k
                        act.wait_ge(mem.gathered[slot], 16 * (rounds + i + 1))
                        wait(act, sums_ready, t - 15)
                        nc.scalar.activation(scaled[:, m % 2 * 8 + k, :], rows[:, slot, :], ACT.Copy,
                                             scale=weight[:, m % 2, k:k + 1]).then_inc(scaled_ready, 1)

                pipeline(act, steps, 0, 4, scale)

        @block.tensor
        def _(pe):
            def sums(s, i, m, on):
                for k in range(8):
                    t, slot, bank = 8 * s + k, 8 * m + k, (8 * m + k) // per_bank % 4
                    if k % per_bank == 0:
                        wait(pe, added, t - 3 * per_bank)
                    pe.wait_ge(onehot_ready, t + 1)
                    if weighted:
                        pe.wait_ge(scaled_ready, t + 1)
                        ps = mem.bank[bank][:, k % 2 * 256:k % 2 * 256 + 256]
                        nc.tensor.matmul(ps[:, 0:P], scaled[:, m % 2 * 8 + k, :], onehot[:, m % 2 * 8 + k, :], start=True, stop=True)
                        nc.tensor.matmul(ps[:, P:2 * P], mem.ones[:, :], onehot[:, m % 2 * 8 + k, :],
                                         start=True, stop=True).then_inc(sums_ready, 1)
                    else:
                        pe.wait_ge(mem.gathered[slot], 16 * (rounds + i + 1))
                        nc.tensor.matmul(mem.bank[bank][:, k % 4 * P:(k % 4 + 1) * P], rows[:, slot, :], onehot[:, m % 2 * 8 + k, :],
                                         start=True, stop=True).then_inc(sums_ready, 1)

            pipeline(pe, steps, 0, 4, sums)


def min_layer(nc, mem, table, src_tiles):
    rounds = mem.gather_rounds
    mem.gather_rounds += TILES // RING
    steps = TILES // 8
    with ExitStack() as ctx:
        sem = semaphores(nc, ctx, "m_")
        rows = sb_in(nc, ctx, "m_rows", [P, RING, D])
        lasts = sb_in(nc, ctx, "lasts", [P, 16, P])
        resets = sb_in(nc, ctx, "m_resets", [P, 2, 8 * P], BF)
        minT = sb_in(nc, ctx, "minT", [P, 4, 4 * P])
        mins = sb_in(nc, ctx, "mins", [P, 4, 4 * D])
        resets_loaded = [sem(f"resets_loaded{i}") for i in range(2)]
        rowsT_ps, minT_ready, mins_ps, mins_ready, picked_ps = sem("rowsT_ps"), sem("minT_ready"), sem("mins_ps"), sem("mins_ready"), sem("picked_ps")
        lasts_ready, added, zeroed = sem("lasts_ready"), sem("added"), sem("zeroed")
        block = ctx.enter_context(nc.Block())

        @block.sync
        def _(sp):
            def loads(s, i, m, on):
                load_idx(mem, sp, src_tiles, s, m, rowsT_ps, 2)
                wait(sp, minT_ready, 2 * (s - 1))
                sp.dma_start(resets[:, m % 2, :], mem.start_pos[:, bass.ds(8 * P * s, 8 * P)].to_broadcast([P, 8 * P])
                             ).then_inc(resets_loaded[m % 2], 16)

            pipeline(sp, steps, 0, 4, loads)

        @block.gpsimd
        def _(pool):
            gather_rows(nc, mem, pool, table, rows, steps, rowsT_ps, 2, rounds)

        @block.vector
        def _(dve):
            nc.vector.memset(mem.acc[:, 0, :], 0.0).then_inc(zeroed, 1)

            def step(s, i, m, on):
                if on(3):
                    firsts = load_firsts(nc, mem, mybir.EngineType.DVE, 8 * (s - 3), 8)
                for g in range(2):
                    if on(0):
                        q, slot = 2 * s + g, m % 2 * 2 + g
                        dve.wait_ge(rowsT_ps, q + 1)
                        if g == 0:
                            dve.wait_ge(resets_loaded[m % 2], 16 * (2 * i + m // 2 + 1))
                        wait(dve, minT_ready, q)
                        wait(dve, mins_ps, q - 3)
                        start = 0.0 if isinstance(q, int) and q == 0 else minT[:, (slot - 1) % 4, 4 * P - 1:4 * P]
                        nc.vector.tensor_tensor_scan(minT[:, slot, :], resets[:, m % 2, g * 512:g * 512 + 512], mem.bank[g][:, :],
                                                     start, ALU.add, ALU.min).then_inc(minT_ready, 1)
                    for k in range(4 * g, 4 * g + 4):
                        if on(1):
                            t = 8 * (s - 1) + k
                            wait(dve, picked_ps, 2 * (s - 3) + g + 1)
                            nc.vector.tensor_scalar(lasts[:, (m - 1) % 2 * 8 + k, :], mem.iota[:, :], mem.rel_end[:, bass.ds(t, 1)],
                                                    None, ALU.is_equal).then_inc(lasts_ready, 1)
                        if on(3):
                            t = 8 * (s - 3) + k
                            dve.wait_ge(picked_ps, 2 * (s - 3) + g + 1)
                            dve.wait_ge(zeroed, 1)
                            wait(dve, added, t)
                            window = mem.acc[:, 0, bass.ds(firsts[k], P)]
                            nc.vector.tensor_tensor(window, window, mem.bank[4 + (m - 3) % 2 * 2 + g][:, k % 4 * P:(k % 4 + 1) * P],
                                                    ALU.add).then_inc(added, 1)

            pipeline(dve, steps, 3, 4, step)

        @block.tensor
        def _(pe):
            def step(s, i, m, on):
                for g in range(2):
                    if on(0):
                        q = 2 * s + g
                        wait(pe, minT_ready, q - 1)
                        for k in range(4):
                            slot = 8 * m + 4 * g + k
                            pe.wait_ge(mem.gathered[slot], 16 * (rounds + i + 1))
                            last = nc.tensor.transpose(mem.bank[g][:, k * P:(k + 1) * P], rows[:, slot, :], mem.ident[:, :])
                        last.then_inc(rowsT_ps, 1)
                    if on(1):
                        q, slot = 2 * (s - 1) + g, (m - 1) % 2 * 2 + g
                        pe.wait_ge(minT_ready, q + 1)
                        wait(pe, mins_ready, q - 1)
                        for k in range(4):
                            last = nc.tensor.transpose(mem.bank[2 + g][:, k * D:(k + 1) * D], minT[:, slot, k * P:(k + 1) * P], mem.ident[:, :])
                        last.then_inc(mins_ps, 1)
                    if on(2):
                        q, slot = 2 * (s - 2) + g, m % 2 * 2 + g
                        pe.wait_ge(mins_ready, q + 1)
                        pe.wait_ge(lasts_ready, 4 * (q + 1))
                        wait(pe, added, 4 * (q - 3))
                        for k in range(4):
                            last = nc.tensor.matmul(mem.bank[4 + slot][:, k * P:(k + 1) * P], mins[:, slot, k * D:(k + 1) * D],
                                                    lasts[:, 4 * slot + k, :], start=True, stop=True)
                        last.then_inc(picked_ps, 1)

            pipeline(pe, steps, 2, 4, step)

        @block.scalar
        def _(act):
            def step(s, i, m, on):
                for g in range(2):
                    if on(1):
                        q, slot = 2 * (s - 1) + g, (m - 1) % 2 * 2 + g
                        act.wait_ge(mins_ps, q + 1)
                        wait(act, picked_ps, q - 3)
                        nc.scalar.copy(mins[:, slot, :], mem.bank[2 + g][:, :]).then_inc(mins_ready, 1)

            pipeline(act, steps, 1, 4, step)


def node_stage(nc, mem, kind, table, x_from=None, x_to=None, w=None, w_low=None, bias=None, w_next=None):
    norm = kind != "first_conv"
    makes_y = kind in ("max", "first_conv")
    lag_out = 5 if makes_y else 4
    with ExitStack() as ctx:
        sem = semaphores(nc, ctx, kind + "_")
        sb = lambda n, *shape: sb_in(nc, ctx, f"{kind}_{n}", [P, *shape])
        x_in, pre, proj, degree, r = (sb(n, 3, CHUNK) for n in ("x_in", "pre", "proj", "degree", "r"))
        centred, square, std, x_new, y, rows = (sb(n, 3, CHUNK) for n in ("centred", "square", "std", "x_new", "y", "rows"))
        w_sb, w_low_sb, w_next_sb, bias_sb, eps_sb = sb("w", D), sb("w_low", D), sb("w_next", D), sb("bias", 1), sb("eps", 1)
        loaded, eps_ready = sem("loaded"), sem("eps_ready")
        x_loaded = [sem(f"x_loaded{i}") for i in range(3)]
        x_stored = [sem(f"x_stored{i}") for i in range(3)]
        rows_stored = [sem(f"rows_stored{i}") for i in range(3)]
        half_ready, pre_ready, degree_ready, root_ready, dinv_ready = (sem(n) for n in ("half_ready", "pre_ready", "degree_ready", "root_ready", "dinv_ready"))
        proj_ps, proj_ready, scaled_ready, r_ready = (sem(n) for n in ("proj_ps", "proj_ready", "scaled_ready", "r_ready"))
        mean_ps, centred_ready, square_ready, var_ps = (sem(n) for n in ("mean_ps", "centred_ready", "square_ready", "var_ps"))
        std_ready, inverse_ready, x_ready = (sem(n) for n in ("std_ready", "inverse_ready", "x_ready"))
        dinv_steps = sem("dinv_steps")
        next_ps, y_ready, started, rows_ps, rows_ready = (sem(n) for n in ("next_ps", "y_ready", "started", "rows_ps", "rows_ready"))
        ps_proj, ps_mean, ps_var, ps_next, ps_rows = (mem.bank[i][:, 0:CHUNK] for i in range(5))
        block = ctx.enter_context(nc.Block())
        weights = [(dst, src) for dst, src in ((w_sb, w), (w_low_sb, w_low), (w_next_sb, w_next)) if src is not None]
        n_loads = len(weights) + (bias is not None)
        table_view = table.rearrange("(c k p) f -> c p k f", k=3, p=P)

        @block.sync
        def _(sp):
            for dst, src in weights:
                sp.dma_start(dst[:, :], src).then_inc(loaded, 16)
            if bias is not None:
                sp.dma_start(bias_sb[:, :], bias.rearrange("o f -> f o")).then_inc(loaded, 16)

            def step(s, i, m, on):
                if on(0) and norm:
                    wait(sp, r_ready, s - 2)
                    sp.dma_start(x_in[:, m, :], x_from[:, bass.ds(s * CHUNK, CHUNK)]).then_inc(x_loaded[m], 16)
                if on(4) and x_to is not None:
                    c, slot = s - 4, (m - 4) % 3
                    sp.wait_ge(x_ready, c + 1)
                    sp.dma_start(x_to[:, bass.ds(c * CHUNK, CHUNK)], x_new[:, slot, :]).then_inc(x_stored[slot], 16)
                if on(lag_out):
                    c, slot = s - lag_out, (m - lag_out) % 3
                    sp.wait_ge(rows_ready, c + 1)
                    sp.dma_start(table_view[bass.ds(c, 1), :, :, :].rearrange("o p k f -> (o p) k f"),
                                 rows[:, slot, :].rearrange("p (k f) -> p k f", k=3)).then_inc(rows_stored[slot], 16)

            pipeline(sp, CHUNKS, lag_out, 3, step, peel=lag_out + 3)
            for n in range(3):
                sp.wait_ge(rows_stored[n], 16 * (CHUNKS // 3))
                if x_to is not None:
                    sp.wait_ge(x_stored[n], 16 * (CHUNKS // 3))

        @block.vector
        def _(dve):
            nc.vector.memset(eps_sb[:, :], EPS).then_inc(eps_ready, 1)
            if n_loads:
                dve.wait_ge(loaded, 16 * n_loads)

            def step(s, i, m, on):
                sums = lambda c: mem.acc[:, 0, bass.ds(c * CHUNK, CHUNK)]
                counts = lambda c: mem.acc[:, 1, bass.ds(c * CHUNK, CHUNK)]
                if on(5) and makes_y:
                    c, slot = s - 5, (m - 5) % 3
                    dve.wait_ge(next_ps, c + 1)
                    if kind == "max":
                        dve.wait_ge(dinv_ready, c + 1)
                    wait(dve, rows_ps, c - 2)
                    wait(dve, started, c - 2)
                    nc.vector.tensor_tensor(y[:, slot, :], ps_next, counts(c), ALU.mult).then_inc(y_ready, 1)
                    dve.wait_ge(y_ready, c + 1)
                    dve.wait_ge(pre_ready, c + 1)
                    nc.vector.tensor_copy(sums(c), y[:, slot, :]).then_inc(started, 1)
                if on(4) and norm:
                    c, slot = s - 4, (m - 4) % 3
                    dve.wait_ge(std_ready, c + 1)
                    nc.vector.reciprocal(std[:, slot, :], std[:, slot, :]).then_inc(inverse_ready, 1)
                    dve.wait_ge(inverse_ready, c + 1)
                    wait(dve, next_ps if makes_y else rows_ps, c - 2)
                    if x_to is not None:
                        wait(dve, x_stored[slot], 16 * (i + (m - 4) // 3))
                    nc.vector.tensor_tensor(x_new[:, slot, :], centred[:, slot, :], std[:, slot, :], ALU.mult).then_inc(x_ready, 1)
                if on(3) and norm:
                    c, slot = s - 3, (m - 3) % 3
                    dve.wait_ge(mean_ps, c + 1)
                    wait(dve, x_ready, c - 2)
                    nc.vector.tensor_tensor(centred[:, slot, :], r[:, slot, :], ps_mean, ALU.subtract).then_inc(centred_ready, 1)
                if on(2):
                    c, slot = s - 2, (m - 2) % 3
                    if norm:
                        dve.wait_ge(x_loaded[slot], 16 * (i + (m - 2) // 3 + 1))
                        wait(dve, centred_ready, c - 2)
                    if kind == "attention":
                        dve.wait_ge(pre_ready, c + 1)
                        nc.vector.tensor_tensor(r[:, slot, :], sums(c), pre[:, slot, :], ALU.mult).then_inc(scaled_ready, 1)
                        dve.wait_ge(scaled_ready, c + 1)
                        nc.vector.tensor_tensor(r[:, slot, :], r[:, slot, :], x_in[:, slot, :], ALU.add).then_inc(r_ready, 1)
                    if kind == "weighted":
                        nc.vector.tensor_tensor(r[:, slot, :], sums(c), x_in[:, slot, :], ALU.add).then_inc(r_ready, 1)
                    if kind == "max":
                        dve.wait_ge(proj_ready, c + 1)
                        nc.vector.tensor_tensor(r[:, slot, :], proj[:, slot, :], x_in[:, slot, :], ALU.add).then_inc(r_ready, 1)
                        dve.wait_ge(root_ready, c + 1)
                        dve.sem_inc(dinv_steps, 1)
                        nc.vector.reciprocal(counts(c), degree[:, slot, :]).then_inc(dinv_ready, 1)
                    if kind == "first_conv":
                        wait(dve, x_ready, c - 2)
                        nc.vector.tensor_tensor(pre[:, slot, :], sums(c), counts(c), ALU.mult).then_inc(pre_ready, 1)
                    if kind == "second_conv":
                        wait(dve, r_ready, c - 2)
                        nc.vector.tensor_tensor(pre[:, slot, :], sums(c), counts(c), ALU.mult).then_inc(pre_ready, 1)
                        dve.wait_ge(pre_ready, c + 1)
                        nc.vector.scalar_tensor_tensor(r[:, slot, :], pre[:, slot, :], bias_sb[:, 0:1], x_in[:, slot, :],
                                                       ALU.add, ALU.add).then_inc(r_ready, 1)
                if on(1) and kind == "attention":
                    c, slot = s - 1, (m - 1) % 3
                    wait(dve, r_ready, c - 2)
                    nc.vector.tensor_scalar(pre[:, slot, :], counts(c), TINY, None, ALU.max).then_inc(half_ready, 1)
                    dve.wait_ge(half_ready, c + 1)
                    nc.vector.reciprocal(pre[:, slot, :], pre[:, slot, :]).then_inc(pre_ready, 1)
                if on(1) and kind == "max":
                    c, slot = s - 1, (m - 1) % 3
                    dve.wait_ge(x_loaded[slot], 16 * (i + (m - 1) // 3 + 1))
                    wait(dve, proj_ps, c - 2)
                    nc.vector.tensor_tensor(pre[:, slot, :], x_in[:, slot, :], sums(c), ALU.subtract).then_inc(half_ready, 1)
                    dve.wait_ge(half_ready, c + 1)
                    nc.vector.scalar_tensor_tensor(pre[:, slot, :], counts(c), 1.0, pre[:, slot, :], ALU.min, ALU.mult).then_inc(pre_ready, 1)
                    wait(dve, dinv_ready, c - 2)
                    nc.vector.tensor_scalar(degree[:, slot, :], counts(c), 1.0, None, ALU.add).then_inc(degree_ready, 1)

            pipeline(dve, CHUNKS, lag_out, 3, step, peel=lag_out + 3)

        @block.tensor
        def _(pe):
            if n_loads:
                pe.wait_ge(loaded, 16 * n_loads)

            def step(s, i, m, on):
                if on(lag_out):
                    c, slot = s - lag_out, (m - lag_out) % 3
                    pe.wait_ge(y_ready if makes_y else x_ready, c + 1)
                    wait(pe, rows_ready, c)
                    source = y if makes_y else x_new
                    for k in range(3):
                        last = nc.tensor.transpose(ps_rows[:, k * P:(k + 1) * P], source[:, slot, k * P:(k + 1) * P], mem.ident[:, :])
                    last.then_inc(rows_ps, 1)
                if on(4) and makes_y:
                    c, slot = s - 4, (m - 4) % 3
                    pe.wait_ge(x_ready, c + 1)
                    wait(pe, y_ready, c)
                    nc.tensor.matmul(ps_next, w_next_sb[:, :], x_new[:, slot, :], start=True, stop=True).then_inc(next_ps, 1)
                if on(3) and norm:
                    c, slot = s - 3, (m - 3) % 3
                    pe.wait_ge(square_ready, c + 1)
                    wait(pe, std_ready, c)
                    nc.tensor.matmul(ps_var, mem.mean_w[:, :], square[:, slot, :], start=True, stop=True).then_inc(var_ps, 1)
                if on(2) and norm:
                    c, slot = s - 2, (m - 2) % 3
                    pe.wait_ge(r_ready, c + 1)
                    wait(pe, centred_ready, c)
                    nc.tensor.matmul(ps_mean, mem.mean_w[:, :], r[:, slot, :], start=True, stop=True).then_inc(mean_ps, 1)
                if on(1) and kind == "max":
                    c, slot = s - 1, (m - 1) % 3
                    pe.wait_ge(pre_ready, c + 1)
                    pe.wait_ge(x_loaded[slot], 16 * (i + (m - 1) // 3 + 1))
                    wait(pe, proj_ready, c)
                    nc.tensor.matmul(ps_proj, w_sb[:, :], x_in[:, slot, :], start=True, stop=False)
                    nc.tensor.matmul(ps_proj, w_low_sb[:, :], pre[:, slot, :], start=False, stop=True).then_inc(proj_ps, 1)

            pipeline(pe, CHUNKS, lag_out, 3, step, peel=lag_out + 3)

        @block.scalar
        def _(act):
            act.wait_ge(eps_ready, 1)
            if n_loads:
                act.wait_ge(loaded, 16 * n_loads)

            def step(s, i, m, on):
                if on(lag_out):
                    c, slot = s - lag_out, (m - lag_out) % 3
                    act.wait_ge(rows_ps, c + 1)
                    wait(act, rows_stored[slot], 16 * (i + (m - lag_out) // 3))
                    nc.scalar.copy(rows[:, slot, :], ps_rows).then_inc(rows_ready, 1)
                if on(3) and norm:
                    c, slot = s - 3, (m - 3) % 3
                    act.wait_ge(centred_ready, c + 1)
                    wait(act, var_ps, c - 2)
                    nc.scalar.activation(square[:, slot, :], centred[:, slot, :], ACT.Square).then_inc(square_ready, 1)
                    act.wait_ge(var_ps, c + 1)
                    wait(act, x_ready, c - 2)
                    nc.scalar.activation(std[:, slot, :], ps_var, ACT.Sqrt, bias=eps_sb[:, 0:1]).then_inc(std_ready, 1)
                if on(2) and kind == "first_conv":
                    c, slot = s - 2, (m - 2) % 3
                    act.wait_ge(pre_ready, c + 1)
                    wait(act, next_ps, c - 2)
                    nc.scalar.activation(x_new[:, slot, :], pre[:, slot, :], ACT.Relu, bias=bias_sb[:, 0:1]).then_inc(x_ready, 1)
                if on(1) and kind == "max":
                    c, slot = s - 1, (m - 1) % 3
                    act.wait_ge(proj_ps, c + 1)
                    wait(act, r_ready, c - 2)
                    nc.scalar.activation(proj[:, slot, :], ps_proj, ACT.Relu, bias=bias_sb[:, 0:1]).then_inc(proj_ready, 1)
                    act.wait_ge(degree_ready, c + 1)
                    nc.scalar.activation(degree[:, slot, :], degree[:, slot, :], ACT.Sqrt).then_inc(root_ready, 1)

            pipeline(act, CHUNKS, lag_out, 3, step, peel=lag_out + 3)


def build(nc, t, out):
    with ExitStack() as ctx:
        mem = Memory(nc, ctx)
        prepare(nc, mem, t["dst_tiles"], t["next_tiles"], t["dst_flat"], t["prev_flat"], t["next_flat"], t["first_dst"])
        project_inputs(nc, mem, t["xT"], t["W_in"], t["b_in"], t["Wq"], t["bq"], t["Wk"], t["bk"], t["Wv"], t["bv"])
        attention(nc, mem, t["src_tiles"])
        node_stage(nc, mem, "attention", mem.rows_dram[0], x_from=t["xT"], x_to=mem.xT_dram[0])
        sum_layer(nc, mem, "w_", mem.rows_dram[0], t["src_tiles"], t["attr64"], t["attr8"])
        node_stage(nc, mem, "weighted", mem.rows_dram[1], x_from=mem.xT_dram[0], x_to=mem.xT_dram[1])
        min_layer(nc, mem, mem.rows_dram[1], t["src_tiles"])
        node_stage(nc, mem, "max", mem.rows_dram[2], x_from=mem.xT_dram[1], x_to=mem.xT_dram[2],
                   w=t["W_max"][0:D, :], w_low=t["W_max"][D:2 * D, :], bias=t["b_max"], w_next=t["W1"])
        sum_layer(nc, mem, "c1_", mem.rows_dram[2], t["src_tiles"])
        node_stage(nc, mem, "first_conv", mem.rows_dram[3], bias=t["b1"], w_next=t["W2"])
        sum_layer(nc, mem, "c2_", mem.rows_dram[3], t["src_tiles"])
        node_stage(nc, mem, "second_conv", out, x_from=mem.xT_dram[2], bias=t["b2"])


def kernel(**inputs):
    import numpy as np
    import concourse.bacc as bacc
    from concourse.bass_utils import run_bass_kernel_spmd as run

    edges = TILES * P
    nc = bacc.Bacc("TRN2", target_bir_lowering=False, num_devices=1)
    x, src, dst = (np.asarray(inputs[name]) for name in ("x", "src", "dst"))

    def padded(a, value):
        return np.concatenate([a, np.full((edges - len(a),) + a.shape[1:], value, a.dtype)])

    def tiles(a):
        return np.ascontiguousarray(a.reshape((TILES, P) + a.shape[1:]).swapaxes(0, 1))

    dst_flat = padded(dst, N)
    prev_flat = np.concatenate([np.full(1, -1, dst.dtype), dst_flat[:-1]])
    next_flat = np.concatenate([dst_flat[1:], np.full(1, -1, dst.dtype)])
    xT = np.zeros((P, NP), x.dtype)
    xT[:, :N] = x.T
    row = lambda name: np.asarray(inputs[name]).reshape(1, D)
    arrays = {
        "xT": xT,
        "src_tiles": tiles(padded(src, 0)),
        "dst_tiles": tiles(dst_flat),
        "next_tiles": tiles(next_flat),
        "dst_flat": dst_flat.reshape(P, TILES),
        "prev_flat": prev_flat.reshape(P, TILES),
        "next_flat": next_flat.reshape(P, TILES),
        "first_dst": np.ascontiguousarray(dst_flat[::P]).reshape(1, TILES),
        "attr64": tiles(padded(np.asarray(inputs["edge_attr_64"]), 0)),
        "attr8": tiles(padded(np.asarray(inputs["edge_attr_8"]), 0)),
        "W_in": np.asarray(inputs["L0_gnn_W_in"]), "b_in": row("L0_gnn_b_in"),
        "Wq": np.asarray(inputs["L0_gnn_Wq"]), "bq": row("L0_gnn_bq"),
        "Wk": np.asarray(inputs["L0_gnn_Wk"]), "bk": row("L0_gnn_bk"),
        "Wv": np.asarray(inputs["L0_gnn_Wv"]), "bv": row("L0_gnn_bv"),
        "W_max": np.asarray(inputs["L2_gnn_W"]), "b_max": row("L2_gnn_b"),
        "W1": np.asarray(inputs["L3_gnn_W1"]), "b1": row("L3_gnn_b1"),
        "W2": np.asarray(inputs["L3_gnn_W2"]), "b2": row("L3_gnn_b2"),
    }
    t = {name: nc.dram_tensor("in_" + name, a.shape, mybir.dt.from_np(a.dtype), kind="ExternalInput").ap()
         for name, a in arrays.items()}
    out = nc.dram_tensor("out", (NP, D), FP, kind="ExternalOutput").ap()
    build(nc, t, out)
    r = run(nc, [{"in_" + name: a for name, a in arrays.items()}], core_ids=[0])
    return r.results[0]["out"][:N]
```

```python
import concourse.bass as bass
from concourse import mybir
from contextlib import ExitStack


FP = mybir.dt.float32
BF = mybir.dt.bfloat16
I32 = mybir.dt.int32
ALU = mybir.AluOpType
ACT = mybir.ActivationFunctionType
AX = mybir.AxisListType

N = 12500
E = 212500
D = 128
HEADS = 8
DH = D // HEADS
P = 128
RING = 32
TILES = -(-E // (P * RING)) * RING
BATCHES = TILES // 8
CHUNK = 3 * P
CHUNKS = -(-(N + P) // CHUNK)
NP = CHUNKS * CHUNK
BIG = 3.0e38
TINY = 1e-30
EPS = 1e-5


def wait(engine, sem, value):
    if not isinstance(value, int) or value > 0:
        engine.wait_ge(sem, value)


def pipeline(engine, count, lag, unroll, emit, peel=0):
    head = -(-max(lag, unroll, peel) // unroll)
    full = count // unroll

    def peeled(first, last):
        for s in range(first, last):
            emit(s, s // unroll, s % unroll, lambda l, s=s: 0 <= s - l < count)

    peeled(0, head * unroll)
    with engine.Fori(head, full) as i:
        for m in range(unroll):
            emit(i * unroll + m, i, m, lambda l: True)
    peeled(full * unroll, count + lag)


class Memory:

    def __init__(self, nc, ctx):
        self.nc, self.ctx = nc, ctx
        self.acc = self.sb("acc", [P, NP])
        self.den = self.sb("den", [HEADS + 1, NP])
        self.rel = self.sb("rel", [P, TILES], BF)
        self.rel_end = self.sb("rel_end", [P, TILES], BF)
        self.base = self.sb("base", [1, TILES], I32)
        self.tight = self.sb("tight", [1, BATCHES], I32)
        self.iota = self.sb("iota", [P, P])
        self.ident = self.sb("ident", [P, P])
        self.ones = self.sb("ones", [P, P])
        self.count, self.mask, self.dinv = (self.sb(name, [P, NP // P]) for name in ("count", "mask", "dinv"))
        self.expand = self.sb("expand", [HEADS, P])
        self.idx = self.sb("idx", [P, RING], I32)
        self.bank = [ctx.enter_context(nc.psum_tensor(f"bank{i}", [P, 512], FP)) for i in range(8)]
        self.gathered = [self.sem(f"gathered{i}") for i in range(RING)]
        self.idx_loaded = [self.sem(f"idx_loaded{i}") for i in range(4)]
        self.q_dram = nc.dram_tensor("q_rows", [NP, D], FP, kind="Internal").ap()
        self.kv_dram = nc.dram_tensor("kv_rows", [NP, 2 * D], FP, kind="Internal").ap()
        self.rows_dram = [nc.dram_tensor(f"rows{i}", [NP, D], FP, kind="Internal").ap() for i in range(5)]
        self.start_neg = nc.dram_tensor("start_neg", [1, TILES * P], BF, kind="Internal").ap()
        self.end_neg = nc.dram_tensor("end_neg", [1, TILES * P], BF, kind="Internal").ap()
        self.start_pos = nc.dram_tensor("start_pos", [1, TILES * P], BF, kind="Internal").ap()
        self.gather_steps = self.sem("gather_steps")
        self.gather_rounds = 0

    def sb(self, name, shape, dt=FP):
        return self.ctx.enter_context(self.nc.sbuf_tensor(name, shape, dt))

    def sem(self, name):
        return self.ctx.enter_context(self.nc.semaphore(name))


def semaphores(nc, ctx, prefix):
    made = []

    def release():
        nc.clear_and_free_semaphores(made)
        nc.all_engine_barrier(sem_only=True)

    def sem(name):
        made.append(nc.alloc_semaphore(prefix + name))
        return made[-1]

    ctx.callback(release)
    return sem


def sb_in(nc, ctx, name, shape, dt=FP):
    return ctx.enter_context(nc.sbuf_tensor(name, shape, dt))


def load_tight(nc, mem, engine_type, batch):
    _, values = nc.values_load_multi_w_load_instructions(
        mem.tight[0:1, bass.ds(batch, 1)], engines=[engine_type], min_val=0, max_val=1,
        skip_runtime_bounds_check_because="the result of a comparison")
    return values[0]


def load_bases(nc, mem, engine_type, first, count):
    _, values = nc.values_load_multi_w_load_instructions(
        mem.base[0:1, bass.ds(first, count)], engines=[engine_type], min_val=0, max_val=N,
        skip_runtime_bounds_check_because="dst lies in 0..N-1 and the padding edges have N")
    return values


def prepare(nc, mem, dst_tiles, next_tiles, dst_flat, prev_flat, next_flat, first_dst, batch_last):
    with ExitStack() as ctx:
        sem = semaphores(nc, ctx, "p_")
        tmp = sb_in(nc, ctx, "prep_i", [P, 5, TILES], I32)
        f = sb_in(nc, ctx, "prep_f", [P, 4, TILES])
        pen = sb_in(nc, ctx, "prep_pen", [P, 3, TILES], BF)
        first = sb_in(nc, ctx, "prep_first", [1, TILES], I32)
        last = sb_in(nc, ctx, "prep_last", [1, BATCHES], I32)
        span = sb_in(nc, ctx, "prep_span", [1, BATCHES])
        tight = sb_in(nc, ctx, "prep_tight", [1, BATCHES])
        base = sb_in(nc, ctx, "prep_base", [1, TILES])
        loaded, rows_loaded, stored = sem("loaded"), sem("rows_loaded"), sem("stored")
        filled, ones_ready, ident_ready = sem("filled"), sem("ones_ready"), sem("ident_ready")
        base_ready, bc_ready, step, pens_ready = sem("base_ready"), sem("bc_ready"), sem("step"), sem("pens_ready")
        block = ctx.enter_context(nc.Block())
        quarter = TILES // 4

        @block.sync
        def _(sp):
            sp.dma_start(first[:, :], first_dst).then_inc(rows_loaded, 16)
            sp.dma_start(last[:, :], batch_last).then_inc(rows_loaded, 16)
            for i, src in enumerate((dst_tiles, next_tiles, dst_flat, prev_flat, next_flat)):
                sp.dma_start(tmp[:, i, :], src).then_inc(loaded, 16)
            sp.wait_ge(pens_ready, 3)
            for i, dst in enumerate((mem.start_neg, mem.end_neg, mem.start_pos)):
                sp.dma_start(dst.rearrange("o (p c) -> (o p) c", p=P), pen[:, i, :]).then_inc(stored, 16)
            sp.wait_ge(stored, 48)

        @block.gpsimd
        def _(pool):
            nc.gpsimd.memset(mem.ones[:, :], 1.0).then_inc(ones_ready, 1)
            nc.gpsimd.iota(mem.iota[:, :], [[1, P]], base=0, channel_multiplier=0,
                           allow_small_or_imprecise_dtypes=True)
            pool.wait_ge(ones_ready, 1)
            nc.gpsimd.affine_select(mem.ident[:, :], mem.ones[:, :], [[-1, P]], ALU.is_equal, 0.0,
                                    base=0, channel_multiplier=1)
            nc.gpsimd.affine_select(mem.expand[:, :].rearrange("h (d g) -> h d g", g=HEADS),
                                    mem.ones[0:HEADS, :].rearrange("h (d g) -> h d g", g=HEADS),
                                    [[0, DH], [-1, HEADS]], ALU.is_equal, 0.0,
                                    base=0, channel_multiplier=1)
            nc.gpsimd.memset(mem.den[:, :], 0.0)

        @block.tensor
        def _(pe):
            pe.wait_ge(ones_ready, 1)
            pe.wait_ge(base_ready, 1)
            for c in range(4):
                nc.tensor.matmul(mem.bank[c][:, 0:quarter], mem.ones[0:1, :], base[:, c * quarter:(c + 1) * quarter],
                                 start=True, stop=True).then_inc(bc_ready, 1)

        @block.vector
        def _(dve):
            by_batch = lambda row: row.rearrange("o (b t) -> o b t", t=8)
            firsts = by_batch(first[:, :])
            batch_first = firsts[:, :, 0:1]
            dve.wait_ge(rows_loaded, 32)
            nc.vector.tensor_tensor(span[:, :], last[:, :], batch_first.rearrange("o b t -> o (b t)"), ALU.subtract).then_inc(step, 1)
            nc.vector.tensor_tensor(by_batch(base[:, :]), batch_first.to_broadcast([1, BATCHES, 8]), firsts, ALU.subtract).then_inc(step, 1)
            dve.wait_ge(step, 2)
            nc.vector.tensor_scalar(tight[:, :], span[:, :], float(P), None, ALU.is_lt).then_inc(step, 1)
            dve.wait_ge(step, 3)
            nc.vector.tensor_tensor(by_batch(base[:, :]), by_batch(base[:, :]), tight[:, :].unsqueeze(2).to_broadcast([1, BATCHES, 8]),
                                    ALU.mult).then_inc(step, 1)
            nc.vector.tensor_copy(mem.tight[:, :], tight[:, :])
            dve.wait_ge(step, 4)
            nc.vector.tensor_tensor(base[:, :], base[:, :], first[:, :], ALU.add).then_inc(base_ready, 1)
            dve.wait_ge(base_ready, 1)
            nc.vector.tensor_copy(mem.base[:, :], base[:, :])
            dve.wait_ge(loaded, 80)
            nc.vector.tensor_tensor(f[:, 2, :], tmp[:, 2, :], tmp[:, 3, :], ALU.not_equal).then_inc(step, 1)
            nc.vector.tensor_tensor(f[:, 3, :], tmp[:, 2, :], tmp[:, 4, :], ALU.not_equal).then_inc(step, 1)
            dve.wait_ge(step, 6)
            nc.vector.tensor_scalar(pen[:, 0, :], f[:, 2, :], -BIG, None, ALU.mult).then_inc(pens_ready, 1)
            nc.vector.tensor_scalar(pen[:, 1, :], f[:, 3, :], -BIG, None, ALU.mult).then_inc(pens_ready, 1)
            nc.vector.tensor_scalar(pen[:, 2, :], f[:, 2, :], BIG, None, ALU.mult).then_inc(pens_ready, 1)
            nc.vector.tensor_tensor(f[:, 1, :], tmp[:, 0, :], tmp[:, 1, :], ALU.not_equal).then_inc(step, 1)
            dve.wait_ge(bc_ready, 4)
            for c in range(4):
                cols = slice(c * quarter, (c + 1) * quarter)
                nc.vector.tensor_tensor(f[:, 0, cols], tmp[:, 0, cols], mem.bank[c][:, 0:quarter],
                                        ALU.subtract).then_inc(step, 1)
            dve.wait_ge(step, 11)
            nc.vector.tensor_copy(mem.rel[:, :], f[:, 0, :])
            dve.wait_ge(pens_ready, 3)
            nc.vector.scalar_tensor_tensor(f[:, 2, :], f[:, 0, :], 1.0, f[:, 1, :], ALU.add, ALU.mult).then_inc(step, 1)
            dve.wait_ge(step, 12)
            nc.vector.tensor_scalar(mem.rel_end[:, :], f[:, 2, :], -1.0, None, ALU.add)
            nc.vector.memset(mem.acc[:, :], 0.0)


def project_inputs(nc, mem, xT, W_in, b_in, Wq, bq, Wk, bk, Wv, bv):
    with ExitStack() as ctx:
        sem = semaphores(nc, ctx, "d_")
        w_in = sb_in(nc, ctx, "w_in", [P, D])
        w_qkv = sb_in(nc, ctx, "w_qkv", [P, 3 * D])
        bias_in = sb_in(nc, ctx, "bias_in", [P, 1])
        bias_qkv = sb_in(nc, ctx, "bias_qkv", [P, 3 * D])
        x_in = sb_in(nc, ctx, "x_in", [P, 3, CHUNK])
        hT = sb_in(nc, ctx, "hT", [P, 3, CHUNK])
        qkv = sb_in(nc, ctx, "qkv", [P, 3, 3, 3 * D])
        w_loaded, scaled = sem("w_loaded"), sem("scaled")
        x_loaded = [sem(f"x_loaded{i}") for i in range(3)]
        stored = [sem(f"stored{i}") for i in range(3)]
        h_ready, hT_ready, qkv_ps_ready, qkv_ready = sem("h_ready"), sem("hT_ready"), sem("qkv_ps_ready"), sem("qkv_ready")
        block = ctx.enter_context(nc.Block())
        q_view = mem.q_dram.rearrange("(c k p) f -> c p k f", k=3, p=P)
        kv_view = mem.kv_dram.rearrange("(c k p) f -> c p k f", k=3, p=P)

        @block.sync
        def _(sp):
            sp.dma_start(w_in[:, :], W_in).then_inc(w_loaded, 16)
            for i, (w, b) in enumerate(((Wq, bq), (Wk, bk), (Wv, bv))):
                sp.dma_start(w_qkv[:, i * D:(i + 1) * D], w).then_inc(w_loaded, 16)
                sp.dma_start(bias_qkv[:, i * D:(i + 1) * D], b.to_broadcast([P, D])).then_inc(w_loaded, 16)
            sp.dma_start(bias_in[:, :], b_in.rearrange("o f -> f o")).then_inc(w_loaded, 16)

            def load_and_store(s, i, m, on):
                if on(0):
                    wait(sp, h_ready, s - 2)
                    sp.dma_start(x_in[:, m, :], xT[:, bass.ds(s * CHUNK, CHUNK)]).then_inc(x_loaded[m], 16)
                if on(2):
                    c, slot = s - 2, (m - 2) % 3
                    sp.wait_ge(qkv_ready, (c + 1) * 3)
                    sp.dma_start(q_view[bass.ds(c, 1), :, :, :].rearrange("o p k f -> (o p) k f"),
                                 qkv[:, slot, :, 0:D]).then_inc(stored[slot], 16)
                    sp.dma_start(kv_view[bass.ds(c, 1), :, :, :].rearrange("o p k f -> (o p) k f"),
                                 qkv[:, slot, :, D:3 * D]).then_inc(stored[slot], 16)

            pipeline(sp, CHUNKS, 2, 3, load_and_store)
            for i in range(3):
                sp.wait_ge(stored[i], 32 * (CHUNKS // 3))

        @block.tensor
        def _(pe):
            pe.wait_ge(w_loaded, 128)
            pe.wait_ge(scaled, 2)

            def products(s, i, m, on):
                if on(0):
                    pe.wait_ge(x_loaded[m], 16 * (i + 1))
                    wait(pe, hT_ready, s)
                    nc.tensor.matmul(mem.bank[0][:, 0:CHUNK], w_in[:, :], x_in[:, m, :], start=True, stop=True).then_inc(h_ready, 1)
                if on(1):
                    c, slot = s - 1, (m - 1) % 3
                    pe.wait_ge(hT_ready, c + 1)
                    for k in range(3):
                        wait(pe, qkv_ready, c * 3 + k - 2)
                        nc.tensor.matmul(mem.bank[1 + k][:, 0:3 * D], hT[:, slot, k * P:(k + 1) * P], w_qkv[:, :],
                                         start=True, stop=True).then_inc(qkv_ps_ready, 1)

            pipeline(pe, CHUNKS, 1, 3, products)

        @block.scalar
        def _(act):
            act.wait_ge(w_loaded, 128)

            def add_bias(s, i, m, on):
                act.wait_ge(h_ready, s + 1)
                wait(act, qkv_ps_ready, (s - 2) * 3)
                nc.scalar.activation(hT[:, m, :], mem.bank[0][:, 0:CHUNK], ACT.Identity, bias=bias_in[:, 0:1]).then_inc(hT_ready, 1)

            pipeline(act, CHUNKS, 0, 3, add_bias)

        @block.vector
        def _(dve):
            dve.wait_ge(w_loaded, 128)
            nc.vector.tensor_scalar(w_qkv[:, 0:D], w_qkv[:, 0:D], DH ** -0.5, None, ALU.mult).then_inc(scaled, 1)
            nc.vector.tensor_scalar(bias_qkv[:, 0:D], bias_qkv[:, 0:D], DH ** -0.5, None, ALU.mult).then_inc(scaled, 1)
            dve.wait_ge(scaled, 2)

            def add_bias(s, i, m, on):
                wait(dve, stored[m], 32 * i)
                for k in range(3):
                    dve.wait_ge(qkv_ps_ready, s * 3 + k + 1)
                    nc.vector.tensor_tensor(qkv[:, m, k, :], mem.bank[1 + k][:, 0:3 * D], bias_qkv[:, :],
                                            ALU.add).then_inc(qkv_ready, 1)

            pipeline(dve, CHUNKS, 0, 3, add_bias)


def mark_targets(nc, mem, rel, out, batch):
    targets = rel[:, bass.ds(8 * batch, 8)].unsqueeze(2).to_broadcast([P, 8, P])
    nodes = mem.iota[:, :].unsqueeze(1).to_broadcast([P, 8, P])
    return nc.vector.tensor_tensor(out, nodes, targets, ALU.is_equal)


def gather_rows(nc, mem, pool, table, ring, steps, released, released_per_step, rounds):

    def gather(s, i, m, on):
        pool.wait_ge(mem.idx_loaded[m], 16 * (rounds + i + 1))
        wait(pool, released, released_per_step * (s - 3))
        pool.sem_inc(mem.gather_steps, 1)
        for k in range(8):
            slot = 8 * m + k
            pool.indirect_dma_start(ring[:, slot, :], None, table,
                                    bass.IndirectOffsetOnAxis(ap=mem.idx[:, slot:slot + 1], axis=0)
                                    ).then_inc(mem.gathered[slot], 16)

    pipeline(pool, steps, 0, 4, gather)


def load_idx(mem, sp, src_tiles, s, m, used, used_per_step):
    wait(sp, used, used_per_step * (s - 3))
    sp.dma_start(mem.idx[:, 8 * m:8 * m + 8], src_tiles[:, bass.ds(8 * s, 8)]).then_inc(mem.idx_loaded[m], 16)


def attention(nc, mem, src_tiles):
    rounds = mem.gather_rounds
    mem.gather_rounds += TILES // RING
    wide = D + HEADS + 1
    with ExitStack() as ctx:
        sem = semaphores(nc, ctx, "a_")
        kv = sb_in(nc, ctx, "kv", [P, RING, 2 * D])
        onehot = sb_in(nc, ctx, "onehot", [P, RING, P])
        onehotT = sb_in(nc, ctx, "onehotT", [P, 2, 4 * P])
        q_win = sb_in(nc, ctx, "q_win", [P, 2, 8, D])
        prod = sb_in(nc, ctx, "prod", [P, 2, 4 * D])
        pv = sb_in(nc, ctx, "pv", [P, 2, 8, wide])
        score = sb_in(nc, ctx, "score", [P, 2, 8 * HEADS])
        below = sb_in(nc, ctx, "below", [P, 8 * HEADS])
        total = sb_in(nc, ctx, "total", [P, wide])
        scan = sb_in(nc, ctx, "scan", [HEADS, 8 * P])
        resets = sb_in(nc, ctx, "resets", [HEADS, 2, 2, 8 * P], BF)
        carry = sb_in(nc, ctx, "carry", [HEADS, 2])
        gap = sb_in(nc, ctx, "gap", [HEADS, 1])
        alpha = sb_in(nc, ctx, "alpha", [HEADS, 1])
        ps_onehotT, ps_q, ps_score, ps_ref, ps_total, ps_win = mem.bank[0:2], mem.bank[2:4], *mem.bank[4:8]
        q_loaded = [sem(f"q_loaded{i}") for i in range(2)]
        resets_loaded = [sem(f"resets_loaded{i}") for i in range(2)]
        windows_ready, added = sem("windows_ready"), sem("added")
        onehotT_ps, onehotT_ready, qe_ready = sem("onehotT_ps"), sem("onehotT_ready"), sem("qe_ready")
        prod_ready, score_ready, pv_ready = sem("prod_ready"), sem("score_ready"), sem("pv_ready")
        score_ps, scan_loaded = sem("score_ps"), sem("scan_loaded")
        forward_done, carry_ready, backward_done, gap_ready = sem("forward_done"), sem("carry_ready"), sem("backward_done"), sem("gap_ready")
        ref_steps, ref_ps, below_ready, p_ready = sem("ref_steps"), sem("ref_ps"), sem("below_ready"), sem("p_ready")
        alpha_ready, alpha_ps, rescaled = sem("alpha_ready"), sem("alpha_ps"), sem("rescaled")
        q_steps, add_steps, product_steps = sem("q_steps"), sem("add_steps"), sem("product_steps")
        onehot_ready, products_done, total_copied = sem("onehot_ready"), sem("products_done"), sem("total_copied")
        block = ctx.enter_context(nc.Block())

        @block.sync
        def _(sp):
            def loads(s, i, m, on):
                if on(2):
                    b, par = s - 2, m % 2
                    wait(sp, qe_ready, 2 * (b - 1))
                    sp.sem_inc(q_steps, 1)
                    bases = load_bases(nc, mem, mybir.EngineType.SP, 8 * b, 8)
                    with sp.If(load_tight(nc, mem, mybir.EngineType.SP, b)):
                        sp.dma_start(q_win[:, par, 0, :], mem.q_dram[bass.ds(bases[0], P), :]).then_inc(q_loaded[par], 128)
                    with sp.Else():
                        for k in range(8):
                            sp.dma_start(q_win[:, par, k, :], mem.q_dram[bass.ds(bases[k], P), :]).then_inc(q_loaded[par], 16)
                if on(0):
                    load_idx(mem, sp, src_tiles, s, m, score_ready, 2)
                if on(2):
                    wait(sp, backward_done, b - 1)
                    edges = bass.ds(8 * P * b, 8 * P)
                    sp.dma_start(resets[:, par, 0, :], mem.start_neg[:, edges].to_broadcast([HEADS, 8 * P])).then_inc(resets_loaded[par], 16)
                    sp.dma_start(resets[:, par, 1, :], mem.end_neg[:, edges].to_broadcast([HEADS, 8 * P])).then_inc(resets_loaded[par], 16)

            pipeline(sp, BATCHES, 2, 4, loads)

        @block.gpsimd
        def _(pool):
            gather_rows(nc, mem, pool, mem.kv_dram, kv, BATCHES, pv_ready, 2, rounds)

        @block.vector
        def _(dve):
            nc.vector.memset(carry[:, :], 0.0).then_inc(carry_ready, 1)
            nc.vector.memset(pv[:, :, :, D + HEADS:wide], 1.0)

            def batch(s, i, m, on):
                m1, m2, m3 = (m - 1) % 4, (m - 2) % 4, (m - 3) % 4
                if on(1):
                    for g in range(2):
                        q, slot = 2 * (s - 1) + g, 8 * m1 + 4 * g
                        dve.wait_ge(qe_ready, q + 1)
                        for k in range(4):
                            dve.wait_ge(mem.gathered[slot + k], 16 * (rounds + i + 1 - int(m < 1)))
                        wait(dve, score_ready, q - 1)
                        nc.vector.tensor_tensor(prod[:, g, :].rearrange("e (k f) -> e k f", k=4), kv[:, slot:slot + 4, 0:D],
                                                ps_q[g][:, :].rearrange("e (k f) -> e k f", k=4), ALU.mult).then_inc(prod_ready, 1)
                if on(4):
                    first = load_bases(nc, mem, mybir.EngineType.DVE, 8 * (s - 4), 1)[0]
                    tight = load_tight(nc, mem, mybir.EngineType.DVE, s - 4)
                if on(3):
                    node = bass.ds(load_bases(nc, mem, mybir.EngineType.DVE, 8 * (s - 3), 1)[0], 1)
                if on(1):
                    for g in range(2):
                        q = 2 * (s - 1) + g
                        dve.wait_ge(prod_ready, q + 1)
                        if g == 0:
                            wait(dve, below_ready, s - 2)
                        nc.vector.tensor_reduce(score[:, m1 % 2, g * 32:g * 32 + 32],
                                                prod[:, g, :].rearrange("e (k d h) -> e k h d", k=4, h=HEADS),
                                                AX.X, ALU.add).then_inc(score_ready, 1)
                if on(4):
                    b = s - 4
                    wait(dve, rescaled, b + 1)
                    wait(dve, windows_ready, 8 * b)
                    dve.sem_inc(add_steps, 1)
                    with dve.If(tight):
                        dve.wait_ge(products_done, b + 1)
                        if on(3):
                            dve.wait_ge(alpha_ps, b + 2)
                        nc.vector.tensor_copy(total[:, :], ps_total[:, 0:wide]).then_inc(total_copied, 1)
                    with dve.Else():
                        bases = load_bases(nc, mem, mybir.EngineType.DVE, 8 * b, 8)
                        for k in range(8):
                            dve.wait_ge(windows_ready, 8 * b + k + 1)
                            wait(dve, added, 8 * b + k)
                            window = mem.acc[:, bass.ds(bases[k], P)]
                            nc.vector.tensor_tensor(window, window, ps_win[:, 0:P], ALU.add)
                            window = mem.den[:, bass.ds(bases[k], P)]
                            nc.vector.tensor_tensor(window, window, ps_win[0:HEADS + 1, P:2 * P], ALU.add).then_inc(added, 1)
                        dve.sem_inc(total_copied, 1)
                if on(0):
                    wait(dve, products_done, s - 3)
                    mark_targets(nc, mem, mem.rel, onehot[:, 8 * m:8 * m + 8, :], s).then_inc(onehot_ready, 1)
                if on(3):
                    b = s - 3
                    dve.wait_ge(p_ready, b + 1)
                    wait(dve, products_done, b - 1)
                    for g in range(2):
                        slot = 8 * m3 + 4 * g
                        p = pv[:, m3 % 2, 4 * g:4 * g + 4, D:D + HEADS].unsqueeze(2).to_broadcast([P, 4, DH, HEADS])
                        nc.vector.tensor_tensor(pv[:, m3 % 2, 4 * g:4 * g + 4, 0:D].rearrange("e k (d h) -> e k d h", h=HEADS),
                                                kv[:, slot:slot + 4, D:2 * D].rearrange("e k (d h) -> e k d h", h=HEADS), p,
                                                ALU.mult).then_inc(pv_ready, 1)
                if on(2):
                    c, par = s - 2, m2 % 2
                    dve.wait_ge(scan_loaded, 2 * (c + 1))
                    dve.wait_ge(resets_loaded[par], 32 * (2 * (i - int(m < 2)) + m2 // 2 + 1))
                    dve.wait_ge(carry_ready, c + 1)
                    nc.vector.tensor_tensor_scan(scan[:, :], resets[:, par, 0, :], scan[:, :], carry[:, 1 - par:2 - par],
                                                 ALU.add, ALU.max).then_inc(forward_done, 1)
                if on(2):
                    dve.wait_ge(forward_done, c + 1)
                    wait(dve, gap_ready, c)
                    nc.vector.tensor_copy(carry[:, par:par + 1], scan[:, 8 * P - 1:8 * P]).then_inc(carry_ready, 1)
                if on(2):
                    dve.wait_ge(carry_ready, c + 2)
                    nc.vector.tensor_tensor_scan(scan[:, ::-1], resets[:, par, 1, ::-1], scan[:, ::-1], -BIG,
                                                 ALU.add, ALU.max).then_inc(backward_done, 1)
                if on(4):
                    b = s - 4
                    with dve.If(tight):
                        dve.wait_ge(windows_ready, 8 * (b + 1))
                        window = mem.acc[:, bass.ds(first, P)]
                        nc.vector.tensor_tensor(window, window, ps_win[:, 0:P], ALU.add)
                        window = mem.den[:, bass.ds(first, P)]
                        nc.vector.tensor_tensor(window, window, ps_win[0:HEADS + 1, P:2 * P], ALU.add).then_inc(added, 8)
                    with dve.Else():
                        dve.sem_inc(add_steps, 1)
                if on(2):
                    dve.wait_ge(backward_done, c + 1)
                    wait(dve, alpha_ready, c)
                    nc.vector.tensor_scalar(gap[:, :], carry[:, 1 - par:2 - par], scan[:, 0:1], 0.0,
                                            ALU.subtract, ALU.min).then_inc(gap_ready, 1)
                if on(3):
                    b = s - 3
                    dve.wait_ge(alpha_ps, b + 1)
                    wait(dve, added, 8 * b)
                    nc.vector.tensor_scalar(mem.acc[:, node], mem.acc[:, node], ps_total[:, 256:257], None, ALU.mult)
                    nc.vector.tensor_scalar(mem.den[0:HEADS, node], mem.den[0:HEADS, node], alpha[:, :], None, ALU.mult).then_inc(rescaled, 1)
                if on(2):
                    dve.wait_ge(ref_ps, c + 1)
                    wait(dve, p_ready, c)
                    nc.vector.tensor_tensor(below[:, :], score[:, par, :], ps_ref[:, 0:64],
                                            ALU.subtract).then_inc(below_ready, 1)

            pipeline(dve, BATCHES, 4, 4, batch)

        @block.tensor
        def _(pe):
            def batch(s, i, m, on):
                m2 = (m - 2) % 4
                c, par = s - 2, m2 % 2
                def scores_to_heads(g):
                    q = 2 * c + g
                    pe.wait_ge(score_ready, q + 1)
                    wait(pe, scan_loaded, q)
                    for k in range(4):
                        last = nc.tensor.transpose(ps_score[0:HEADS, k * P:(k + 1) * P],
                                                   score[:, par, (4 * g + k) * HEADS:(4 * g + k + 1) * HEADS], mem.ident[:, :])
                    last.then_inc(score_ps, 1)

                def targets_to_edges(g):
                    wait(pe, onehotT_ready, 2 * s + g - 1)
                    pe.wait_ge(onehot_ready, s + 1)
                    for k in range(4):
                        last = nc.tensor.transpose(ps_onehotT[g][:, k * P:(k + 1) * P], onehot[:, 8 * m + 4 * g + k, :],
                                                   mem.ident[:, :])
                    last.then_inc(onehotT_ps, 1)

                if on(4):
                    tight = load_tight(nc, mem, mybir.EngineType.PE, s - 4)
                if on(4):
                    b = s - 4
                    pe.wait_ge(pv_ready, 2 * (b + 1))
                    wait(pe, total_copied, b)
                    wait(pe, rescaled, b + 1)
                    pe.sem_inc(product_steps, 1)
                    with pe.If(tight):
                        for k in range(8):
                            last = nc.tensor.matmul(ps_total[:, 0:wide], onehot[:, 8 * m + k, :], pv[:, m % 2, k, :],
                                                    start=(k == 0), stop=(k == 7))
                        last.then_inc(products_done, 1)
                    with pe.Else():
                        for k in range(8):
                            wait(pe, added, 8 * b + k)
                            nc.tensor.matmul(ps_win[:, 0:P], pv[:, m % 2, k, 0:D], onehot[:, 8 * m + k, :], start=True, stop=True)
                            last = nc.tensor.matmul(ps_win[0:HEADS + 1, P:2 * P], pv[:, m % 2, k, D:wide], onehot[:, 8 * m + k, :],
                                                    start=True, stop=True)
                            last.then_inc(windows_ready, 1)
                        wait(pe, windows_ready, 8 * (b + 1))
                        pe.sem_inc(products_done, 1)
                if on(3):
                    pe.wait_ge(alpha_ready, s - 2)
                    wait(pe, rescaled, s - 3)
                    wait(pe, total_copied, s - 4)
                    nc.tensor.matmul(ps_total[:, 256:257], mem.expand[:, :], alpha[:, :], start=True, stop=True).then_inc(alpha_ps, 1)
                if on(0):
                    tight_q = load_tight(nc, mem, mybir.EngineType.PE, s)
                if on(2):
                    scores_to_heads(0)
                    scores_to_heads(1)
                if on(0):
                    targets_to_edges(0)
                    targets_to_edges(1)
                if on(4):
                    with pe.If(tight):
                        pe.wait_ge(total_copied, b + 1)
                        wait(pe, added, 8 * b)
                        nc.tensor.transpose(ps_win[:, 0:P], total[:, 0:D], mem.ident[:, :])
                        nc.tensor.transpose(ps_win[0:HEADS + 1, P:2 * P], total[:, D:wide], mem.ident[:, :]).then_inc(windows_ready, 8)
                    with pe.Else():
                        pe.sem_inc(product_steps, 1)
                if on(0):
                    pe.wait_ge(q_loaded[m % 2], 128 * (2 * i + m // 2 + 1))
                    pe.sem_inc(product_steps, 1)

                    def q_of_edges(shared):
                        for g in range(2):
                            q = 2 * s + g
                            pe.wait_ge(onehotT_ready, q + 1)
                            wait(pe, prod_ready, q - 1)
                            for k in range(4):
                                last = nc.tensor.matmul(ps_q[g][:, k * D:(k + 1) * D], onehotT[:, g, k * P:(k + 1) * P],
                                                        q_win[:, m % 2, 0 if shared else 4 * g + k, :], start=True, stop=True)
                            last.then_inc(qe_ready, 1)

                    with pe.If(tight_q):
                        q_of_edges(True)
                    with pe.Else():
                        q_of_edges(False)
                if on(2):
                    pe.wait_ge(backward_done, c + 1)
                    wait(pe, below_ready, c)
                    pe.sem_inc(ref_steps, 1)
                    for k in range(8):
                        last = nc.tensor.transpose(ps_ref[:, k * HEADS:(k + 1) * HEADS], scan[:, k * P:(k + 1) * P],
                                                   mem.ident[0:HEADS, 0:HEADS])
                    last.then_inc(ref_ps, 1)

            pipeline(pe, BATCHES, 4, 4, batch)

        @block.scalar
        def _(act):
            def batch(s, i, m, on):
                c, par = s - 2, (m - 2) % 4 % 2
                if on(2):
                    for g in range(2):
                        act.wait_ge(score_ps, 2 * c + g + 1)
                        if g == 0:
                            wait(act, ref_ps, c)
                            wait(act, gap_ready, c)
                        nc.scalar.copy(scan[:, g * 512:g * 512 + 512], ps_score[0:HEADS, :]).then_inc(scan_loaded, 1)
                if on(0):
                    for g in range(2):
                        q = 2 * s + g
                        act.wait_ge(onehotT_ps, q + 1)
                        wait(act, qe_ready, q - 1)
                        nc.scalar.copy(onehotT[:, g, :], ps_onehotT[g][:, :]).then_inc(onehotT_ready, 1)
                if on(2):
                    act.wait_ge(gap_ready, c + 1)
                    wait(act, rescaled, c)
                    nc.scalar.activation(alpha[:, :], gap[:, :], ACT.Exp).then_inc(alpha_ready, 1)
                    act.wait_ge(below_ready, c + 1)
                    wait(act, products_done, c - 1)
                    nc.scalar.activation(pv[:, par, :, D:D + HEADS], below[:, :].rearrange("e (k h) -> e k h", h=HEADS),
                                         ACT.Exp).then_inc(p_ready, 1)

            pipeline(act, BATCHES, 4, 4, batch)


def sum_layer(nc, mem, name, table, src_tiles, attr64=None, attr8=None):
    rounds = mem.gather_rounds
    mem.gather_rounds += TILES // RING
    weighted = attr64 is not None
    with ExitStack() as ctx:
        sem = semaphores(nc, ctx, name)
        rows = sb_in(nc, ctx, name + "rows", [P, RING, D])
        onehot = sb_in(nc, ctx, name + "onehot", [P, 2, 8, P])
        if weighted:
            scaled = sb_in(nc, ctx, name + "scaled", [P, 2, 8, D])
            a64 = sb_in(nc, ctx, name + "a64", [P, 2, 8, 64])
            a8 = sb_in(nc, ctx, name + "a8", [P, 2, 8, 8])
            sum64 = sb_in(nc, ctx, name + "sum64", [P, 8])
            sum8 = sb_in(nc, ctx, name + "sum8", [P, 8])
            weight = sb_in(nc, ctx, name + "weight", [P, 2, 8])
            attrs_loaded = [sem(f"attrs_loaded{i}") for i in range(2)]
            attrs_summed, weight_ready, scaled_ready = sem("attrs_summed"), sem("weight_ready"), sem("scaled_ready")
        zeroed, onehot_ready, sums_ready, added = sem("zeroed"), sem("onehot_ready"), sem("sums_ready"), sem("added")
        block = ctx.enter_context(nc.Block())

        @block.sync
        def _(sp):
            def loads(s, i, m, on):
                load_idx(mem, sp, src_tiles, s, m, sums_ready, 8)
                if weighted:
                    wait(sp, attrs_summed, 2 * (s - 1))
                    sp.dma_start(a64[:, m % 2, :, :], attr64[:, bass.ds(8 * s, 8), :]).then_inc(attrs_loaded[m % 2], 16)
                    sp.dma_start(a8[:, m % 2, :, :], attr8[:, bass.ds(8 * s, 8), :]).then_inc(attrs_loaded[m % 2], 16)

            pipeline(sp, BATCHES, 0, 4, loads)

        @block.gpsimd
        def _(pool):
            if weighted:
                gather_rows(nc, mem, pool, table, rows, BATCHES, scaled_ready, 8, rounds)
            else:
                gather_rows(nc, mem, pool, table, rows, BATCHES, sums_ready, 8, rounds)

        @block.vector
        def _(dve):
            nc.vector.memset(mem.acc[:, :], 0.0).then_inc(zeroed, 1)

            def step(s, i, m, on):
                if on(0) and weighted:
                    dve.wait_ge(attrs_loaded[m % 2], 32 * (2 * i + m // 2 + 1))
                    wait(dve, weight_ready, s)
                    nc.vector.tensor_reduce(sum64[:, :], a64[:, m % 2, :, :], AX.X, ALU.add).then_inc(attrs_summed, 1)
                    nc.vector.tensor_reduce(sum8[:, :], a8[:, m % 2, :, :], AX.X, ALU.add).then_inc(attrs_summed, 1)
                    dve.wait_ge(attrs_summed, 2 * (s + 1))
                    wait(dve, scaled_ready, 8 * (s - 1))
                    nc.vector.tensor_tensor(weight[:, m % 2, :], sum64[:, :], sum8[:, :], ALU.mult).then_inc(weight_ready, 1)
                if on(0):
                    wait(dve, sums_ready, 8 * (s - 1))
                    mark_targets(nc, mem, mem.rel, onehot[:, m % 2, :, :], s).then_inc(onehot_ready, 1)
                if on(1):
                    bases = load_bases(nc, mem, mybir.EngineType.DVE, 8 * (s - 1), 8)
                    for k in range(8):
                        t, bank = 8 * (s - 1) + k, (m - 1) % 2 * 2 + k // 4
                        dve.wait_ge(sums_ready, t + 4 - k % 4)
                        if isinstance(s, int) and s == 1 and k == 0:
                            dve.wait_ge(zeroed, 1)
                        wait(dve, added, t)
                        window = mem.acc[:, bass.ds(bases[k], P)]
                        nc.vector.tensor_tensor(window, window, mem.bank[bank][:, k % 4 * P:(k % 4 + 1) * P], ALU.add).then_inc(added, 1)

            pipeline(dve, BATCHES, 1, 4, step)

        if weighted:
            @block.scalar
            def _(act):
                def scale(s, i, m, on):
                    act.wait_ge(weight_ready, s + 1)
                    for k in range(8):
                        t, slot = 8 * s + k, 8 * m + k
                        act.wait_ge(mem.gathered[slot], 16 * (rounds + i + 1))
                        wait(act, sums_ready, t - 15)
                        nc.scalar.activation(scaled[:, m % 2, k, :], rows[:, slot, :], ACT.Copy,
                                             scale=weight[:, m % 2, k:k + 1]).then_inc(scaled_ready, 1)

                pipeline(act, BATCHES, 0, 4, scale)

        @block.tensor
        def _(pe):
            def sums(s, i, m, on):
                for k in range(8):
                    t, slot, bank = 8 * s + k, 8 * m + k, m % 2 * 2 + k // 4
                    if k % 4 == 0:
                        wait(pe, added, t - 12)
                    if k == 0:
                        pe.wait_ge(onehot_ready, s + 1)
                    if weighted:
                        pe.wait_ge(scaled_ready, t + 1)
                        source = scaled[:, m % 2, k, :]
                    else:
                        pe.wait_ge(mem.gathered[slot], 16 * (rounds + i + 1))
                        source = rows[:, slot, :]
                    nc.tensor.matmul(mem.bank[bank][:, k % 4 * P:(k % 4 + 1) * P], source, onehot[:, m % 2, k, :],
                                     start=True, stop=True).then_inc(sums_ready, 1)

            pipeline(pe, BATCHES, 0, 4, sums)


def min_layer(nc, mem, table, src_tiles):
    rounds = mem.gather_rounds
    mem.gather_rounds += TILES // RING
    with ExitStack() as ctx:
        sem = semaphores(nc, ctx, "m_")
        rows = sb_in(nc, ctx, "m_rows", [P, RING, D])
        lasts = sb_in(nc, ctx, "lasts", [P, 2, 8, P])
        resets = sb_in(nc, ctx, "m_resets", [P, 2, 8 * P], BF)
        minT = sb_in(nc, ctx, "minT", [P, 4, 4 * P])
        mins = sb_in(nc, ctx, "mins", [P, 4, 4 * D])
        resets_loaded = [sem(f"resets_loaded{i}") for i in range(2)]
        rowsT_ps, minT_ready, mins_ps, mins_ready, picked_ps = sem("rowsT_ps"), sem("minT_ready"), sem("mins_ps"), sem("mins_ready"), sem("picked_ps")
        lasts_ready, added, zeroed = sem("lasts_ready"), sem("added"), sem("zeroed")
        block = ctx.enter_context(nc.Block())

        @block.sync
        def _(sp):
            def loads(s, i, m, on):
                load_idx(mem, sp, src_tiles, s, m, rowsT_ps, 2)
                wait(sp, minT_ready, 2 * (s - 1))
                sp.dma_start(resets[:, m % 2, :], mem.start_pos[:, bass.ds(8 * P * s, 8 * P)].to_broadcast([P, 8 * P])
                             ).then_inc(resets_loaded[m % 2], 16)

            pipeline(sp, BATCHES, 0, 4, loads)

        @block.gpsimd
        def _(pool):
            gather_rows(nc, mem, pool, table, rows, BATCHES, rowsT_ps, 2, rounds)

        @block.vector
        def _(dve):
            nc.vector.memset(mem.acc[:, :], 0.0).then_inc(zeroed, 1)

            def step(s, i, m, on):
                if on(0):
                    for g in range(2):
                        q, slot = 2 * s + g, m % 2 * 2 + g
                        dve.wait_ge(rowsT_ps, q + 1)
                        if g == 0:
                            dve.wait_ge(resets_loaded[m % 2], 16 * (2 * i + m // 2 + 1))
                        wait(dve, minT_ready, q)
                        wait(dve, mins_ps, q - 3)
                        start = 0.0 if isinstance(q, int) and q == 0 else minT[:, (slot - 1) % 4, 4 * P - 1:4 * P]
                        nc.vector.tensor_tensor_scan(minT[:, slot, :], resets[:, m % 2, g * 512:g * 512 + 512], mem.bank[g][:, :],
                                                     start, ALU.add, ALU.min).then_inc(minT_ready, 1)
                if on(1):
                    wait(dve, picked_ps, 2 * (s - 2))
                    mark_targets(nc, mem, mem.rel_end, lasts[:, (m - 1) % 2, :, :], s - 1).then_inc(lasts_ready, 1)
                if on(3):
                    bases = load_bases(nc, mem, mybir.EngineType.DVE, 8 * (s - 3), 8)
                    for k in range(8):
                        t = 8 * (s - 3) + k
                        dve.wait_ge(picked_ps, 2 * (s - 3) + k // 4 + 1)
                        if isinstance(s, int) and s == 3 and k == 0:
                            dve.wait_ge(zeroed, 1)
                        wait(dve, added, t)
                        window = mem.acc[:, bass.ds(bases[k], P)]
                        nc.vector.tensor_tensor(window, window, mem.bank[4 + (m - 3) % 2 * 2 + k // 4][:, k % 4 * P:(k % 4 + 1) * P],
                                                ALU.add).then_inc(added, 1)

            pipeline(dve, BATCHES, 3, 4, step)

        @block.tensor
        def _(pe):
            def step(s, i, m, on):
                for g in range(2):
                    if on(0):
                        q = 2 * s + g
                        wait(pe, minT_ready, q - 1)
                        for k in range(4):
                            slot = 8 * m + 4 * g + k
                            pe.wait_ge(mem.gathered[slot], 16 * (rounds + i + 1))
                            last = nc.tensor.transpose(mem.bank[g][:, k * P:(k + 1) * P], rows[:, slot, :], mem.ident[:, :])
                        last.then_inc(rowsT_ps, 1)
                    if on(1):
                        q, slot = 2 * (s - 1) + g, (m - 1) % 2 * 2 + g
                        pe.wait_ge(minT_ready, q + 1)
                        wait(pe, mins_ready, q - 1)
                        for k in range(4):
                            last = nc.tensor.transpose(mem.bank[2 + g][:, k * D:(k + 1) * D], minT[:, slot, k * P:(k + 1) * P], mem.ident[:, :])
                        last.then_inc(mins_ps, 1)
                    if on(2):
                        q, slot = 2 * (s - 2) + g, m % 2 * 2 + g
                        pe.wait_ge(mins_ready, q + 1)
                        pe.wait_ge(lasts_ready, s - 1)
                        wait(pe, added, 4 * (q - 3))
                        for k in range(4):
                            last = nc.tensor.matmul(mem.bank[4 + slot][:, k * P:(k + 1) * P], mins[:, slot, k * D:(k + 1) * D],
                                                    lasts[:, m % 2, 4 * g + k, :], start=True, stop=True)
                        last.then_inc(picked_ps, 1)

            pipeline(pe, BATCHES, 2, 4, step)

        @block.scalar
        def _(act):
            def step(s, i, m, on):
                for g in range(2):
                    if on(1):
                        q, slot = 2 * (s - 1) + g, (m - 1) % 2 * 2 + g
                        act.wait_ge(mins_ps, q + 1)
                        wait(act, picked_ps, q - 3)
                        nc.scalar.copy(mins[:, slot, :], mem.bank[2 + g][:, :]).then_inc(mins_ready, 1)

            pipeline(act, BATCHES, 1, 4, step)


def node_stage(nc, mem, kind, x_from=None, x_to=None, y_from=None, y_to=None, w=None, w_low=None, bias=None, w_next=None):
    norm = kind != "first_conv"
    makes_y = y_to is not None
    COMBINE = 2 if kind == "max" else 1
    STATS = COMBINE + 1
    XNEW = COMBINE + 2 if norm else COMBINE + 1
    FLIP = XNEW + 1
    YNEW = FLIP + 1
    STORE = YNEW + 1 if makes_y else XNEW + 1
    with ExitStack() as ctx:
        sem = semaphores(nc, ctx, kind + "_")
        sb = lambda n, *shape: sb_in(nc, ctx, f"{kind}_{n}", [P, *shape])
        sumsT, x_in, y_in, r, x_new, y = (sb(n, 3, CHUNK) for n in ("sumsT", "x_in", "y_in", "r", "x_new", "y"))
        xT, preT, x_newT = (sb(n, 3, CHUNK) for n in ("xT", "preT", "x_newT"))
        den_in = sb_in(nc, ctx, kind + "_den_in", [HEADS + 1, 3, CHUNK])
        inverse = sb("inverse", 3, 3 * HEADS)
        stats, mean_var = sb("stats", 3, 3, 6), sb("mean_var", 3, 3, 2)
        std, rstd, shift = sb("std", 3, 3), sb("rstd", 3, 3), sb("shift", 3, 3)
        w_sb, w_low_sb, w_next_sb, bias_sb, eps_sb = sb("w", D), sb("w_low", D), sb("w_next", D), sb("bias", D), sb("eps", 1)
        weights_loaded, eps_ready, dinv_steps = sem("weights_loaded"), sem("eps_ready"), sem("dinv_steps")
        loaded = [sem(f"loaded{i}") for i in range(3)]
        stored = [sem(f"stored{i}") for i in range(3)]
        turned_ps, pre_ready, xT_ready, proj_ps, combined = (sem(n) for n in ("turned_ps", "pre_ready", "xT_ready", "proj_ps", "combined"))
        den_ps, den_read, inverse_ready, stats_ready, var_ready = (sem(n) for n in ("den_ps", "den_read", "inverse_ready", "stats_ready", "var_ready"))
        std_ready, rstd_ready, shift_ready, x_ready = (sem(n) for n in ("std_ready", "rstd_ready", "shift_ready", "x_ready"))
        x_newT_ps, x_newT_ready, y_ps, y_ready = (sem(n) for n in ("x_newT_ps", "x_newT_ready", "y_ps", "y_ready"))
        partial, steps, pe_steps = sem("partial"), sem("steps"), sem("pe_steps")
        ps_turned = [mem.bank[i][:, 0:CHUNK] for i in range(3)]
        ps_high, ps_low, ps_newT, ps_y, ps_den = (mem.bank[i] for i in range(3, 8))
        block = ctx.enter_context(nc.Block())
        weights = [(dst, src) for dst, src in ((w_sb, w), (w_low_sb, w_low), (w_next_sb, w_next)) if src is not None]
        if bias is not None:
            weights.append((bias_sb, bias.to_broadcast([P, D])))
        n_loads = 1 + (kind == "attention") + (x_from is not None) + (y_from is not None)
        n_stores = (x_to is not None) + makes_y
        by_tile = lambda ap: ap.rearrange("p (k f) -> p k f", k=3)
        rows_of = lambda table, c: table.rearrange("(c k p) f -> c p k f", k=3, p=P)[bass.ds(c, 1), :, :, :].rearrange("o p k f -> (o p) k f")

        @block.sync
        def _(sp):
            for dst, src in weights:
                sp.dma_start(dst[:, :], src).then_inc(weights_loaded, 16)

            def step(s, i, m, on):
                if on(0):
                    wait(sp, combined, s - 2)
                    sp.sem_inc(steps, 1)
                    nodes = bass.ds(s * CHUNK, CHUNK)
                    sp.dma_start(sumsT[:, m, :], mem.acc[:, nodes]).then_inc(loaded[m], 16)
                    if kind == "attention":
                        sp.dma_start(den_in[:, m, :], mem.den[:, nodes]).then_inc(loaded[m], 16)
                    if x_from is not None:
                        sp.dma_start(by_tile(x_in[:, m, :]), rows_of(x_from, s)).then_inc(loaded[m], 16)
                    if y_from is not None:
                        sp.dma_start(by_tile(y_in[:, m, :]), rows_of(y_from, s)).then_inc(loaded[m], 16)
                if on(STORE):
                    c, slot = s - STORE, (m - STORE) % 3
                    sp.wait_ge(x_ready, c + 1)
                    if makes_y:
                        sp.wait_ge(y_ready, c + 1)
                    if x_to is not None:
                        sp.dma_start(rows_of(x_to, c), by_tile(x_new[:, slot, :])).then_inc(stored[slot], 16)
                    if makes_y:
                        sp.dma_start(rows_of(y_to, c), by_tile(y[:, slot, :])).then_inc(stored[slot], 16)

            pipeline(sp, CHUNKS, STORE, 3, step, peel=STORE + 3)
            for n in range(3):
                sp.wait_ge(stored[n], 16 * n_stores * (CHUNKS // 3))

        @block.vector
        def _(dve):
            nc.vector.memset(eps_sb[:, :], EPS).then_inc(eps_ready, 1)
            if weights:
                dve.wait_ge(weights_loaded, 16 * len(weights))
            if kind == "max":
                nc.vector.tensor_scalar(mem.mask[:, :], mem.count[:, :], 1.0, None, ALU.min).then_inc(dinv_steps, 1)
                nc.vector.tensor_scalar(mem.dinv[:, :], mem.count[:, :], 1.0, None, ALU.add).then_inc(dinv_steps, 1)
                dve.wait_ge(dinv_steps, 3)
                nc.vector.reciprocal(mem.dinv[:, :], mem.dinv[:, :]).then_inc(dinv_steps, 1)
                dve.wait_ge(dinv_steps, 4)
            per_node = lambda values, c: values[:, bass.ds(3 * c, 3)].unsqueeze(2).to_broadcast([P, 3, D])

            def step(s, i, m, on):
                if on(YNEW) and makes_y:
                    c, slot = s - YNEW, (m - YNEW) % 3
                    dve.wait_ge(y_ps, c + 1)
                    wait(dve, stored[slot], 16 * n_stores * (i + (m - YNEW) // 3))
                    nc.vector.tensor_tensor(by_tile(y[:, slot, :]), by_tile(ps_y[:, 0:CHUNK]), per_node(mem.dinv, c), ALU.mult).then_inc(y_ready, 1)
                if on(XNEW) and norm:
                    c, slot = s - XNEW, (m - XNEW) % 3
                    dve.wait_ge(std_ready, c + 1)
                    wait(dve, x_ready, c - 2)
                    nc.vector.reciprocal(rstd[:, slot, :], std[:, slot, :]).then_inc(rstd_ready, 1)
                    dve.wait_ge(rstd_ready, c + 1)
                    nc.vector.scalar_tensor_tensor(shift[:, slot, :], mean_var[:, slot, :, 0], -1.0, rstd[:, slot, :],
                                                   ALU.mult, ALU.mult).then_inc(shift_ready, 1)
                if on(STATS) and norm:
                    c, slot = s - STATS, (m - STATS) % 3
                    dve.wait_ge(combined, c + 1)
                    for k in range(3):
                        last = nc.vector.bn_stats(stats[:, slot, k, :], r[:, slot, k * D:(k + 1) * D])
                    last.then_inc(stats_ready, 1)
                if kind == "max":
                    if on(COMBINE):
                        c, slot = s - COMBINE, (m - COMBINE) % 3
                        dve.wait_ge(proj_ps, c + 1)
                        wait(dve, x_ready, c - 2)
                        nc.vector.tensor_tensor(by_tile(r[:, slot, :]), by_tile(ps_low[:, 0:CHUNK]), per_node(mem.mask, c), ALU.mult).then_inc(partial, 1)
                    if on(1):
                        d, d_slot = s - 1, (m - 1) % 3
                        dve.wait_ge(turned_ps, d + 1)
                        wait(dve, proj_ps, d - 2)
                        nc.vector.tensor_tensor(preT[:, d_slot, :], ps_turned[d_slot], sumsT[:, d_slot, :], ALU.subtract).then_inc(pre_ready, 1)
                    if on(COMBINE):
                        dve.wait_ge(partial, 3 * c + 1)
                        nc.vector.tensor_tensor(r[:, slot, :], r[:, slot, :], ps_high[:, 0:CHUNK], ALU.add).then_inc(partial, 1)
                elif on(COMBINE):
                    c, slot = s - COMBINE, (m - COMBINE) % 3
                    if kind == "attention":
                        dve.wait_ge(den_ps, c + 1)
                        dve.sem_inc(steps, 1)
                        heads = ps_den[:, 0:3 * 16].rearrange("p (k h) -> p k h", k=3)
                        nc.vector.tensor_copy(mem.count[:, bass.ds(3 * c, 3)], heads[:, :, HEADS])
                        nc.vector.tensor_scalar(inverse[:, slot, :].rearrange("p (k h) -> p k h", k=3), heads[:, :, 0:HEADS],
                                                TINY, None, ALU.max).then_inc(den_read, 1)
                        dve.wait_ge(den_read, c + 1)
                        nc.vector.reciprocal(inverse[:, slot, :], inverse[:, slot, :]).then_inc(inverse_ready, 1)
                    dve.wait_ge(turned_ps, c + 1)
                    wait(dve, x_ready, c - 2)
                    if kind == "attention":
                        dve.wait_ge(inverse_ready, c + 1)
                        for k in range(3):
                            tile = slice(k * D, (k + 1) * D)
                            last = nc.vector.tensor_tensor(
                                r[:, slot, tile].rearrange("p (d h) -> p d h", h=HEADS),
                                ps_turned[slot][:, tile].rearrange("p (d h) -> p d h", h=HEADS),
                                inverse[:, slot, k * HEADS:(k + 1) * HEADS].unsqueeze(1).to_broadcast([P, DH, HEADS]), ALU.mult)
                        last.then_inc(partial, 1)
                        dve.wait_ge(partial, c + 1)
                        nc.vector.tensor_tensor(r[:, slot, :], r[:, slot, :], x_in[:, slot, :], ALU.add).then_inc(combined, 1)
                    if kind == "weighted":
                        nc.vector.tensor_tensor(r[:, slot, :], ps_turned[slot], x_in[:, slot, :], ALU.add).then_inc(combined, 1)
                    if y_from is not None:
                        nc.vector.tensor_tensor(r[:, slot, :], ps_turned[slot], y_in[:, slot, :], ALU.add).then_inc(partial, 1)
                        dve.wait_ge(partial, (3 if norm else 2) * c + 1)
                        nc.vector.tensor_tensor(by_tile(r[:, slot, :]), by_tile(r[:, slot, :]), per_node(mem.dinv, c), ALU.mult).then_inc(partial, 1)
                if on(STATS) and norm:
                    d, d_slot = s - STATS, (m - STATS) % 3
                    dve.wait_ge(stats_ready, d + 1)
                    wait(dve, shift_ready, d - 2)
                    dve.sem_inc(steps, 1)
                    for k in range(3):
                        last = nc.vector.bn_aggr(mean_var[:, d_slot, k, :], stats[:, d_slot, k, :])
                    last.then_inc(var_ready, 1)
                if on(COMBINE) and bias is not None:
                    per_chunk = 3 if norm else 2
                    dve.wait_ge(partial, per_chunk * c + 2)
                    nc.vector.tensor_tensor(by_tile(r[:, slot, :]), by_tile(r[:, slot, :]), bias_sb[:, :].unsqueeze(1).to_broadcast([P, 3, D]),
                                            ALU.add).then_inc(partial if norm else combined, 1)
                    if norm:
                        dve.wait_ge(partial, 3 * (c + 1))
                        if kind == "max":
                            nc.vector.scalar_tensor_tensor(r[:, slot, :], r[:, slot, :], 0.0, x_in[:, slot, :], ALU.max, ALU.add).then_inc(combined, 1)
                        else:
                            nc.vector.tensor_tensor(r[:, slot, :], r[:, slot, :], x_in[:, slot, :], ALU.add).then_inc(combined, 1)

            pipeline(dve, CHUNKS, STORE, 3, step, peel=STORE + 3)

        @block.tensor
        def _(pe):
            if weights:
                pe.wait_ge(weights_loaded, 16 * len(weights))

            def step(s, i, m, on):
                if on(1):
                    c, slot = s - 1, (m - 1) % 3
                    pe.wait_ge(loaded[slot], 16 * n_loads * (i + (m - 1) // 3 + 1))
                    wait(pe, xT_ready if kind == "max" else combined, c - 2)
                    source = x_in if kind == "max" else sumsT
                    for k in range(3):
                        last = nc.tensor.transpose(ps_turned[slot][:, k * P:(k + 1) * P], source[:, slot, k * P:(k + 1) * P], mem.ident[:, :])
                    last.then_inc(turned_ps, 1)
                    if kind == "attention":
                        wait(pe, den_read, c)
                        pe.sem_inc(pe_steps, 1)
                        for k in range(3):
                            last = nc.tensor.transpose(ps_den[:, 16 * k:16 * k + HEADS + 1], den_in[:, slot, k * P:(k + 1) * P],
                                                       mem.ident[0:HEADS + 1, 0:HEADS + 1])
                        last.then_inc(den_ps, 1)
                if on(2) and kind == "max":
                    c, slot = s - 2, (m - 2) % 3
                    pe.wait_ge(pre_ready, c + 1)
                    pe.wait_ge(xT_ready, c + 1)
                    wait(pe, combined, c)
                    for k in range(3):
                        tile = slice(k * P, (k + 1) * P)
                        nc.tensor.matmul(ps_high[:, tile], xT[:, slot, tile], w_sb[:, :], start=True, stop=True)
                        last = nc.tensor.matmul(ps_low[:, tile], preT[:, slot, tile], w_low_sb[:, :], start=True, stop=True)
                    last.then_inc(proj_ps, 1)
                if on(YNEW) and makes_y:
                    c, slot = s - YNEW, (m - YNEW) % 3
                    pe.wait_ge(x_newT_ready, c + 1)
                    wait(pe, y_ready, c)
                    for k in range(3):
                        last = nc.tensor.matmul(ps_y[:, k * D:(k + 1) * D], x_newT[:, slot, k * P:(k + 1) * P], w_next_sb[:, :],
                                                start=True, stop=True)
                    last.then_inc(y_ps, 1)
                if on(FLIP) and makes_y:
                    c, slot = s - FLIP, (m - FLIP) % 3
                    pe.wait_ge(x_ready, c + 1)
                    wait(pe, x_newT_ready, c)
                    for k in range(3):
                        last = nc.tensor.transpose(ps_newT[:, k * P:(k + 1) * P], x_new[:, slot, k * D:(k + 1) * D], mem.ident[:, :])
                    last.then_inc(x_newT_ps, 1)

            pipeline(pe, CHUNKS, STORE, 3, step, peel=STORE + 3)

        @block.scalar
        def _(act):
            act.wait_ge(eps_ready, 1)
            if kind == "max":
                act.wait_ge(dinv_steps, 2)
                nc.scalar.activation(mem.dinv[:, :], mem.dinv[:, :], ACT.Sqrt).then_inc(dinv_steps, 1)

            def step(s, i, m, on):
                if on(FLIP) and makes_y:
                    c, slot = s - FLIP, (m - FLIP) % 3
                    act.wait_ge(x_newT_ps, c + 1)
                    wait(act, y_ps, c - 2)
                    nc.scalar.copy(x_newT[:, slot, :], ps_newT[:, 0:CHUNK]).then_inc(x_newT_ready, 1)
                if on(XNEW):
                    c, slot = s - XNEW, (m - XNEW) % 3
                    act.wait_ge(shift_ready if norm else combined, c + 1)
                    if makes_y:
                        wait(act, x_newT_ps, c - 2)
                    if x_to is not None:
                        wait(act, stored[slot], 16 * n_stores * (i + (m - XNEW) // 3))
                    if norm:
                        for k in range(3):
                            last = nc.scalar.activation(x_new[:, slot, k * D:(k + 1) * D], r[:, slot, k * D:(k + 1) * D], ACT.Identity,
                                                        bias=shift[:, slot, k:k + 1], scale=rstd[:, slot, k:k + 1])
                        last.then_inc(x_ready, 1)
                    else:
                        nc.scalar.activation(x_new[:, slot, :], r[:, slot, :], ACT.Relu).then_inc(x_ready, 1)
                if on(1) and kind == "max":
                    c, slot = s - 1, (m - 1) % 3
                    act.wait_ge(pre_ready, c + 1)
                    wait(act, proj_ps, c - 2)
                    nc.scalar.copy(xT[:, slot, :], ps_turned[slot]).then_inc(xT_ready, 1)
                if on(STATS) and norm:
                    c, slot = s - STATS, (m - STATS) % 3
                    act.wait_ge(var_ready, c + 1)
                    wait(act, rstd_ready, c - 2)
                    nc.scalar.activation(std[:, slot, :], mean_var[:, slot, :, 1], ACT.Sqrt, bias=eps_sb[:, 0:1]).then_inc(std_ready, 1)

            pipeline(act, CHUNKS, STORE, 3, step, peel=STORE + 3)


def build(nc, t, out):
    with ExitStack() as ctx:
        mem = Memory(nc, ctx)
        rows = mem.rows_dram
        prepare(nc, mem, t["dst_tiles"], t["next_tiles"], t["dst_flat"], t["prev_flat"], t["next_flat"], t["first_dst"], t["batch_last"])
        project_inputs(nc, mem, t["xT"], t["W_in"], t["b_in"], t["Wq"], t["bq"], t["Wk"], t["bk"], t["Wv"], t["bv"])
        attention(nc, mem, t["src_tiles"])
        node_stage(nc, mem, "attention", x_from=t["x_rows"], x_to=rows[0])
        sum_layer(nc, mem, "w_", rows[0], t["src_tiles"], t["attr64"], t["attr8"])
        node_stage(nc, mem, "weighted", x_from=rows[0], x_to=rows[1])
        min_layer(nc, mem, rows[1], t["src_tiles"])
        node_stage(nc, mem, "max", x_from=rows[1], x_to=rows[2], y_to=rows[3],
                   w=t["W_max"][0:D, :], w_low=t["W_max"][D:2 * D, :], bias=t["b_max"], w_next=t["W1"])
        sum_layer(nc, mem, "c1_", rows[3], t["src_tiles"])
        node_stage(nc, mem, "first_conv", y_from=rows[3], y_to=rows[4], bias=t["b1"], w_next=t["W2"])
        sum_layer(nc, mem, "c2_", rows[4], t["src_tiles"])
        node_stage(nc, mem, "second_conv", x_from=rows[2], y_from=rows[4], x_to=out, bias=t["b2"])




def kernel(**inputs):
    import numpy as np
    import concourse.bacc as bacc
    from concourse.bass_utils import run_bass_kernel_spmd as run

    edges = TILES * P
    nc = bacc.Bacc("TRN2", target_bir_lowering=False, num_devices=1)
    x, src, dst = (np.asarray(inputs[name]) for name in ("x", "src", "dst"))

    def padded(a, value):
        return np.concatenate([a, np.full((edges - len(a),) + a.shape[1:], value, a.dtype)])

    def tiles(a):
        return np.ascontiguousarray(a.reshape((TILES, P) + a.shape[1:]).swapaxes(0, 1))

    dst_flat = padded(dst, N)
    prev_flat = np.concatenate([np.full(1, -1, dst.dtype), dst_flat[:-1]])
    next_flat = np.concatenate([dst_flat[1:], np.full(1, -1, dst.dtype)])
    xT = np.zeros((P, NP), x.dtype)
    xT[:, :N] = x.T
    x_rows = np.ascontiguousarray(xT.T)
    row = lambda name: np.asarray(inputs[name]).reshape(1, D)
    arrays = {
        "xT": xT,
        "x_rows": x_rows,
        "src_tiles": tiles(padded(src, 0)),
        "dst_tiles": tiles(dst_flat),
        "next_tiles": tiles(next_flat),
        "dst_flat": dst_flat.reshape(P, TILES),
        "prev_flat": prev_flat.reshape(P, TILES),
        "next_flat": next_flat.reshape(P, TILES),
        "first_dst": np.ascontiguousarray(dst_flat[::P]).reshape(1, TILES),
        "batch_last": np.ascontiguousarray(dst_flat[8 * P - 1::8 * P]).reshape(1, BATCHES),
        "attr64": tiles(padded(np.asarray(inputs["edge_attr_64"]), 0)),
        "attr8": tiles(padded(np.asarray(inputs["edge_attr_8"]), 0)),
        "W_in": np.asarray(inputs["L0_gnn_W_in"]), "b_in": row("L0_gnn_b_in"),
        "Wq": np.asarray(inputs["L0_gnn_Wq"]), "bq": row("L0_gnn_bq"),
        "Wk": np.asarray(inputs["L0_gnn_Wk"]), "bk": row("L0_gnn_bk"),
        "Wv": np.asarray(inputs["L0_gnn_Wv"]), "bv": row("L0_gnn_bv"),
        "W_max": np.asarray(inputs["L2_gnn_W"]), "b_max": row("L2_gnn_b"),
        "W1": np.asarray(inputs["L3_gnn_W1"]), "b1": row("L3_gnn_b1"),
        "W2": np.asarray(inputs["L3_gnn_W2"]), "b2": row("L3_gnn_b2"),
    }
    t = {name: nc.dram_tensor("in_" + name, a.shape, mybir.dt.from_np(a.dtype), kind="ExternalInput").ap()
         for name, a in arrays.items()}
    out = nc.dram_tensor("out", (NP, D), FP, kind="ExternalOutput").ap()
    build(nc, t, out)
    r = run(nc, [{"in_" + name: a for name, a in arrays.items()}], core_ids=[0])
    return r.results[0]["out"][:N]
```

```python
import concourse.bass as bass
from concourse import mybir
from contextlib import ExitStack


FP = mybir.dt.float32
BF = mybir.dt.bfloat16
I32 = mybir.dt.int32
ALU = mybir.AluOpType
ACT = mybir.ActivationFunctionType
AX = mybir.AxisListType

N = 12500
E = 212500
D = 128
HEADS = 8
DH = D // HEADS
P = 128
RING = 32
TILES = -(-E // (P * RING)) * RING
BATCHES = TILES // 8
CHUNK = 3 * P
CHUNKS = -(-(N + P) // CHUNK)
NP = CHUNKS * CHUNK
PAIR = 2 * P
PAIRS = -(-N // PAIR)
PAIR_START = 6
PAIR_DONE = 18
CHECKED = -(-(BATCHES - PAIR_DONE) // 4)
BIG = 3.0e38
TINY = 1e-30
EPS = 1e-5


def wait(engine, sem, value):
    if not isinstance(value, int) or value > 0:
        engine.wait_ge(sem, value)


def pipeline(engine, count, lag, unroll, emit, peel=0):
    head = -(-max(lag, unroll, peel) // unroll)
    full = count // unroll

    def peeled(first, last):
        for s in range(first, last):
            emit(s, s // unroll, s % unroll, lambda l, s=s: 0 <= s - l < count)

    peeled(0, head * unroll)
    with engine.Fori(head, full) as i:
        for m in range(unroll):
            emit(i * unroll + m, i, m, lambda l: True)
    peeled(full * unroll, count + lag)


class Memory:

    def __init__(self, nc, ctx):
        self.nc, self.ctx = nc, ctx
        self.acc = self.sb("acc", [P, NP])
        self.den = self.sb("den", [HEADS + 1, NP])
        self.rel = self.sb("rel", [P, TILES], BF)
        self.rel_end = self.sb("rel_end", [P, TILES], BF)
        self.base = self.sb("base", [1, TILES], I32)
        self.tight = self.sb("tight", [1, BATCHES], I32)
        self.regular = self.sb("regular", [1, 1], I32)
        self.iota = self.sb("iota", [P, P])
        self.ident = self.sb("ident", [P, P])
        self.ones = self.sb("ones", [P, P])
        self.count, self.mask, self.dinv = (self.sb(name, [P, NP // P]) for name in ("count", "mask", "dinv"))
        self.expand = self.sb("expand", [HEADS, P])
        self.idx = self.sb("idx", [P, RING], I32)
        self.bank = [ctx.enter_context(nc.psum_tensor(f"bank{i}", [P, 512], FP)) for i in range(8)]
        self.gathered = [self.sem(f"gathered{i}") for i in range(RING)]
        self.idx_loaded = [self.sem(f"idx_loaded{i}") for i in range(4)]
        self.q_dram = nc.dram_tensor("q_rows", [NP, D], FP, kind="Internal").ap()
        self.kv_dram = nc.dram_tensor("kv_rows", [NP, 2 * D], FP, kind="Internal").ap()
        self.rows_dram = [nc.dram_tensor(f"rows{i}", [PAIRS * PAIR if i else NP, D], FP, kind="Internal").ap() for i in range(5)]
        self.start_neg = nc.dram_tensor("start_neg", [1, TILES * P], BF, kind="Internal").ap()
        self.end_neg = nc.dram_tensor("end_neg", [1, TILES * P], BF, kind="Internal").ap()
        self.start_pos = nc.dram_tensor("start_pos", [1, TILES * P], BF, kind="Internal").ap()
        self.gather_steps = self.sem("gather_steps")
        self.gather_rounds = 0

    def sb(self, name, shape, dt=FP):
        return self.ctx.enter_context(self.nc.sbuf_tensor(name, shape, dt))

    def sem(self, name):
        return self.ctx.enter_context(self.nc.semaphore(name))


def semaphores(nc, ctx, prefix):
    made = []

    def release():
        nc.clear_and_free_semaphores(made)
        nc.all_engine_barrier(sem_only=True)

    def sem(name):
        made.append(nc.alloc_semaphore(prefix + name))
        return made[-1]

    ctx.callback(release)
    return sem


def sb_in(nc, ctx, name, shape, dt=FP):
    return ctx.enter_context(nc.sbuf_tensor(name, shape, dt))


def load_flag(nc, flags, engine_type, at):
    _, values = nc.values_load_multi_w_load_instructions(
        flags[0:1, bass.ds(at, 1)], engines=[engine_type], min_val=0, max_val=1,
        skip_runtime_bounds_check_because="the result of a comparison")
    return values[0]


def load_bases(nc, mem, engine_type, first, count):
    _, values = nc.values_load_multi_w_load_instructions(
        mem.base[0:1, bass.ds(first, count)], engines=[engine_type], min_val=0, max_val=N,
        skip_runtime_bounds_check_because="dst lies in 0..N-1 and the padding edges have N")
    return values


def prepare(nc, mem, dst_tiles, next_tiles, dst_flat, prev_flat, next_flat, first_dst, batch_last):
    with ExitStack() as ctx:
        sem = semaphores(nc, ctx, "p_")
        tmp = sb_in(nc, ctx, "prep_i", [P, 5, TILES], I32)
        f = sb_in(nc, ctx, "prep_f", [P, 4, TILES])
        pen = sb_in(nc, ctx, "prep_pen", [P, 3, TILES], BF)
        first = sb_in(nc, ctx, "prep_first", [1, TILES], I32)
        last = sb_in(nc, ctx, "prep_last", [1, BATCHES], I32)
        span = sb_in(nc, ctx, "prep_span", [1, BATCHES])
        tight = sb_in(nc, ctx, "prep_tight", [1, BATCHES])
        base = sb_in(nc, ctx, "prep_base", [1, TILES])
        pair_end = sb_in(nc, ctx, "prep_pair_end", [1, CHECKED])
        pair_ok = sb_in(nc, ctx, "prep_pair_ok", [1, CHECKED])
        loaded, rows_loaded, stored = sem("loaded"), sem("rows_loaded"), sem("stored")
        pair_ends_ready = sem("pair_ends_ready")
        ones_ready = sem("ones_ready")
        base_ready, bc_ready, step, pens_ready = sem("base_ready"), sem("bc_ready"), sem("step"), sem("pens_ready")
        block = ctx.enter_context(nc.Block())
        quarter = TILES // 4

        @block.sync
        def _(sp):
            sp.dma_start(first[:, :], first_dst).then_inc(rows_loaded, 16)
            sp.dma_start(last[:, :], batch_last).then_inc(rows_loaded, 16)
            for i, src in enumerate((dst_tiles, next_tiles, dst_flat, prev_flat, next_flat)):
                sp.dma_start(tmp[:, i, :], src).then_inc(loaded, 16)
            sp.wait_ge(pens_ready, 3)
            for i, dst in enumerate((mem.start_neg, mem.end_neg, mem.start_pos)):
                sp.dma_start(dst.rearrange("o (p c) -> (o p) c", p=P), pen[:, i, :]).then_inc(stored, 16)
            sp.wait_ge(stored, 48)

        @block.gpsimd
        def _(pool):
            nc.gpsimd.memset(mem.ones[:, :], 1.0).then_inc(ones_ready, 1)
            nc.gpsimd.iota(pair_end[:, :], [[PAIR, CHECKED]], base=PAIR, channel_multiplier=0,
                           allow_small_or_imprecise_dtypes=True).then_inc(pair_ends_ready, 1)
            nc.gpsimd.iota(mem.iota[:, :], [[1, P]], base=0, channel_multiplier=0,
                           allow_small_or_imprecise_dtypes=True)
            pool.wait_ge(ones_ready, 1)
            nc.gpsimd.affine_select(mem.ident[:, :], mem.ones[:, :], [[-1, P]], ALU.is_equal, 0.0,
                                    base=0, channel_multiplier=1)
            nc.gpsimd.affine_select(mem.expand[:, :].rearrange("h (d g) -> h d g", g=HEADS),
                                    mem.ones[0:HEADS, :].rearrange("h (d g) -> h d g", g=HEADS),
                                    [[0, DH], [-1, HEADS]], ALU.is_equal, 0.0,
                                    base=0, channel_multiplier=1)
            nc.gpsimd.memset(mem.den[:, :], 0.0)

        @block.tensor
        def _(pe):
            pe.wait_ge(ones_ready, 1)
            pe.wait_ge(base_ready, 1)
            for c in range(4):
                nc.tensor.matmul(mem.bank[c][:, 0:quarter], mem.ones[0:1, :], base[:, c * quarter:(c + 1) * quarter],
                                 start=True, stop=True).then_inc(bc_ready, 1)

        @block.vector
        def _(dve):
            by_batch = lambda row: row.rearrange("o (b t) -> o b t", t=8)
            firsts = by_batch(first[:, :])
            batch_first = firsts[:, :, 0:1]
            dve.wait_ge(rows_loaded, 32)
            nc.vector.tensor_tensor(span[:, :], last[:, :], batch_first.rearrange("o b t -> o (b t)"), ALU.subtract).then_inc(step, 1)
            nc.vector.tensor_tensor(by_batch(base[:, :]), batch_first.to_broadcast([1, BATCHES, 8]), firsts, ALU.subtract).then_inc(step, 1)
            dve.wait_ge(step, 2)
            nc.vector.tensor_scalar(tight[:, :], span[:, :], float(P), None, ALU.is_lt).then_inc(step, 1)
            dve.wait_ge(step, 3)
            nc.vector.tensor_tensor(by_batch(base[:, :]), by_batch(base[:, :]), tight[:, :].unsqueeze(2).to_broadcast([1, BATCHES, 8]),
                                    ALU.mult).then_inc(step, 1)
            nc.vector.tensor_copy(mem.tight[:, :], tight[:, :])
            dve.wait_ge(step, 4)
            nc.vector.tensor_tensor(base[:, :], base[:, :], first[:, :], ALU.add).then_inc(base_ready, 1)
            dve.wait_ge(base_ready, 1)
            nc.vector.tensor_copy(mem.base[:, :], base[:, :])
            dve.wait_ge(pair_ends_ready, 1)
            nc.vector.tensor_tensor(pair_ok[:, :], first[:, 8 * PAIR_DONE::32], pair_end[:, :], ALU.is_ge).then_inc(step, 1)
            dve.wait_ge(step, 5)
            nc.vector.tensor_reduce(mem.regular[:, :], pair_ok[:, :], AX.X, ALU.min)
            dve.wait_ge(loaded, 80)
            nc.vector.tensor_tensor(f[:, 2, :], tmp[:, 2, :], tmp[:, 3, :], ALU.not_equal).then_inc(step, 1)
            nc.vector.tensor_tensor(f[:, 3, :], tmp[:, 2, :], tmp[:, 4, :], ALU.not_equal).then_inc(step, 1)
            dve.wait_ge(step, 7)
            nc.vector.tensor_scalar(pen[:, 0, :], f[:, 2, :], -BIG, None, ALU.mult).then_inc(pens_ready, 1)
            nc.vector.tensor_scalar(pen[:, 1, :], f[:, 3, :], -BIG, None, ALU.mult).then_inc(pens_ready, 1)
            nc.vector.tensor_scalar(pen[:, 2, :], f[:, 2, :], BIG, None, ALU.mult).then_inc(pens_ready, 1)
            nc.vector.tensor_tensor(f[:, 1, :], tmp[:, 0, :], tmp[:, 1, :], ALU.not_equal).then_inc(step, 1)
            dve.wait_ge(bc_ready, 4)
            for c in range(4):
                cols = slice(c * quarter, (c + 1) * quarter)
                nc.vector.tensor_tensor(f[:, 0, cols], tmp[:, 0, cols], mem.bank[c][:, 0:quarter],
                                        ALU.subtract).then_inc(step, 1)
            dve.wait_ge(step, 12)
            nc.vector.tensor_copy(mem.rel[:, :], f[:, 0, :])
            dve.wait_ge(pens_ready, 3)
            nc.vector.scalar_tensor_tensor(f[:, 2, :], f[:, 0, :], 1.0, f[:, 1, :], ALU.add, ALU.mult).then_inc(step, 1)
            dve.wait_ge(step, 13)
            nc.vector.tensor_scalar(mem.rel_end[:, :], f[:, 2, :], -1.0, None, ALU.add)
            nc.vector.memset(mem.acc[:, :], 0.0)


def project_inputs(nc, mem, xT, W_in, b_in, Wq, bq, Wk, bk, Wv, bv):
    with ExitStack() as ctx:
        sem = semaphores(nc, ctx, "d_")
        w_in = sb_in(nc, ctx, "w_in", [P, D])
        w_inT = sb_in(nc, ctx, "w_inT", [P, D])
        w_qkv = sb_in(nc, ctx, "w_qkv", [P, 3 * D])
        w_all = sb_in(nc, ctx, "w_all", [P, 3 * D])
        bias_in = sb_in(nc, ctx, "bias_in", [P, 1])
        bias_in_wide = sb_in(nc, ctx, "bias_in_wide", [P, P])
        bias_qkv = sb_in(nc, ctx, "bias_qkv", [P, 3 * D])
        x_in = sb_in(nc, ctx, "x_in", [P, 3, CHUNK])
        qkv = sb_in(nc, ctx, "qkv", [P, 3, 3, 3 * D])
        w_loaded, scaled, wide_ready = sem("w_loaded"), sem("scaled"), sem("wide_ready")
        w_inT_ps, w_inT_ready, w_all_ps, w_all_ready = sem("w_inT_ps"), sem("w_inT_ready"), sem("w_all_ps"), sem("w_all_ready")
        x_loaded = [sem(f"x_loaded{i}") for i in range(3)]
        stored = [sem(f"stored{i}") for i in range(3)]
        qkv_ps_ready, qkv_ready = sem("qkv_ps_ready"), sem("qkv_ready")
        block = ctx.enter_context(nc.Block())
        q_view = mem.q_dram.rearrange("(c k p) f -> c p k f", k=3, p=P)
        kv_view = mem.kv_dram.rearrange("(c k p) f -> c p k f", k=3, p=P)

        @block.sync
        def _(sp):
            sp.dma_start(w_in[:, :], W_in).then_inc(w_loaded, 16)
            for i, (w, b) in enumerate(((Wq, bq), (Wk, bk), (Wv, bv))):
                sp.dma_start(w_qkv[:, i * D:(i + 1) * D], w).then_inc(w_loaded, 16)
                sp.dma_start(bias_qkv[:, i * D:(i + 1) * D], b.to_broadcast([P, D])).then_inc(w_loaded, 16)
            sp.dma_start(bias_in[:, :], b_in.rearrange("o f -> f o")).then_inc(w_loaded, 16)

            def load_and_store(s, i, m, on):
                if on(0):
                    wait(sp, qkv_ps_ready, (s - 2) * 3)
                    sp.dma_start(x_in[:, m, :], xT[:, bass.ds(s * CHUNK, CHUNK)]).then_inc(x_loaded[m], 16)
                if on(2):
                    c, slot = s - 2, (m - 2) % 3
                    sp.wait_ge(qkv_ready, (c + 1) * 3)
                    sp.dma_start(q_view[bass.ds(c, 1), :, :, :].rearrange("o p k f -> (o p) k f"),
                                 qkv[:, slot, :, 0:D]).then_inc(stored[slot], 16)
                    sp.dma_start(kv_view[bass.ds(c, 1), :, :, :].rearrange("o p k f -> (o p) k f"),
                                 qkv[:, slot, :, D:3 * D]).then_inc(stored[slot], 16)

            pipeline(sp, CHUNKS, 2, 3, load_and_store)
            for i in range(3):
                sp.wait_ge(stored[i], 32 * (CHUNKS // 3))

        @block.tensor
        def _(pe):
            pe.wait_ge(w_loaded, 128)
            nc.tensor.transpose(mem.bank[0][:, 0:D], w_in[:, :], mem.ident[:, :]).then_inc(w_inT_ps, 1)
            pe.wait_ge(scaled, 2)
            pe.wait_ge(wide_ready, 1)
            pe.wait_ge(w_inT_ready, 1)
            nc.tensor.matmul(mem.bank[1][:, 0:3 * D], w_inT[:, :], w_qkv[:, :], start=True, stop=True)
            nc.tensor.matmul(mem.bank[2][:, 0:3 * D], bias_in_wide[:, :], w_qkv[:, :], start=True, stop=True).then_inc(w_all_ps, 1)
            pe.wait_ge(w_all_ready, 2)

            def products(s, i, m, on):
                pe.wait_ge(x_loaded[m], 16 * (i + 1))
                for k in range(3):
                    wait(pe, qkv_ready, s * 3 + k - 2)
                    nc.tensor.matmul(mem.bank[1 + k][:, 0:3 * D], x_in[:, m, k * P:(k + 1) * P], w_all[:, :],
                                     start=True, stop=True).then_inc(qkv_ps_ready, 1)

            pipeline(pe, CHUNKS, 0, 3, products)

        @block.vector
        def _(dve):
            dve.wait_ge(w_loaded, 128)
            nc.vector.tensor_scalar(w_qkv[:, 0:D], w_qkv[:, 0:D], DH ** -0.5, None, ALU.mult).then_inc(scaled, 1)
            nc.vector.tensor_scalar(bias_qkv[:, 0:D], bias_qkv[:, 0:D], DH ** -0.5, None, ALU.mult).then_inc(scaled, 1)
            nc.vector.tensor_scalar(bias_in_wide[:, :], mem.ones[:, :], bias_in[:, 0:1], None, ALU.mult).then_inc(wide_ready, 1)
            dve.wait_ge(w_inT_ps, 1)
            nc.vector.tensor_copy(w_inT[:, :], mem.bank[0][:, 0:D]).then_inc(w_inT_ready, 1)
            dve.wait_ge(scaled, 2)
            dve.wait_ge(w_all_ps, 1)
            nc.vector.tensor_copy(w_all[:, :], mem.bank[1][:, 0:3 * D]).then_inc(w_all_ready, 1)
            nc.vector.tensor_tensor(bias_qkv[:, :], bias_qkv[:, :], mem.bank[2][:, 0:3 * D], ALU.add).then_inc(w_all_ready, 1)
            dve.wait_ge(w_all_ready, 2)

            def add_bias(s, i, m, on):
                wait(dve, stored[m], 32 * i)
                for k in range(3):
                    dve.wait_ge(qkv_ps_ready, s * 3 + k + 1)
                    nc.vector.tensor_tensor(qkv[:, m, k, :], mem.bank[1 + k][:, 0:3 * D], bias_qkv[:, :],
                                            ALU.add).then_inc(qkv_ready, 1)

            pipeline(dve, CHUNKS, 0, 3, add_bias)


def mark_targets(nc, mem, rel, out, batch):
    targets = rel[:, bass.ds(8 * batch, 8)].unsqueeze(2).to_broadcast([P, 8, P])
    nodes = mem.iota[:, :].unsqueeze(1).to_broadcast([P, 8, P])
    return nc.vector.tensor_tensor(out, nodes, targets, ALU.is_equal)


def gather_rows(nc, mem, pool, table, ring, steps, released, released_per_step, rounds):

    def gather(s, i, m, on):
        pool.wait_ge(mem.idx_loaded[m], 16 * (rounds + i + 1))
        wait(pool, released, released_per_step * (s - 3))
        pool.sem_inc(mem.gather_steps, 1)
        for k in range(8):
            slot = 8 * m + k
            pool.indirect_dma_start(ring[:, slot, :], None, table,
                                    bass.IndirectOffsetOnAxis(ap=mem.idx[:, slot:slot + 1], axis=0)
                                    ).then_inc(mem.gathered[slot], 16)

    pipeline(pool, steps, 0, 4, gather)


def load_idx(mem, sp, src_tiles, s, m, used, used_per_step):
    wait(sp, used, used_per_step * (s - 3))
    sp.dma_start(mem.idx[:, 8 * m:8 * m + 8], src_tiles[:, bass.ds(8 * s, 8)]).then_inc(mem.idx_loaded[m], 16)


def attention(nc, mem, src_tiles):
    rounds = mem.gather_rounds
    mem.gather_rounds += TILES // RING
    wide = D + HEADS + 1
    with ExitStack() as ctx:
        sem = semaphores(nc, ctx, "a_")
        kv = sb_in(nc, ctx, "kv", [P, RING, 2 * D])
        onehot = sb_in(nc, ctx, "onehot", [P, RING, P])
        onehotT = sb_in(nc, ctx, "onehotT", [P, 2, 4 * P])
        q_win = sb_in(nc, ctx, "q_win", [P, 2, 8, D])
        prod = sb_in(nc, ctx, "prod", [P, 2, 4 * D])
        pv = sb_in(nc, ctx, "pv", [P, 2, 8, wide])
        score = sb_in(nc, ctx, "score", [P, 2, 8 * HEADS])
        below = sb_in(nc, ctx, "below", [P, 8 * HEADS])
        total = sb_in(nc, ctx, "total", [P, wide])
        scan = sb_in(nc, ctx, "scan", [HEADS, 8 * P])
        resets = sb_in(nc, ctx, "resets", [HEADS, 2, 2, 8 * P], BF)
        carry = sb_in(nc, ctx, "carry", [HEADS, 2])
        gap = sb_in(nc, ctx, "gap", [HEADS, 1])
        alpha = sb_in(nc, ctx, "alpha", [HEADS, 1])
        ps_onehotT, ps_q, ps_score, ps_ref, ps_total, ps_win = mem.bank[0:2], mem.bank[2:4], *mem.bank[4:8]
        q_loaded = [sem(f"q_loaded{i}") for i in range(2)]
        resets_loaded = [sem(f"resets_loaded{i}") for i in range(2)]
        windows_ready, added = sem("windows_ready"), sem("added")
        onehotT_ps, onehotT_ready, qe_ready = sem("onehotT_ps"), sem("onehotT_ready"), sem("qe_ready")
        prod_ready, score_ready, pv_ready = sem("prod_ready"), sem("score_ready"), sem("pv_ready")
        score_ps, scan_loaded = sem("score_ps"), sem("scan_loaded")
        forward_done, carry_ready, backward_done, gap_ready = sem("forward_done"), sem("carry_ready"), sem("backward_done"), sem("gap_ready")
        ref_steps, ref_ps, below_ready, p_ready = sem("ref_steps"), sem("ref_ps"), sem("below_ready"), sem("p_ready")
        alpha_ready, alpha_ps, rescaled = sem("alpha_ready"), sem("alpha_ps"), sem("rescaled")
        q_steps, add_steps, product_steps = sem("q_steps"), sem("add_steps"), sem("product_steps")
        onehot_ready, products_done, total_copied = sem("onehot_ready"), sem("products_done"), sem("total_copied")
        block = ctx.enter_context(nc.Block())

        @block.sync
        def _(sp):
            def loads(s, i, m, on):
                if on(2):
                    b, par = s - 2, m % 2
                    wait(sp, qe_ready, 2 * (b - 1))
                    sp.sem_inc(q_steps, 1)
                    bases = load_bases(nc, mem, mybir.EngineType.SP, 8 * b, 8)
                    with sp.If(load_flag(nc, mem.tight, mybir.EngineType.SP, b)):
                        sp.dma_start(q_win[:, par, 0, :], mem.q_dram[bass.ds(bases[0], P), :]).then_inc(q_loaded[par], 128)
                    with sp.Else():
                        for k in range(8):
                            sp.dma_start(q_win[:, par, k, :], mem.q_dram[bass.ds(bases[k], P), :]).then_inc(q_loaded[par], 16)
                if on(0):
                    load_idx(mem, sp, src_tiles, s, m, score_ready, 2)
                if on(2):
                    wait(sp, backward_done, b - 1)
                    edges = bass.ds(8 * P * b, 8 * P)
                    sp.dma_start(resets[:, par, 0, :], mem.start_neg[:, edges].to_broadcast([HEADS, 8 * P])).then_inc(resets_loaded[par], 16)
                    sp.dma_start(resets[:, par, 1, :], mem.end_neg[:, edges].to_broadcast([HEADS, 8 * P])).then_inc(resets_loaded[par], 16)

            pipeline(sp, BATCHES, 2, 4, loads)

        @block.gpsimd
        def _(pool):
            gather_rows(nc, mem, pool, mem.kv_dram, kv, BATCHES, pv_ready, 2, rounds)

        @block.vector
        def _(dve):
            nc.vector.memset(carry[:, :], 0.0).then_inc(carry_ready, 1)
            nc.vector.memset(pv[:, :, :, D + HEADS:wide], 1.0)
            firsts = [None]

            def batch(s, i, m, on):
                m1, m2, m3 = (m - 1) % 4, (m - 2) % 4, (m - 3) % 4
                if on(1):
                    for g in range(2):
                        q, slot = 2 * (s - 1) + g, 8 * m1 + 4 * g
                        dve.wait_ge(qe_ready, q + 1)
                        for k in range(4):
                            dve.wait_ge(mem.gathered[slot + k], 16 * (rounds + i + 1 - int(m < 1)))
                        wait(dve, score_ready, q - 1)
                        nc.vector.tensor_tensor(prod[:, g, :].rearrange("e (k f) -> e k f", k=4), kv[:, slot:slot + 4, 0:D],
                                                ps_q[g][:, :].rearrange("e (k f) -> e k f", k=4), ALU.mult).then_inc(prod_ready, 1)
                if on(4):
                    first = firsts[0] if m else load_bases(nc, mem, mybir.EngineType.DVE, 8 * (s - 4), 1)[0]
                    tight = load_flag(nc, mem.tight, mybir.EngineType.DVE, s - 4)
                if on(3):
                    firsts[0] = load_bases(nc, mem, mybir.EngineType.DVE, 8 * (s - 3), 1)[0]
                    node = bass.ds(firsts[0], 1)
                if on(1):
                    for g in range(2):
                        q = 2 * (s - 1) + g
                        dve.wait_ge(prod_ready, q + 1)
                        if g == 0:
                            wait(dve, below_ready, s - 2)
                        nc.vector.tensor_reduce(score[:, m1 % 2, g * 32:g * 32 + 32],
                                                prod[:, g, :].rearrange("e (k d h) -> e k h d", k=4, h=HEADS),
                                                AX.X, ALU.add).then_inc(score_ready, 1)
                if on(4):
                    b = s - 4
                    wait(dve, rescaled, b + 1)
                    wait(dve, windows_ready, 8 * b)
                    dve.sem_inc(add_steps, 1)
                    with dve.If(tight):
                        dve.wait_ge(products_done, b + 1)
                        if on(3):
                            dve.wait_ge(alpha_ps, b + 2)
                        nc.vector.tensor_copy(total[:, :], ps_total[:, 0:wide]).then_inc(total_copied, 1)
                    with dve.Else():
                        bases = load_bases(nc, mem, mybir.EngineType.DVE, 8 * b, 8)
                        for k in range(8):
                            dve.wait_ge(windows_ready, 8 * b + k + 1)
                            wait(dve, added, 8 * b + k)
                            window = mem.acc[:, bass.ds(bases[k], P)]
                            nc.vector.tensor_tensor(window, window, ps_win[:, 0:P], ALU.add)
                            window = mem.den[:, bass.ds(bases[k], P)]
                            nc.vector.tensor_tensor(window, window, ps_win[0:HEADS + 1, P:2 * P], ALU.add).then_inc(added, 1)
                        dve.sem_inc(total_copied, 1)
                if on(0):
                    wait(dve, products_done, s - 3)
                    mark_targets(nc, mem, mem.rel, onehot[:, 8 * m:8 * m + 8, :], s).then_inc(onehot_ready, 1)
                if on(3):
                    b = s - 3
                    dve.wait_ge(p_ready, b + 1)
                    wait(dve, products_done, b - 1)
                    for g in range(2):
                        slot = 8 * m3 + 4 * g
                        p = pv[:, m3 % 2, 4 * g:4 * g + 4, D:D + HEADS].unsqueeze(2).to_broadcast([P, 4, DH, HEADS])
                        nc.vector.tensor_tensor(pv[:, m3 % 2, 4 * g:4 * g + 4, 0:D].rearrange("e k (d h) -> e k d h", h=HEADS),
                                                kv[:, slot:slot + 4, D:2 * D].rearrange("e k (d h) -> e k d h", h=HEADS), p,
                                                ALU.mult).then_inc(pv_ready, 1)
                if on(2):
                    c, par = s - 2, m2 % 2
                    dve.wait_ge(scan_loaded, 2 * (c + 1))
                    dve.wait_ge(resets_loaded[par], 32 * (2 * (i - int(m < 2)) + m2 // 2 + 1))
                    dve.wait_ge(carry_ready, c + 1)
                    nc.vector.tensor_tensor_scan(scan[:, :], resets[:, par, 0, :], scan[:, :], carry[:, 1 - par:2 - par],
                                                 ALU.add, ALU.max).then_inc(forward_done, 1)
                if on(2):
                    dve.wait_ge(forward_done, c + 1)
                    wait(dve, gap_ready, c)
                    nc.vector.tensor_copy(carry[:, par:par + 1], scan[:, 8 * P - 1:8 * P]).then_inc(carry_ready, 1)
                if on(2):
                    dve.wait_ge(carry_ready, c + 2)
                    nc.vector.tensor_tensor_scan(scan[:, ::-1], resets[:, par, 1, ::-1], scan[:, ::-1], -BIG,
                                                 ALU.add, ALU.max).then_inc(backward_done, 1)
                if on(4):
                    b = s - 4
                    with dve.If(tight):
                        dve.wait_ge(windows_ready, 8 * (b + 1))
                        window = mem.acc[:, bass.ds(first, P)]
                        nc.vector.tensor_tensor(window, window, ps_win[:, 0:P], ALU.add)
                        window = mem.den[:, bass.ds(first, P)]
                        nc.vector.tensor_tensor(window, window, ps_win[0:HEADS + 1, P:2 * P], ALU.add).then_inc(added, 8)
                    with dve.Else():
                        dve.sem_inc(add_steps, 1)
                if on(2):
                    dve.wait_ge(backward_done, c + 1)
                    wait(dve, alpha_ready, c)
                    nc.vector.tensor_scalar(gap[:, :], carry[:, 1 - par:2 - par], scan[:, 0:1], 0.0,
                                            ALU.subtract, ALU.min).then_inc(gap_ready, 1)
                if on(3):
                    b = s - 3
                    dve.wait_ge(alpha_ps, b + 1)
                    wait(dve, added, 8 * b)
                    nc.vector.tensor_scalar(mem.acc[:, node], mem.acc[:, node], ps_total[:, 256:257], None, ALU.mult)
                    nc.vector.tensor_scalar(mem.den[0:HEADS, node], mem.den[0:HEADS, node], alpha[:, :], None, ALU.mult).then_inc(rescaled, 1)
                if on(2):
                    dve.wait_ge(ref_ps, c + 1)
                    wait(dve, p_ready, c)
                    nc.vector.tensor_tensor(below[:, :], score[:, par, :], ps_ref[:, 0:64],
                                            ALU.subtract).then_inc(below_ready, 1)

            pipeline(dve, BATCHES, 4, 4, batch)

        @block.tensor
        def _(pe):
            def batch(s, i, m, on):
                m2 = (m - 2) % 4
                c, par = s - 2, m2 % 2
                def scores_to_heads(g):
                    q = 2 * c + g
                    pe.wait_ge(score_ready, q + 1)
                    wait(pe, scan_loaded, q)
                    for k in range(4):
                        last = nc.tensor.transpose(ps_score[0:HEADS, k * P:(k + 1) * P],
                                                   score[:, par, (4 * g + k) * HEADS:(4 * g + k + 1) * HEADS], mem.ident[:, :])
                    last.then_inc(score_ps, 1)

                def targets_to_edges(g):
                    wait(pe, onehotT_ready, 2 * s + g - 1)
                    pe.wait_ge(onehot_ready, s + 1)
                    for k in range(4):
                        last = nc.tensor.transpose(ps_onehotT[g][:, k * P:(k + 1) * P], onehot[:, 8 * m + 4 * g + k, :],
                                                   mem.ident[:, :])
                    last.then_inc(onehotT_ps, 1)

                if on(4):
                    tight = load_flag(nc, mem.tight, mybir.EngineType.PE, s - 4)
                if on(4):
                    b = s - 4
                    pe.wait_ge(pv_ready, 2 * (b + 1))
                    wait(pe, total_copied, b)
                    wait(pe, rescaled, b + 1)
                    pe.sem_inc(product_steps, 1)
                    with pe.If(tight):
                        for k in range(8):
                            last = nc.tensor.matmul(ps_total[:, 0:wide], onehot[:, 8 * m + k, :], pv[:, m % 2, k, :],
                                                    start=(k == 0), stop=(k == 7))
                        last.then_inc(products_done, 1)
                    with pe.Else():
                        for k in range(8):
                            wait(pe, added, 8 * b + k)
                            nc.tensor.matmul(ps_win[:, 0:P], pv[:, m % 2, k, 0:D], onehot[:, 8 * m + k, :], start=True, stop=True)
                            last = nc.tensor.matmul(ps_win[0:HEADS + 1, P:2 * P], pv[:, m % 2, k, D:wide], onehot[:, 8 * m + k, :],
                                                    start=True, stop=True)
                            last.then_inc(windows_ready, 1)
                        wait(pe, windows_ready, 8 * (b + 1))
                        pe.sem_inc(products_done, 1)
                if on(3):
                    pe.wait_ge(alpha_ready, s - 2)
                    wait(pe, rescaled, s - 3)
                    wait(pe, total_copied, s - 4)
                    nc.tensor.matmul(ps_total[:, 256:257], mem.expand[:, :], alpha[:, :], start=True, stop=True).then_inc(alpha_ps, 1)
                if on(0):
                    tight_q = load_flag(nc, mem.tight, mybir.EngineType.PE, s)
                if on(2):
                    scores_to_heads(0)
                    scores_to_heads(1)
                if on(0):
                    targets_to_edges(0)
                    targets_to_edges(1)
                if on(4):
                    with pe.If(tight):
                        pe.wait_ge(total_copied, b + 1)
                        wait(pe, added, 8 * b)
                        nc.tensor.transpose(ps_win[:, 0:P], total[:, 0:D], mem.ident[:, :])
                        nc.tensor.transpose(ps_win[0:HEADS + 1, P:2 * P], total[:, D:wide], mem.ident[:, :]).then_inc(windows_ready, 8)
                    with pe.Else():
                        pe.sem_inc(product_steps, 1)
                if on(0):
                    pe.wait_ge(q_loaded[m % 2], 128 * (2 * i + m // 2 + 1))
                    pe.sem_inc(product_steps, 1)

                    def q_of_edges(shared):
                        for g in range(2):
                            q = 2 * s + g
                            pe.wait_ge(onehotT_ready, q + 1)
                            wait(pe, prod_ready, q - 1)
                            for k in range(4):
                                last = nc.tensor.matmul(ps_q[g][:, k * D:(k + 1) * D], onehotT[:, g, k * P:(k + 1) * P],
                                                        q_win[:, m % 2, 0 if shared else 4 * g + k, :], start=True, stop=True)
                            last.then_inc(qe_ready, 1)

                    with pe.If(tight_q):
                        q_of_edges(True)
                    with pe.Else():
                        q_of_edges(False)
                if on(2):
                    pe.wait_ge(backward_done, c + 1)
                    wait(pe, below_ready, c)
                    pe.sem_inc(ref_steps, 1)
                    for k in range(8):
                        last = nc.tensor.transpose(ps_ref[:, k * HEADS:(k + 1) * HEADS], scan[:, k * P:(k + 1) * P],
                                                   mem.ident[0:HEADS, 0:HEADS])
                    last.then_inc(ref_ps, 1)

            pipeline(pe, BATCHES, 4, 4, batch)

        @block.scalar
        def _(act):
            def batch(s, i, m, on):
                c, par = s - 2, (m - 2) % 4 % 2
                if on(2):
                    for g in range(2):
                        act.wait_ge(score_ps, 2 * c + g + 1)
                        if g == 0:
                            wait(act, ref_ps, c)
                            wait(act, gap_ready, c)
                        nc.scalar.copy(scan[:, g * 512:g * 512 + 512], ps_score[0:HEADS, :]).then_inc(scan_loaded, 1)
                if on(0):
                    for g in range(2):
                        q = 2 * s + g
                        act.wait_ge(onehotT_ps, q + 1)
                        wait(act, qe_ready, q - 1)
                        nc.scalar.copy(onehotT[:, g, :], ps_onehotT[g][:, :]).then_inc(onehotT_ready, 1)
                if on(2):
                    act.wait_ge(gap_ready, c + 1)
                    wait(act, rescaled, c)
                    nc.scalar.activation(alpha[:, :], gap[:, :], ACT.Exp).then_inc(alpha_ready, 1)
                    act.wait_ge(below_ready, c + 1)
                    wait(act, products_done, c - 1)
                    nc.scalar.activation(pv[:, par, :, D:D + HEADS], below[:, :].rearrange("e (k h) -> e k h", h=HEADS),
                                         ACT.Exp).then_inc(p_ready, 1)

            pipeline(act, BATCHES, 4, 4, batch)



def run_pass(nc, mem, engine, engine_type, edge_lag, edges, pairs, last_step, pairs_first=False):
    def peeled(first, last, with_edges, start):
        for s in range(first, last):
            i, m = s // 4, s % 4
            if with_edges and not pairs_first:
                edges(s, i, m, lambda l: 0 <= s - l < BATCHES)
            for j in range(m + 4 * ((last_step - m) // 4), -1, -4):
                if 0 <= i - start - j // 4 < PAIRS:
                    pairs(j, i - start - j // 4, start > 0)
            if with_edges and pairs_first:
                edges(s, i, m, lambda l: 0 <= s - l < BATCHES)

    def loop(first, last, with_edges, start=None):
        with engine.Fori(first, last) as i:
            for m in range(4):
                if with_edges and not pairs_first:
                    edges(4 * i + m, i, m, lambda l: True)
                if start is not None:
                    for j in range(m + 4 * ((last_step - m) // 4), -1, -4):
                        pairs(j, i - start - j // 4, start > 0)
                if with_edges and pairs_first:
                    edges(4 * i + m, i, m, lambda l: True)

    full = BATCHES // 4
    with engine.If(load_flag(nc, mem.regular, engine_type, 0)):
        peeled(0, 4, True, PAIR_START)
        loop(1, PAIR_START, True)
        peeled(4 * PAIR_START, 4 * PAIR_START + 8, True, PAIR_START)
        loop(PAIR_START + 2, full, True, PAIR_START)
        peeled(4 * full, 4 * (PAIR_START + PAIRS) + last_step, True, PAIR_START)
    with engine.Else():
        pipeline(engine, BATCHES, edge_lag, 4, edges)
        peeled(0, 8, False, 0)
        loop(2, PAIRS, False, 0)
        peeled(4 * PAIRS, 4 * PAIRS + last_step, False, 0)


class PairStage:

    def __init__(self, nc, mem, ctx, sem, added, kind, x_from=None, x_to=None, y_from=None, y_to=None,
                 w=None, w_low=None, bias=None, w_next=None):
        self.nc, self.mem, self.kind, self.added, self.bias = nc, mem, kind, added, bias
        self.x_from, self.x_to, self.y_from, self.y_to = x_from, x_to, y_from, y_to
        self.norm, self.makes_y = kind != "first_conv", y_to is not None
        self.combine = 2 if kind == "max" else 1
        self.x_new_at = self.combine + 1 if self.norm else self.combine
        self.flip = self.x_new_at + 1
        self.y_at = self.flip + 1
        self.last_step = self.y_at if self.makes_y else self.flip
        sb = lambda n, *shape: sb_in(nc, ctx, f"{kind}_{n}", [P, *shape])
        self.sumsT, self.x_in, self.y_in, self.r, self.x_new, self.y = (sb(n, PAIR) for n in ("sumsT", "x_in", "y_in", "r", "x_new", "y"))
        self.xT, self.preT, self.x_newT = (sb(n, PAIR) for n in ("xT", "preT", "x_newT"))
        self.stats, self.mean_var, self.std, self.rstd, self.shift = sb("stats", 2, 6), sb("mean_var", 2, 2), sb("std", 2), sb("rstd", 2), sb("shift", 2)
        self.w_sb, self.w_low_sb, self.w_next_sb, self.bias_sb, self.eps_sb = sb("w", D), sb("w_low", D), sb("w_next", D), sb("bias", D), sb("eps", 1)
        self.weights_loaded, self.eps_ready, self.dinv_steps = sem("weights_loaded"), sem("eps_ready"), sem("dinv_steps")
        self.loaded, self.x_stored, self.y_stored = sem("loaded"), sem("x_stored"), sem("y_stored")
        self.turned_ps, self.pre_ready, self.xT_ready, self.proj_ps, self.combined = (sem(n) for n in ("turned_ps", "pre_ready", "xT_ready", "proj_ps", "combined"))
        self.stats_ready, self.var_ready, self.std_ready = sem("stats_ready"), sem("var_ready"), sem("std_ready")
        self.rstd_ready, self.shift_ready, self.x_ready = sem("rstd_ready"), sem("shift_ready"), sem("x_ready")
        self.x_newT_ps, self.x_newT_ready, self.y_ps, self.y_ready = (sem(n) for n in ("x_newT_ps", "x_newT_ready", "y_ps", "y_ready"))
        self.partial = sem("partial")
        self.sp_steps, self.dve_steps = sem("sp_steps"), sem("dve_steps")
        self.ps_turned = mem.bank[6][:, 0:PAIR]
        self.ps_high, self.ps_low, self.ps_y = mem.bank[7][:, 0:PAIR], mem.bank[7][:, PAIR:2 * PAIR], mem.bank[7][:, 0:PAIR]
        self.weights = [(dst, src) for dst, src in ((self.w_sb, w), (self.w_low_sb, w_low), (self.w_next_sb, w_next)) if src is not None]
        if bias is not None:
            self.weights.append((self.bias_sb, bias.to_broadcast([P, D])))
        self.n_loads = 1 + (x_from is not None) + (y_from is not None)

    @staticmethod
    def by_tile(ap):
        return ap.rearrange("p (k f) -> p k f", k=2)

    @staticmethod
    def rows_of(table, c):
        rows = table[0:PAIRS * PAIR, :].rearrange("(c k p) f -> c p k f", k=2, p=P)
        return rows[bass.ds(c, 1), :, :, :].rearrange("o p k f -> (o p) k f")

    @staticmethod
    def per_node(values, c):
        return values[:, bass.ds(2 * c, 2)].unsqueeze(2).to_broadcast([P, 2, D])

    def load_weights(self, sp):
        for dst, src in self.weights:
            sp.dma_start(dst[:, :], src).then_inc(self.weights_loaded, 16)

    def wait_weights(self, engine):
        if self.weights:
            engine.wait_ge(self.weights_loaded, 16 * len(self.weights))

    def wait_stored(self, act):
        if self.x_to is not None:
            act.wait_ge(self.x_stored, 16 * PAIRS)
        if self.makes_y:
            act.wait_ge(self.y_stored, 16 * PAIRS)

    def sync(self, j, c, early):
        sp = self.nc.sync
        if j == 0:
            done = 8 * (4 * c + PAIR_DONE) if early else TILES
            if isinstance(done, int):
                done = min(done, TILES)
            sp.wait_ge(self.added, done)
            wait(sp, self.combined, c)
            sp.sem_inc(self.sp_steps, 1)
            sp.dma_start(self.sumsT[:, :], self.mem.acc[:, bass.ds(c * PAIR, PAIR)]).then_inc(self.loaded, 16)
            if self.x_from is not None:
                sp.dma_start(self.by_tile(self.x_in[:, :]), self.rows_of(self.x_from, c)).then_inc(self.loaded, 16)
            if self.y_from is not None:
                sp.dma_start(self.by_tile(self.y_in[:, :]), self.rows_of(self.y_from, c)).then_inc(self.loaded, 16)

    def prepare_vector(self, dve):
        nc, mem = self.nc, self.mem
        nc.vector.memset(self.eps_sb[:, :], EPS).then_inc(self.eps_ready, 1)
        self.wait_weights(dve)
        if self.kind == "max":
            nc.vector.tensor_scalar(mem.mask[:, :], mem.count[:, :], 1.0, None, ALU.min).then_inc(self.dinv_steps, 1)
            nc.vector.tensor_scalar(mem.dinv[:, :], mem.count[:, :], 1.0, None, ALU.add).then_inc(self.dinv_steps, 1)
            dve.wait_ge(self.dinv_steps, 3)
            nc.vector.reciprocal(mem.dinv[:, :], mem.dinv[:, :]).then_inc(self.dinv_steps, 1)
            dve.wait_ge(self.dinv_steps, 4)

    def vector(self, j, c, early):
        nc, mem, dve, by_tile = self.nc, self.mem, self.nc.vector, self.by_tile
        r = self.r[:, :]
        if self.makes_y and j == self.y_at:
            dve.wait_ge(self.y_ps, c + 1)
            wait(dve, self.y_stored, 16 * c)
            nc.vector.tensor_tensor(by_tile(self.y[:, :]), by_tile(self.ps_y), self.per_node(mem.dinv, c), ALU.mult).then_inc(self.y_ready, 1)
        if self.norm and j == self.x_new_at:
            dve.wait_ge(self.std_ready, c + 1)
            wait(dve, self.x_ready, c)
            nc.vector.reciprocal(self.rstd[:, :], self.std[:, :]).then_inc(self.rstd_ready, 1)
            dve.wait_ge(self.rstd_ready, c + 1)
            nc.vector.scalar_tensor_tensor(self.shift[:, :], self.mean_var[:, :, 0], -1.0, self.rstd[:, :],
                                           ALU.mult, ALU.mult).then_inc(self.shift_ready, 1)
        if self.kind == "max" and j == 1:
            dve.wait_ge(self.turned_ps, c + 1)
            wait(dve, self.proj_ps, c)
            nc.vector.tensor_tensor(self.preT[:, :], self.ps_turned, self.sumsT[:, :], ALU.subtract).then_inc(self.pre_ready, 1)
        if j == self.combine:
            partials = 3 if self.norm else 2
            if self.kind == "weighted":
                dve.wait_ge(self.turned_ps, c + 1)
                wait(dve, self.x_ready, c)
                nc.vector.tensor_tensor(r, self.ps_turned, self.x_in[:, :], ALU.add).then_inc(self.combined, 1)
            if self.kind == "max":
                dve.wait_ge(self.proj_ps, c + 1)
                wait(dve, self.x_ready, c)
                nc.vector.tensor_tensor(by_tile(r), by_tile(self.ps_low), self.per_node(mem.mask, c), ALU.mult).then_inc(self.partial, 1)
                dve.wait_ge(self.partial, 3 * c + 1)
                nc.vector.tensor_tensor(r, r, self.ps_high, ALU.add).then_inc(self.partial, 1)
            if self.y_from is not None:
                dve.wait_ge(self.turned_ps, c + 1)
                wait(dve, self.x_ready, c)
                nc.vector.tensor_tensor(r, self.ps_turned, self.y_in[:, :], ALU.add).then_inc(self.partial, 1)
                dve.wait_ge(self.partial, partials * c + 1)
                nc.vector.tensor_tensor(by_tile(r), by_tile(r), self.per_node(mem.dinv, c), ALU.mult).then_inc(self.partial, 1)
            if self.bias is not None:
                dve.wait_ge(self.partial, partials * c + 2)
                nc.vector.tensor_tensor(by_tile(r), by_tile(r), self.bias_sb[:, :].unsqueeze(1).to_broadcast([P, 2, D]),
                                        ALU.add).then_inc(self.partial if self.norm else self.combined, 1)
            if self.bias is not None and self.norm:
                dve.wait_ge(self.partial, 3 * c + 3)
                if self.kind == "max":
                    nc.vector.scalar_tensor_tensor(r, r, 0.0, self.x_in[:, :], ALU.max, ALU.add).then_inc(self.combined, 1)
                else:
                    nc.vector.tensor_tensor(r, r, self.x_in[:, :], ALU.add).then_inc(self.combined, 1)
            if self.norm:
                dve.wait_ge(self.combined, c + 1)
                for k in range(2):
                    last = nc.vector.bn_stats(self.stats[:, k, :], self.r[:, k * D:(k + 1) * D])
                last.then_inc(self.stats_ready, 1)
                dve.wait_ge(self.stats_ready, c + 1)
                wait(dve, self.shift_ready, c)
                dve.sem_inc(self.dve_steps, 1)
                for k in range(2):
                    last = nc.vector.bn_aggr(self.mean_var[:, k, :], self.stats[:, k, :])
                last.then_inc(self.var_ready, 1)

    def tensor(self, j, c, early):
        nc, mem, pe = self.nc, self.mem, self.nc.tensor
        tiles = [slice(k * P, (k + 1) * P) for k in range(2)]
        if self.makes_y and j == self.y_at:
            pe.wait_ge(self.x_newT_ready, c + 1)
            wait(pe, self.y_ready, c)
            for tile in tiles:
                last = nc.tensor.matmul(self.ps_y[:, tile], self.x_newT[:, tile], self.w_next_sb[:, :], start=True, stop=True)
            last.then_inc(self.y_ps, 1)
        if self.makes_y and j == self.flip:
            pe.wait_ge(self.x_ready, c + 1)
            for tile in tiles:
                last = nc.tensor.transpose(self.ps_turned[:, tile], self.x_new[:, tile], mem.ident[:, :])
            last.then_inc(self.x_newT_ps, 1)
        if self.kind == "max" and j == 2:
            pe.wait_ge(self.pre_ready, c + 1)
            pe.wait_ge(self.xT_ready, c + 1)
            wait(pe, self.combined, c)
            wait(pe, self.y_ready, c)
            for tile in tiles:
                nc.tensor.matmul(self.ps_high[:, tile], self.xT[:, tile], self.w_sb[:, :], start=True, stop=True)
                last = nc.tensor.matmul(self.ps_low[:, tile], self.preT[:, tile], self.w_low_sb[:, :], start=True, stop=True)
            last.then_inc(self.proj_ps, 1)
        if j == 1:
            pe.wait_ge(self.loaded, 16 * self.n_loads * (c + 1))
            wait(pe, self.x_newT_ready if self.makes_y else self.combined, c)
            source = self.x_in if self.kind == "max" else self.sumsT
            for tile in tiles:
                last = nc.tensor.transpose(self.ps_turned[:, tile], source[:, tile], mem.ident[:, :])
            last.then_inc(self.turned_ps, 1)

    def prepare_scalar(self, act):
        act.wait_ge(self.eps_ready, 1)
        if self.kind == "max":
            act.wait_ge(self.dinv_steps, 2)
            self.nc.scalar.activation(self.mem.dinv[:, :], self.mem.dinv[:, :], ACT.Sqrt).then_inc(self.dinv_steps, 1)

    def scalar(self, j, c, early):
        nc, act = self.nc, self.nc.scalar
        if self.makes_y and j == self.y_at:
            act.wait_ge(self.y_ready, c + 1)
            act.dma_start(self.rows_of(self.y_to, c), self.by_tile(self.y[:, :])).then_inc(self.y_stored, 16)
        if j == self.flip:
            if self.x_to is not None:
                act.wait_ge(self.x_ready, c + 1)
                act.dma_start(self.rows_of(self.x_to, c), self.by_tile(self.x_new[:, :])).then_inc(self.x_stored, 16)
            if self.makes_y:
                act.wait_ge(self.x_newT_ps, c + 1)
                wait(act, self.y_ps, c)
                nc.scalar.copy(self.x_newT[:, :], self.ps_turned).then_inc(self.x_newT_ready, 1)
        if self.norm and j == self.combine:
            act.wait_ge(self.var_ready, c + 1)
            wait(act, self.rstd_ready, c)
            nc.scalar.activation(self.std[:, :], self.mean_var[:, :, 1], ACT.Sqrt, bias=self.eps_sb[:, 0:1]).then_inc(self.std_ready, 1)
        if j == self.x_new_at:
            act.wait_ge(self.shift_ready if self.norm else self.combined, c + 1)
            if self.makes_y:
                wait(act, self.x_newT_ps, c)
            if self.x_to is not None:
                wait(act, self.x_stored, 16 * c)
            if self.norm:
                for k in range(2):
                    tile = slice(k * D, (k + 1) * D)
                    last = nc.scalar.activation(self.x_new[:, tile], self.r[:, tile], ACT.Identity,
                                                bias=self.shift[:, k:k + 1], scale=self.rstd[:, k:k + 1])
                last.then_inc(self.x_ready, 1)
            else:
                nc.scalar.activation(self.x_new[:, :], self.r[:, :], ACT.Relu).then_inc(self.x_ready, 1)
        if self.kind == "max" and j == 1:
            act.wait_ge(self.pre_ready, c + 1)
            wait(act, self.proj_ps, c)
            nc.scalar.copy(self.xT[:, :], self.ps_turned).then_inc(self.xT_ready, 1)


def sum_layer(nc, mem, name, table, src_tiles, stage, attr64=None, attr8=None):
    rounds = mem.gather_rounds
    mem.gather_rounds += TILES // RING
    weighted = attr64 is not None
    with ExitStack() as ctx:
        sem = semaphores(nc, ctx, name)
        rows = sb_in(nc, ctx, name + "rows", [P, RING, D])
        onehot = sb_in(nc, ctx, name + "onehot", [P, 2, 8, P])
        if weighted:
            scaled = sb_in(nc, ctx, name + "scaled", [P, 2, 8, D])
            a64 = sb_in(nc, ctx, name + "a64", [P, 2, 8, 64])
            a8 = sb_in(nc, ctx, name + "a8", [P, 2, 8, 8])
            sum64 = sb_in(nc, ctx, name + "sum64", [P, 8])
            sum8 = sb_in(nc, ctx, name + "sum8", [P, 8])
            weight = sb_in(nc, ctx, name + "weight", [P, 2, 8])
            attrs_loaded = [sem(f"attrs_loaded{i}") for i in range(2)]
            attrs_summed, weight_ready, scaled_ready = sem("attrs_summed"), sem("weight_ready"), sem("scaled_ready")
        zeroed, onehot_ready, sums_ready, added = sem("zeroed"), sem("onehot_ready"), sem("sums_ready"), sem("added")
        pairs = PairStage(nc, mem, ctx, sem, added, **stage)
        block = ctx.enter_context(nc.Block())

        @block.sync
        def _(sp):
            def loads(s, i, m, on):
                if not on(0):
                    return
                load_idx(mem, sp, src_tiles, s, m, sums_ready, 8)
                if weighted:
                    wait(sp, attrs_summed, 2 * (s - 1))
                    sp.dma_start(a64[:, m % 2, :, :], attr64[:, bass.ds(8 * s, 8), :]).then_inc(attrs_loaded[m % 2], 16)
                    sp.dma_start(a8[:, m % 2, :, :], attr8[:, bass.ds(8 * s, 8), :]).then_inc(attrs_loaded[m % 2], 16)

            pairs.load_weights(sp)
            run_pass(nc, mem, sp, mybir.EngineType.SP, 0, loads, pairs.sync, pairs.last_step)

        @block.gpsimd
        def _(pool):
            if weighted:
                gather_rows(nc, mem, pool, table, rows, BATCHES, scaled_ready, 8, rounds)
            else:
                gather_rows(nc, mem, pool, table, rows, BATCHES, sums_ready, 8, rounds)

        @block.vector
        def _(dve):
            nc.vector.memset(mem.acc[:, :], 0.0).then_inc(zeroed, 1)

            def step(s, i, m, on):
                if on(0) and weighted:
                    dve.wait_ge(attrs_loaded[m % 2], 32 * (2 * i + m // 2 + 1))
                    wait(dve, weight_ready, s)
                    nc.vector.tensor_reduce(sum64[:, :], a64[:, m % 2, :, :], AX.X, ALU.add).then_inc(attrs_summed, 1)
                    nc.vector.tensor_reduce(sum8[:, :], a8[:, m % 2, :, :], AX.X, ALU.add).then_inc(attrs_summed, 1)
                    dve.wait_ge(attrs_summed, 2 * (s + 1))
                    wait(dve, scaled_ready, 8 * (s - 1))
                    nc.vector.tensor_tensor(weight[:, m % 2, :], sum64[:, :], sum8[:, :], ALU.mult).then_inc(weight_ready, 1)
                if on(0):
                    wait(dve, sums_ready, 8 * (s - 1))
                    mark_targets(nc, mem, mem.rel, onehot[:, m % 2, :, :], s).then_inc(onehot_ready, 1)
                if on(1):
                    bases = load_bases(nc, mem, mybir.EngineType.DVE, 8 * (s - 1), 8)
                    for k in range(8):
                        t, bank = 8 * (s - 1) + k, (m - 1) % 2 * 2 + k // 4
                        dve.wait_ge(sums_ready, t + 4 - k % 4)
                        if isinstance(s, int) and s == 1 and k == 0:
                            dve.wait_ge(zeroed, 1)
                        wait(dve, added, t)
                        window = mem.acc[:, bass.ds(bases[k], P)]
                        nc.vector.tensor_tensor(window, window, mem.bank[bank][:, k % 4 * P:(k % 4 + 1) * P], ALU.add).then_inc(added, 1)

            pairs.prepare_vector(dve)
            run_pass(nc, mem, dve, mybir.EngineType.DVE, 1, step, pairs.vector, pairs.last_step)

        @block.scalar
        def _(act):
            def scale(s, i, m, on):
                if on(0) and weighted:
                    act.wait_ge(weight_ready, s + 1)
                    for k in range(8):
                        t, slot = 8 * s + k, 8 * m + k
                        act.wait_ge(mem.gathered[slot], 16 * (rounds + i + 1))
                        wait(act, sums_ready, t - 15)
                        nc.scalar.activation(scaled[:, m % 2, k, :], rows[:, slot, :], ACT.Copy,
                                             scale=weight[:, m % 2, k:k + 1]).then_inc(scaled_ready, 1)

            pairs.prepare_scalar(act)
            run_pass(nc, mem, act, mybir.EngineType.Activation, 0, scale, pairs.scalar, pairs.last_step)
            pairs.wait_stored(act)

        @block.tensor
        def _(pe):
            def sums(s, i, m, on):
                if not on(0):
                    return
                for k in range(8):
                    t, slot, bank = 8 * s + k, 8 * m + k, m % 2 * 2 + k // 4
                    if k % 4 == 0:
                        wait(pe, added, t - 12)
                    if k == 0:
                        pe.wait_ge(onehot_ready, s + 1)
                    if weighted:
                        pe.wait_ge(scaled_ready, t + 1)
                        source = scaled[:, m % 2, k, :]
                    else:
                        pe.wait_ge(mem.gathered[slot], 16 * (rounds + i + 1))
                        source = rows[:, slot, :]
                    nc.tensor.matmul(mem.bank[bank][:, k % 4 * P:(k % 4 + 1) * P], source, onehot[:, m % 2, k, :],
                                     start=True, stop=True).then_inc(sums_ready, 1)

            pairs.wait_weights(pe)
            run_pass(nc, mem, pe, mybir.EngineType.PE, 0, sums, pairs.tensor, pairs.last_step, pairs_first=True)


def min_layer(nc, mem, table, src_tiles, stage):
    rounds = mem.gather_rounds
    mem.gather_rounds += TILES // RING
    with ExitStack() as ctx:
        sem = semaphores(nc, ctx, "m_")
        rows = sb_in(nc, ctx, "m_rows", [P, RING, D])
        lasts = sb_in(nc, ctx, "lasts", [P, 2, 8, P])
        resets = sb_in(nc, ctx, "m_resets", [P, 2, 8 * P], BF)
        minT = sb_in(nc, ctx, "minT", [P, 4, 4 * P])
        mins = sb_in(nc, ctx, "mins", [P, 4, 4 * D])
        resets_loaded = [sem(f"resets_loaded{i}") for i in range(2)]
        rowsT_ps, minT_ready, mins_ps, mins_ready, picked_ps = sem("rowsT_ps"), sem("minT_ready"), sem("mins_ps"), sem("mins_ready"), sem("picked_ps")
        lasts_ready, added, zeroed = sem("lasts_ready"), sem("added"), sem("zeroed")
        pairs = PairStage(nc, mem, ctx, sem, added, **stage)
        block = ctx.enter_context(nc.Block())

        @block.sync
        def _(sp):
            def loads(s, i, m, on):
                if not on(0):
                    return
                load_idx(mem, sp, src_tiles, s, m, rowsT_ps, 2)
                wait(sp, minT_ready, 2 * (s - 1))
                sp.dma_start(resets[:, m % 2, :], mem.start_pos[:, bass.ds(8 * P * s, 8 * P)].to_broadcast([P, 8 * P])
                             ).then_inc(resets_loaded[m % 2], 16)

            pairs.load_weights(sp)
            run_pass(nc, mem, sp, mybir.EngineType.SP, 0, loads, pairs.sync, pairs.last_step)

        @block.gpsimd
        def _(pool):
            gather_rows(nc, mem, pool, table, rows, BATCHES, rowsT_ps, 2, rounds)

        @block.vector
        def _(dve):
            nc.vector.memset(mem.acc[:, :], 0.0).then_inc(zeroed, 1)

            def step(s, i, m, on):
                if on(3):
                    bases = load_bases(nc, mem, mybir.EngineType.DVE, 8 * (s - 3), 8)
                    for k in range(8):
                        t = 8 * (s - 3) + k
                        dve.wait_ge(picked_ps, 2 * (s - 3) + k // 4 + 1)
                        if isinstance(s, int) and s == 3 and k == 0:
                            dve.wait_ge(zeroed, 1)
                        wait(dve, added, t)
                        window = mem.acc[:, bass.ds(bases[k], P)]
                        nc.vector.tensor_tensor(window, window, mem.bank[4 + k // 4][:, k % 4 * P:(k % 4 + 1) * P],
                                                ALU.add).then_inc(added, 1)
                if on(0):
                    for g in range(2):
                        q, slot = 2 * s + g, m % 2 * 2 + g
                        dve.wait_ge(rowsT_ps, q + 1)
                        if g == 0:
                            dve.wait_ge(resets_loaded[m % 2], 16 * (2 * i + m // 2 + 1))
                        wait(dve, minT_ready, q)
                        wait(dve, mins_ps, q - 3)
                        start = 0.0 if isinstance(q, int) and q == 0 else minT[:, (slot - 1) % 4, 4 * P - 1:4 * P]
                        nc.vector.tensor_tensor_scan(minT[:, slot, :], resets[:, m % 2, g * 512:g * 512 + 512], mem.bank[g][:, :],
                                                     start, ALU.add, ALU.min).then_inc(minT_ready, 1)
                if on(1):
                    wait(dve, picked_ps, 2 * (s - 2))
                    mark_targets(nc, mem, mem.rel_end, lasts[:, (m - 1) % 2, :, :], s - 1).then_inc(lasts_ready, 1)

            pairs.prepare_vector(dve)
            run_pass(nc, mem, dve, mybir.EngineType.DVE, 3, step, pairs.vector, pairs.last_step)

        @block.tensor
        def _(pe):
            def step(s, i, m, on):
                if on(0):
                    for g in range(2):
                        q = 2 * s + g
                        wait(pe, minT_ready, q - 1)
                        for k in range(4):
                            slot = 8 * m + 4 * g + k
                            pe.wait_ge(mem.gathered[slot], 16 * (rounds + i + 1))
                            last = nc.tensor.transpose(mem.bank[g][:, k * P:(k + 1) * P], rows[:, slot, :], mem.ident[:, :])
                        last.then_inc(rowsT_ps, 1)
                if on(1):
                    for g in range(2):
                        q, slot = 2 * (s - 1) + g, (m - 1) % 2 * 2 + g
                        pe.wait_ge(minT_ready, q + 1)
                        wait(pe, mins_ready, q - 1)
                        for k in range(4):
                            last = nc.tensor.transpose(mem.bank[2 + g][:, k * D:(k + 1) * D], minT[:, slot, k * P:(k + 1) * P], mem.ident[:, :])
                        last.then_inc(mins_ps, 1)
                if on(2):
                    for g in range(2):
                        q, slot = 2 * (s - 2) + g, m % 2 * 2 + g
                        pe.wait_ge(mins_ready, q + 1)
                        pe.wait_ge(lasts_ready, s - 1)
                        wait(pe, added, 4 * (q - 1))
                        for k in range(4):
                            last = nc.tensor.matmul(mem.bank[4 + g][:, k * P:(k + 1) * P], mins[:, slot, k * D:(k + 1) * D],
                                                    lasts[:, m % 2, 4 * g + k, :], start=True, stop=True)
                        last.then_inc(picked_ps, 1)

            pairs.wait_weights(pe)
            run_pass(nc, mem, pe, mybir.EngineType.PE, 2, step, pairs.tensor, pairs.last_step, pairs_first=True)

        @block.scalar
        def _(act):
            def step(s, i, m, on):
                for g in range(2):
                    if on(1):
                        q, slot = 2 * (s - 1) + g, (m - 1) % 2 * 2 + g
                        act.wait_ge(mins_ps, q + 1)
                        wait(act, picked_ps, q - 3)
                        nc.scalar.copy(mins[:, slot, :], mem.bank[2 + g][:, :]).then_inc(mins_ready, 1)

            pairs.prepare_scalar(act)
            run_pass(nc, mem, act, mybir.EngineType.Activation, 1, step, pairs.scalar, pairs.last_step)
            pairs.wait_stored(act)


def normalise_attention(nc, mem, x_rows, out_rows):
    with ExitStack() as ctx:
        sem = semaphores(nc, ctx, "n_")
        sb = lambda n, *shape: sb_in(nc, ctx, f"n_{n}", [P, *shape])
        sumsT, x_in, r, x_new = (sb(n, 3, CHUNK) for n in ("sumsT", "x_in", "r", "x_new"))
        den_in = sb_in(nc, ctx, "n_den_in", [HEADS + 1, 3, CHUNK])
        inverse = sb("inverse", 3, 3 * HEADS)
        stats, mean_var = sb("stats", 3, 3, 6), sb("mean_var", 3, 3, 2)
        std, rstd, shift, eps_sb = sb("std", 3, 3), sb("rstd", 3, 3), sb("shift", 3, 3), sb("eps", 1)
        eps_ready = sem("eps_ready")
        loaded = [sem(f"loaded{i}") for i in range(3)]
        stored = [sem(f"stored{i}") for i in range(3)]
        turned_ps, den_ps, den_read, inverse_ready, scaled_ready = (sem(n) for n in ("turned_ps", "den_ps", "den_read", "inverse_ready", "scaled_ready"))
        combined, stats_ready, var_ready = sem("combined"), sem("stats_ready"), sem("var_ready")
        std_ready, rstd_ready, shift_ready, x_ready = (sem(n) for n in ("std_ready", "rstd_ready", "shift_ready", "x_ready"))
        sp_steps, dve_steps, pe_steps = sem("sp_steps"), sem("dve_steps"), sem("pe_steps")
        ps_turned = [mem.bank[i][:, 0:CHUNK] for i in range(3)]
        ps_den = mem.bank[3]
        block = ctx.enter_context(nc.Block())
        by_tile = lambda ap: ap.rearrange("p (k f) -> p k f", k=3)
        rows_of = lambda table, c: table.rearrange("(c k p) f -> c p k f", k=3, p=P)[bass.ds(c, 1), :, :, :].rearrange("o p k f -> (o p) k f")

        @block.sync
        def _(sp):
            def step(s, i, m, on):
                if on(0):
                    wait(sp, combined, s - 2)
                    sp.sem_inc(sp_steps, 1)
                    nodes = bass.ds(s * CHUNK, CHUNK)
                    sp.dma_start(sumsT[:, m, :], mem.acc[:, nodes]).then_inc(loaded[m], 16)
                    sp.dma_start(den_in[:, m, :], mem.den[:, nodes]).then_inc(loaded[m], 16)
                    sp.dma_start(by_tile(x_in[:, m, :]), rows_of(x_rows, s)).then_inc(loaded[m], 16)
                if on(4):
                    c, slot = s - 4, (m - 4) % 3
                    sp.wait_ge(x_ready, c + 1)
                    sp.dma_start(rows_of(out_rows, c), by_tile(x_new[:, slot, :])).then_inc(stored[slot], 16)

            pipeline(sp, CHUNKS, 4, 3, step, peel=7)
            for n in range(3):
                sp.wait_ge(stored[n], 16 * (CHUNKS // 3))

        @block.vector
        def _(dve):
            nc.vector.memset(eps_sb[:, :], EPS).then_inc(eps_ready, 1)

            def step(s, i, m, on):
                if on(3):
                    c, slot = s - 3, (m - 3) % 3
                    dve.wait_ge(std_ready, c + 1)
                    wait(dve, x_ready, c - 2)
                    nc.vector.reciprocal(rstd[:, slot, :], std[:, slot, :]).then_inc(rstd_ready, 1)
                    dve.wait_ge(rstd_ready, c + 1)
                    nc.vector.scalar_tensor_tensor(shift[:, slot, :], mean_var[:, slot, :, 0], -1.0, rstd[:, slot, :],
                                                   ALU.mult, ALU.mult).then_inc(shift_ready, 1)
                if on(2):
                    c, slot = s - 2, (m - 2) % 3
                    dve.wait_ge(combined, c + 1)
                    for k in range(3):
                        last = nc.vector.bn_stats(stats[:, slot, k, :], r[:, slot, k * D:(k + 1) * D])
                    last.then_inc(stats_ready, 1)
                if on(1):
                    c, slot = s - 1, (m - 1) % 3
                    dve.wait_ge(den_ps, c + 1)
                    dve.sem_inc(dve_steps, 1)
                    heads = ps_den[:, 0:3 * 16].rearrange("p (k h) -> p k h", k=3)
                    nc.vector.tensor_copy(mem.count[:, bass.ds(3 * c, 3)], heads[:, :, HEADS])
                    nc.vector.tensor_scalar(inverse[:, slot, :].rearrange("p (k h) -> p k h", k=3), heads[:, :, 0:HEADS],
                                            TINY, None, ALU.max).then_inc(den_read, 1)
                    dve.wait_ge(den_read, c + 1)
                    nc.vector.reciprocal(inverse[:, slot, :], inverse[:, slot, :]).then_inc(inverse_ready, 1)
                    dve.wait_ge(turned_ps, c + 1)
                    wait(dve, x_ready, c - 2)
                    dve.wait_ge(inverse_ready, c + 1)
                    for k in range(3):
                        tile = slice(k * D, (k + 1) * D)
                        last = nc.vector.tensor_tensor(
                            r[:, slot, tile].rearrange("p (d h) -> p d h", h=HEADS),
                            ps_turned[slot][:, tile].rearrange("p (d h) -> p d h", h=HEADS),
                            inverse[:, slot, k * HEADS:(k + 1) * HEADS].unsqueeze(1).to_broadcast([P, DH, HEADS]), ALU.mult)
                    last.then_inc(scaled_ready, 1)
                    dve.wait_ge(scaled_ready, c + 1)
                    nc.vector.tensor_tensor(r[:, slot, :], r[:, slot, :], x_in[:, slot, :], ALU.add).then_inc(combined, 1)
                if on(2):
                    d, d_slot = s - 2, (m - 2) % 3
                    dve.wait_ge(stats_ready, d + 1)
                    wait(dve, shift_ready, d - 2)
                    dve.sem_inc(dve_steps, 1)
                    for k in range(3):
                        last = nc.vector.bn_aggr(mean_var[:, d_slot, k, :], stats[:, d_slot, k, :])
                    last.then_inc(var_ready, 1)

            pipeline(dve, CHUNKS, 4, 3, step, peel=7)

        @block.tensor
        def _(pe):
            def step(s, i, m, on):
                if on(1):
                    c, slot = s - 1, (m - 1) % 3
                    pe.wait_ge(loaded[slot], 48 * (i + (m - 1) // 3 + 1))
                    wait(pe, combined, c - 2)
                    for k in range(3):
                        last = nc.tensor.transpose(ps_turned[slot][:, k * P:(k + 1) * P], sumsT[:, slot, k * P:(k + 1) * P], mem.ident[:, :])
                    last.then_inc(turned_ps, 1)
                    wait(pe, den_read, c)
                    pe.sem_inc(pe_steps, 1)
                    for k in range(3):
                        last = nc.tensor.transpose(ps_den[:, 16 * k:16 * k + HEADS + 1], den_in[:, slot, k * P:(k + 1) * P],
                                                   mem.ident[0:HEADS + 1, 0:HEADS + 1])
                    last.then_inc(den_ps, 1)

            pipeline(pe, CHUNKS, 4, 3, step, peel=7)

        @block.scalar
        def _(act):
            act.wait_ge(eps_ready, 1)

            def step(s, i, m, on):
                if on(3):
                    c, slot = s - 3, (m - 3) % 3
                    act.wait_ge(shift_ready, c + 1)
                    wait(act, stored[slot], 16 * (i + (m - 3) // 3))
                    for k in range(3):
                        last = nc.scalar.activation(x_new[:, slot, k * D:(k + 1) * D], r[:, slot, k * D:(k + 1) * D], ACT.Identity,
                                                    bias=shift[:, slot, k:k + 1], scale=rstd[:, slot, k:k + 1])
                    last.then_inc(x_ready, 1)
                if on(2):
                    c, slot = s - 2, (m - 2) % 3
                    act.wait_ge(var_ready, c + 1)
                    wait(act, rstd_ready, c - 2)
                    nc.scalar.activation(std[:, slot, :], mean_var[:, slot, :, 1], ACT.Sqrt, bias=eps_sb[:, 0:1]).then_inc(std_ready, 1)

            pipeline(act, CHUNKS, 4, 3, step, peel=7)


def build(nc, t, out):
    with ExitStack() as ctx:
        mem = Memory(nc, ctx)
        rows = mem.rows_dram
        prepare(nc, mem, t["dst_tiles"], t["next_tiles"], t["dst_flat"], t["prev_flat"], t["next_flat"], t["first_dst"], t["batch_last"])
        project_inputs(nc, mem, t["xT"], t["W_in"], t["b_in"], t["Wq"], t["bq"], t["Wk"], t["bk"], t["Wv"], t["bv"])
        attention(nc, mem, t["src_tiles"])
        normalise_attention(nc, mem, t["x_rows"], rows[0])
        sum_layer(nc, mem, "w_", rows[0], t["src_tiles"], dict(kind="weighted", x_from=rows[0], x_to=rows[1]), t["attr64"], t["attr8"])
        min_layer(nc, mem, rows[1], t["src_tiles"],
                  dict(kind="max", x_from=rows[1], x_to=rows[2], y_to=rows[3],
                       w=t["W_max"][0:D, :], w_low=t["W_max"][D:2 * D, :], bias=t["b_max"], w_next=t["W1"]))
        sum_layer(nc, mem, "c1_", rows[3], t["src_tiles"], dict(kind="first_conv", y_from=rows[3], y_to=rows[4], bias=t["b1"], w_next=t["W2"]))
        sum_layer(nc, mem, "c2_", rows[4], t["src_tiles"],
                  dict(kind="second_conv", x_from=rows[2], y_from=rows[4], x_to=out, bias=t["b2"]))




def kernel(**inputs):
    import numpy as np
    import concourse.bacc as bacc
    from concourse.bass_utils import run_bass_kernel_spmd as run

    edges = TILES * P
    nc = bacc.Bacc("TRN2", target_bir_lowering=False, num_devices=1)
    x, src, dst = (np.asarray(inputs[name]) for name in ("x", "src", "dst"))

    def padded(a, value):
        return np.concatenate([a, np.full((edges - len(a),) + a.shape[1:], value, a.dtype)])

    def tiles(a):
        return np.ascontiguousarray(a.reshape((TILES, P) + a.shape[1:]).swapaxes(0, 1))

    dst_flat = padded(dst, N)
    prev_flat = np.concatenate([np.full(1, -1, dst.dtype), dst_flat[:-1]])
    next_flat = np.concatenate([dst_flat[1:], np.full(1, -1, dst.dtype)])
    xT = np.zeros((P, NP), x.dtype)
    xT[:, :N] = x.T
    x_rows = np.ascontiguousarray(xT.T)
    row = lambda name: np.asarray(inputs[name]).reshape(1, D)
    arrays = {
        "xT": xT,
        "x_rows": x_rows,
        "src_tiles": tiles(padded(src, 0)),
        "dst_tiles": tiles(dst_flat),
        "next_tiles": tiles(next_flat),
        "dst_flat": dst_flat.reshape(P, TILES),
        "prev_flat": prev_flat.reshape(P, TILES),
        "next_flat": next_flat.reshape(P, TILES),
        "first_dst": np.ascontiguousarray(dst_flat[::P]).reshape(1, TILES),
        "batch_last": np.ascontiguousarray(dst_flat[8 * P - 1::8 * P]).reshape(1, BATCHES),
        "attr64": tiles(padded(np.asarray(inputs["edge_attr_64"]), 0)),
        "attr8": tiles(padded(np.asarray(inputs["edge_attr_8"]), 0)),
        "W_in": np.asarray(inputs["L0_gnn_W_in"]), "b_in": row("L0_gnn_b_in"),
        "Wq": np.asarray(inputs["L0_gnn_Wq"]), "bq": row("L0_gnn_bq"),
        "Wk": np.asarray(inputs["L0_gnn_Wk"]), "bk": row("L0_gnn_bk"),
        "Wv": np.asarray(inputs["L0_gnn_Wv"]), "bv": row("L0_gnn_bv"),
        "W_max": np.asarray(inputs["L2_gnn_W"]), "b_max": row("L2_gnn_b"),
        "W1": np.asarray(inputs["L3_gnn_W1"]), "b1": row("L3_gnn_b1"),
        "W2": np.asarray(inputs["L3_gnn_W2"]), "b2": row("L3_gnn_b2"),
    }
    t = {name: nc.dram_tensor("in_" + name, a.shape, mybir.dt.from_np(a.dtype), kind="ExternalInput").ap()
         for name, a in arrays.items()}
    out = nc.dram_tensor("out", (PAIRS * PAIR, D), FP, kind="ExternalOutput").ap()
    build(nc, t, out)
    r = run(nc, [{"in_" + name: a for name, a in arrays.items()}], core_ids=[0])
    return r.results[0]["out"][:N]
```
